# Optimizing a Trainium2 kernel written in Bass

```python
import numpy as np
import jax
import jax.numpy as jnp

def _softmax(x, axis=-1):
    return jax.nn.softmax(x, axis=axis)

def _gelu(x):
    return jax.nn.gelu(x, approximate=True)

def _silu(x):
    return jax.nn.silu(x)

def _sigmoid(x):
    return jax.nn.sigmoid(x)

def _layernorm(x, axis=-1, eps=1e-05):
    m = jnp.mean(x, axis=axis, keepdims=True)
    v = jnp.var(x, axis=axis, keepdims=True)
    return (x - m) / jnp.sqrt(v + eps)

def _scatter_add(tgt, idx, src, axis=0):
    return tgt.at[idx].add(src)

def _segment_sum(src, seg, n):
    return jax.ops.segment_sum(src, seg, n)
kernel_name = 'mk_decoder_postln_d2_seqx_r8_1a74d7'

def setup_inputs(seed: int=0):
    np.random.seed(seed)
    _w = jnp.asarray

    def _rec_inputs():
        import jax
        import jax.numpy as jnp
        _rk = jax.random.key(seed)
        x = -9.806e-05 + 1 * jax.random.normal(jax.random.fold_in(_rk, 1), (16, 128, 128), jnp.float32)
        _lenS = 128 - jax.random.randint(jax.random.fold_in(_rk, 7), (16,), 0, max(1, 128 // 4) + 1, jnp.int32)
        _lenS2 = 128 - jax.random.randint(jax.random.fold_in(_rk, 8), (16,), 0, max(1, 128 // 4) + 1, jnp.int32)
        _ctx_1024P = jax.random.normal(jax.random.fold_in(_rk, 11), (16, 16, 128), jnp.float32)
        _ctx_1024c = jax.random.dirichlet(jax.random.fold_in(_rk, 511), 0.3 * jnp.ones((16,), jnp.float32), (16, 128))
        _ctx_1024t = jnp.einsum('bsk,bkd->bsd', _ctx_1024c, _ctx_1024P)
        _ctx_1024t = _ctx_1024t * jax.lax.rsqrt(jnp.mean(jnp.square(_ctx_1024t)) + 1e-12) * 0.953939
        ctx_1024 = 1.29246e-06 + 0.0312476 * (_ctx_1024t + 0.3 * jax.random.normal(jax.random.fold_in(_rk, 611), (16, 128, 128), jnp.float32))
        _validS = jnp.arange(128)[None, :] < _lenS[:, None]
        _validS2 = jnp.arange(128)[None, :] < _lenS2[:, None]
        _causal = jnp.tril(jnp.ones((128, 128), dtype=bool))
        mask_Bx1xSxS2_if1 = jnp.where(jnp.ones((16, 1, 128, 128), dtype=bool), 1, 0).astype(jnp.int32)
        return (x, ctx_1024, mask_Bx1xSxS2_if1)
    x, ctx_1024, mask_Bx1xSxS2_if1 = _rec_inputs()

    def _L0_attn_setup():
        import jax, jax.numpy as jnp
        import numpy as np
        import math
        B, T, C = (4, 256, 128)
        H, DQK, DV = (16, 64, 64)
        key = jax.random.key(seed)
        k1, k2, k3, k4, k5 = jax.random.split(key, 5)
        x_q = jax.random.normal(k1, (B, T, C), dtype=jnp.float32)
        w_q = jax.random.normal(k2, (H, DQK, C), dtype=jnp.float32) / math.sqrt(C)
        w_k = jax.random.normal(k3, (H, DQK, C), dtype=jnp.float32) / math.sqrt(C)
        w_v = jax.random.normal(k4, (H, DV, C), dtype=jnp.float32) / math.sqrt(C)
        w_o = jax.random.normal(k5, (DV * H, C), dtype=jnp.float32) / math.sqrt(C)
        return {'x_q': x_q, 'w_q': w_q, 'w_k': w_k, 'w_v': w_v, 'w_o': w_o}
    _L0_attn_all = _L0_attn_setup()
    _L0_attn_in = {k: v for k, v in _L0_attn_all.items() if k in ('w_q', 'w_k', 'w_v', 'w_o')}
    del _L0_attn_all

    def _L0_xattn_setup():
        import jax, jax.numpy as jnp
        import numpy as np
        from jax import lax
        N_INPUT = 128
        N_OUTPUT = 128
        B, T = (8, 64)
        key = jax.random.key(seed)
        k1, k2 = jax.random.split(key)
        X = jax.random.normal(k1, (B, T, N_INPUT), dtype=jnp.float32)
        W_init = jax.random.normal(k2, (B, N_OUTPUT, N_INPUT), dtype=jnp.float32) / np.sqrt(N_INPUT)
        return {'X': X, 'W_init': W_init}
    _L0_xattn_all = _L0_xattn_setup()
    _L0_xattn_in = {k: v for k, v in _L0_xattn_all.items() if k in ()}
    del _L0_xattn_all

    def _L0_ffn_setup():
        import jax, jax.numpy as jnp
        import numpy as np
        B, L, C1, C2, K, K_IN = (4, 128, 128, 128, 32, 32)
        BN_EPS = 1e-05

        def _gated_bottleneck(x2d, conv_w, conv_b, gamma, beta, lin_w, lin_b):
            n = x2d.shape[0]
            g = conv_w.shape[0]
            xc = jnp.einsum('ngf,gf->ng', x2d.reshape(n, g, 4), conv_w) + conv_b
            mean = jnp.mean(xc, axis=0)
            var = jnp.mean((xc - mean) ** 2, axis=0)
            xn = (xc - mean) * jax.lax.rsqrt(var + BN_EPS) * gamma + beta
            xa = jax.nn.gelu(xn, approximate=False)
            return xa @ lin_w.T + lin_b
        key = jax.random.key(seed)
        ks = jax.random.split(key, 8)
        g = C1 // 4
        w_std = (2.0 / C2) ** 0.5
        lin_std = (1.0 / g) ** 0.5
        return {'x': jax.random.normal(ks[0], (B, L, C1), jnp.float32), 'weight': jax.random.normal(ks[1], (C1, C2), jnp.float32) * w_std, 'bias': jnp.zeros((C2,), jnp.float32), 'so_conv_w': jax.random.normal(ks[2], (g, 4), jnp.float32) * 0.5, 'so_conv_b': jnp.zeros((g,), jnp.float32), 'so_gamma': jnp.ones((g,), jnp.float32), 'so_beta': jnp.zeros((g,), jnp.float32), 'so_lin_w': jax.random.normal(ks[3], (C2, g), jnp.float32) * lin_std, 'so_lin_b': jnp.zeros((C2,), jnp.float32), 'si_conv_w': jax.random.normal(ks[4], (g, 4), jnp.float32) * 0.5, 'si_conv_b': jnp.zeros((g,), jnp.float32), 'si_gamma': jnp.ones((g,), jnp.float32), 'si_beta': jnp.zeros((g,), jnp.float32), 'si_lin_w': jax.random.normal(ks[5], (C1, g), jnp.float32) * lin_std, 'si_lin_b': jnp.zeros((C1,), jnp.float32)}
    _L0_ffn_all = _L0_ffn_setup()
    _L0_ffn_in = {k: v for k, v in _L0_ffn_all.items() if k in ('weight', 'bias', 'so_conv_w', 'so_conv_b', 'so_gamma', 'so_beta', 'so_lin_w', 'so_lin_b', 'si_conv_w', 'si_conv_b', 'si_gamma', 'si_beta', 'si_lin_w', 'si_lin_b')}
    del _L0_ffn_all

    def _L1_attn_setup():
        import jax, jax.numpy as jnp
        import numpy as np
        D_MODEL = 128
        N_HEADS = 16
        WINDOW = 32
        CAUSAL = True

        def build_sliding_window_mask(T, window_size, causal=True):
            half = window_size // 2
            i = jnp.arange(T)[:, None]
            j = jnp.arange(T)[None, :]
            attend = jnp.abs(i - j) <= half
            if causal:
                attend = attend & (j <= i)
            return jnp.where(attend, 0.0, -jnp.inf).astype(jnp.float32)
        key = jax.random.key(seed)
        kx, kq, kk, kv, ko = jax.random.split(key, 5)
        B, T, D = (2, 256, D_MODEL)
        s = 1.0 / np.sqrt(D)
        return {'x': jax.random.normal(kx, (B, T, D), jnp.float32), 'Wq': jax.random.normal(kq, (D, D), jnp.float32) * s, 'Wk': jax.random.normal(kk, (D, D), jnp.float32) * s, 'Wv': jax.random.normal(kv, (D, D), jnp.float32) * s, 'Wo': jax.random.normal(ko, (D, D), jnp.float32) * s}
    _L1_attn_all = _L1_attn_setup()
    _L1_attn_in = {k: v for k, v in _L1_attn_all.items() if k in ('Wq', 'Wk', 'Wv', 'Wo')}
    del _L1_attn_all

    def _L1_xattn_setup():
        import jax, jax.numpy as jnp
        import numpy as np
        D_MODEL = 128
        HEADS = 16
        HEAD_DIM = D_MODEL // HEADS
        NEG_INF = -1000000000.0

        def _mha(query, key, value, mask, Wq, bq, Wk, bk, Wv, bv, Wo, bo):
            B, S, _ = query.shape

            def proj(x, W, b):
                y = x @ W.T + b
                return y.reshape(B, -1, HEADS, HEAD_DIM).transpose(0, 2, 1, 3)
            q = proj(query, Wq, bq)
            k = proj(key, Wk, bk)
            v = proj(value, Wv, bv)
            scores = jnp.einsum('bhsd,bhtd->bhst', q, k) / np.sqrt(HEAD_DIM)
            if mask is not None:
                scores = jnp.where(mask == 0, NEG_INF, scores)
            probs = jax.nn.softmax(scores, axis=-1)
            x = jnp.einsum('bhst,bhtd->bhsd', probs, v)
            x = x.transpose(0, 2, 1, 3).reshape(B, -1, D_MODEL)
            return x @ Wo.T + bo
        key = jax.random.key(seed)
        ks = jax.random.split(key, 12)
        B, S = (4, 256)
        scale = 1.0 / np.sqrt(D_MODEL)
        inp = {'query': jax.random.normal(ks[0], (B, S, D_MODEL), jnp.float32), 'key': jax.random.normal(ks[1], (B, S, D_MODEL), jnp.float32), 'value': jax.random.normal(ks[2], (B, S, D_MODEL), jnp.float32), 'mask': jnp.ones((B, 1, S, S), jnp.int32), 'Wq': jax.random.normal(ks[3], (D_MODEL, D_MODEL), jnp.float32) * scale, 'bq': jax.random.normal(ks[4], (D_MODEL,), jnp.float32) * 0.02, 'Wk': jax.random.normal(ks[5], (D_MODEL, D_MODEL), jnp.float32) * scale, 'bk': jax.random.normal(ks[6], (D_MODEL,), jnp.float32) * 0.02, 'Wv': jax.random.normal(ks[7], (D_MODEL, D_MODEL), jnp.float32) * scale, 'bv': jax.random.normal(ks[8], (D_MODEL,), jnp.float32) * 0.02, 'Wo': jax.random.normal(ks[9], (D_MODEL, D_MODEL), jnp.float32) * scale, 'bo': jax.random.normal(ks[10], (D_MODEL,), jnp.float32) * 0.02}
        return inp
    _L1_xattn_all = _L1_xattn_setup()
    _L1_xattn_in = {k: v for k, v in _L1_xattn_all.items() if k in ('Wq', 'bq', 'Wk', 'bk', 'Wv', 'bv', 'Wo', 'bo')}
    del _L1_xattn_all

    def _L1_ffn_setup():
        import jax, jax.numpy as jnp
        import numpy as np
        from jax import lax
        B, S, D = (4, 256, 128)
        E = 8
        K = 2
        F = 408
        NORM_TOPK = True
        key = jax.random.key(seed)
        ks = jax.random.split(key, 8)
        sd = 0.02
        return {'x': jax.random.normal(ks[0], (B, S, D), jnp.float32), 'gate_w': jax.random.normal(ks[1], (E, D), jnp.float32) * sd, 'gate_b': jnp.zeros((E,), jnp.float32), 'up_w': jax.random.normal(ks[2], (E, F, D), jnp.float32) * sd, 'up_b': jnp.zeros((E, F), jnp.float32), 'gp_w': jax.random.normal(ks[3], (E, F, D), jnp.float32) * sd, 'gp_b': jnp.zeros((E, F), jnp.float32), 'down_w': jax.random.normal(ks[4], (E, D, F), jnp.float32) * sd, 'down_b': jnp.zeros((E, D), jnp.float32)}
    _L1_ffn_all = _L1_ffn_setup()
    _L1_ffn_in = {k: v for k, v in _L1_ffn_all.items() if k in ('gate_w', 'gate_b', 'up_w', 'up_b', 'gp_w', 'gp_b', 'down_w', 'down_b')}
    del _L1_ffn_all
    return {'x': x, 'ctx_1024': ctx_1024, 'mask_Bx1xSxS2_if1': mask_Bx1xSxS2_if1, 'L0_attn_w_q': _L0_attn_in['w_q'], 'L0_attn_w_k': _L0_attn_in['w_k'], 'L0_attn_w_v': _L0_attn_in['w_v'], 'L0_attn_w_o': _L0_attn_in['w_o'], 'L0_ffn_weight': _L0_ffn_in['weight'], 'L0_ffn_bias': _L0_ffn_in['bias'], 'L0_ffn_so_conv_w': _L0_ffn_in['so_conv_w'], 'L0_ffn_so_conv_b': _L0_ffn_in['so_conv_b'], 'L0_ffn_so_gamma': _L0_ffn_in['so_gamma'], 'L0_ffn_so_beta': _L0_ffn_in['so_beta'], 'L0_ffn_so_lin_w': _L0_ffn_in['so_lin_w'], 'L0_ffn_so_lin_b': _L0_ffn_in['so_lin_b'], 'L0_ffn_si_conv_w': _L0_ffn_in['si_conv_w'], 'L0_ffn_si_conv_b': _L0_ffn_in['si_conv_b'], 'L0_ffn_si_gamma': _L0_ffn_in['si_gamma'], 'L0_ffn_si_beta': _L0_ffn_in['si_beta'], 'L0_ffn_si_lin_w': _L0_ffn_in['si_lin_w'], 'L0_ffn_si_lin_b': _L0_ffn_in['si_lin_b'], 'L1_attn_Wq': _L1_attn_in['Wq'], 'L1_attn_Wk': _L1_attn_in['Wk'], 'L1_attn_Wv': _L1_attn_in['Wv'], 'L1_attn_Wo': _L1_attn_in['Wo'], 'L1_xattn_Wq': _L1_xattn_in['Wq'], 'L1_xattn_bq': _L1_xattn_in['bq'], 'L1_xattn_Wk': _L1_xattn_in['Wk'], 'L1_xattn_bk': _L1_xattn_in['bk'], 'L1_xattn_Wv': _L1_xattn_in['Wv'], 'L1_xattn_bv': _L1_xattn_in['bv'], 'L1_xattn_Wo': _L1_xattn_in['Wo'], 'L1_xattn_bo': _L1_xattn_in['bo'], 'L1_ffn_gate_w': _L1_ffn_in['gate_w'], 'L1_ffn_gate_b': _L1_ffn_in['gate_b'], 'L1_ffn_up_w': _L1_ffn_in['up_w'], 'L1_ffn_up_b': _L1_ffn_in['up_b'], 'L1_ffn_gp_w': _L1_ffn_in['gp_w'], 'L1_ffn_gp_b': _L1_ffn_in['gp_b'], 'L1_ffn_down_w': _L1_ffn_in['down_w'], 'L1_ffn_down_b': _L1_ffn_in['down_b']}

def reference(x, ctx_1024, mask_Bx1xSxS2_if1, L0_attn_w_q, L0_attn_w_k, L0_attn_w_v, L0_attn_w_o, L0_ffn_weight, L0_ffn_bias, L0_ffn_so_conv_w, L0_ffn_so_conv_b, L0_ffn_so_gamma, L0_ffn_so_beta, L0_ffn_so_lin_w, L0_ffn_so_lin_b, L0_ffn_si_conv_w, L0_ffn_si_conv_b, L0_ffn_si_gamma, L0_ffn_si_beta, L0_ffn_si_lin_w, L0_ffn_si_lin_b, L1_attn_Wq, L1_attn_Wk, L1_attn_Wv, L1_attn_Wo, L1_xattn_Wq, L1_xattn_bq, L1_xattn_Wk, L1_xattn_bk, L1_xattn_Wv, L1_xattn_bv, L1_xattn_Wo, L1_xattn_bo, L1_ffn_gate_w, L1_ffn_gate_b, L1_ffn_up_w, L1_ffn_up_b, L1_ffn_gp_w, L1_ffn_gp_b, L1_ffn_down_w, L1_ffn_down_b):
    import jax
    import jax.numpy as jnp

    def _L0_attn_ref(x_q, w_q, w_k, w_v, w_o):
        import jax, jax.numpy as jnp
        import numpy as np
        import math
        B, T, C = (4, 256, 128)
        H, DQK, DV = (16, 64, 64)
        q = jnp.einsum('ntc,hdc->nhtd', x_q, w_q)
        k = jnp.einsum('ntc,hdc->nhtd', x_q, w_k)
        v = jnp.einsum('ntc,hdc->nhtd', x_q, w_v)
        a = jnp.einsum('nhtd,nhsd->nhts', q, k) / math.sqrt(q.shape[3])
        t = a.shape[2]
        causal_forbidden = jnp.arange(t)[:, None] < jnp.arange(t)[None, :]
        a = jnp.where(causal_forbidden[None, None], -jnp.inf, a)
        a = jax.nn.softmax(a, axis=3)
        y = jnp.einsum('nhts,nhsd->nthd', a, v).reshape(a.shape[0], t, -1)
        return y @ w_o

    def _L0_xattn_ref(X, W_init):
        import jax, jax.numpy as jnp
        import numpy as np
        from jax import lax
        N_INPUT = 128
        N_OUTPUT = 128
        B, T = (8, 64)
        lr = 1.0 / X.shape[-1]

        def step(W, x_t):
            pre = jnp.einsum('boi,bi->bo', W, x_t)
            y_t = jax.nn.sigmoid(pre)
            dW = jnp.einsum('bo,bi->boi', y_t, x_t) - (y_t ** 2)[..., None] * W
            W_new = W + lr * dW
            return (W_new, y_t)
        _, m_traj = lax.scan(step, W_init, jnp.swapaxes(X, 0, 1))
        return jnp.swapaxes(m_traj, 0, 1)

    def _L0_ffn_ref(x, weight, bias, so_conv_w, so_conv_b, so_gamma, so_beta, so_lin_w, so_lin_b, si_conv_w, si_conv_b, si_gamma, si_beta, si_lin_w, si_lin_b):
        import jax, jax.numpy as jnp
        import numpy as np
        B, L, C1, C2, K, K_IN = (4, 128, 128, 128, 32, 32)
        BN_EPS = 1e-05

        def _gated_bottleneck(x2d, conv_w, conv_b, gamma, beta, lin_w, lin_b):
            n = x2d.shape[0]
            g = conv_w.shape[0]
            xc = jnp.einsum('ngf,gf->ng', x2d.reshape(n, g, 4), conv_w) + conv_b
            mean = jnp.mean(xc, axis=0)
            var = jnp.mean((xc - mean) ** 2, axis=0)
            xn = (xc - mean) * jax.lax.rsqrt(var + BN_EPS) * gamma + beta
            xa = jax.nn.gelu(xn, approximate=False)
            return xa @ lin_w.T + lin_b
        b, l, c1 = x.shape
        c2 = weight.shape[1]
        x2d = x.reshape(b * l, c1)
        bi = jnp.arange(b)[:, None, None]
        li = jnp.arange(l)[None, :, None]
        score_out = jax.nn.softmax(_gated_bottleneck(x2d, so_conv_w, so_conv_b, so_gamma, so_beta, so_lin_w, so_lin_b).reshape(b, l, c2), axis=-1)
        s_v_out, s_i_out = jax.lax.top_k(score_out, K)
        full = jnp.einsum('blc,co->blo', x, weight)
        out_k = jnp.take_along_axis(full, s_i_out, axis=-1) * s_v_out
        out_branch = jnp.zeros((b, l, c2), x.dtype).at[bi, li, s_i_out].add(out_k)
        score_in = jax.nn.softmax(_gated_bottleneck(x2d, si_conv_w, si_conv_b, si_gamma, si_beta, si_lin_w, si_lin_b).reshape(b, l, c1), axis=-1)
        s_v_in, s_i_in = jax.lax.top_k(score_in, K_IN)
        x_gated = jnp.take_along_axis(x, s_i_in, axis=-1) * s_v_in
        x_sparse = jnp.zeros((b, l, c1), x.dtype).at[bi, li, s_i_in].add(x_gated)
        in_branch = jnp.einsum('blc,co->blo', x_sparse, weight)
        return out_branch + in_branch + bias

    def _L1_attn_ref(x, Wq, Wk, Wv, Wo):
        import jax, jax.numpy as jnp
        import numpy as np
        D_MODEL = 128
        N_HEADS = 16
        WINDOW = 32
        CAUSAL = True

        def build_sliding_window_mask(T, window_size, causal=True):
            half = window_size // 2
            i = jnp.arange(T)[:, None]
            j = jnp.arange(T)[None, :]
            attend = jnp.abs(i - j) <= half
            if causal:
                attend = attend & (j <= i)
            return jnp.where(attend, 0.0, -jnp.inf).astype(jnp.float32)
        B, T, D = x.shape
        H = N_HEADS
        dh = D // H

        def proj(W):
            return (x @ W.T).reshape(B, T, H, dh).transpose(0, 2, 1, 3)
        q, k, v = (proj(Wq), proj(Wk), proj(Wv))
        scale = jnp.sqrt(jnp.asarray(dh, x.dtype))
        scores = jnp.einsum('bhtd,bhsd->bhts', q, k) / scale
        mask = build_sliding_window_mask(T, WINDOW, CAUSAL)
        scores = scores + mask[None, None]
        attn = jax.nn.softmax(scores, axis=-1)
        attn = jnp.nan_to_num(attn, nan=0.0)
        out = jnp.einsum('bhts,bhsd->bhtd', attn, v)
        out = out.transpose(0, 2, 1, 3).reshape(B, T, D)
        return out @ Wo.T

    def _L1_xattn_ref(query, key, value, mask, Wq, bq, Wk, bk, Wv, bv, Wo, bo):
        import jax, jax.numpy as jnp
        import numpy as np
        D_MODEL = 128
        HEADS = 16
        HEAD_DIM = D_MODEL // HEADS
        NEG_INF = -1000000000.0

        def _mha(query, key, value, mask, Wq, bq, Wk, bk, Wv, bv, Wo, bo):
            B, S, _ = query.shape

            def proj(x, W, b):
                y = x @ W.T + b
                return y.reshape(B, -1, HEADS, HEAD_DIM).transpose(0, 2, 1, 3)
            q = proj(query, Wq, bq)
            k = proj(key, Wk, bk)
            v = proj(value, Wv, bv)
            scores = jnp.einsum('bhsd,bhtd->bhst', q, k) / np.sqrt(HEAD_DIM)
            if mask is not None:
                scores = jnp.where(mask == 0, NEG_INF, scores)
            probs = jax.nn.softmax(scores, axis=-1)
            x = jnp.einsum('bhst,bhtd->bhsd', probs, v)
            x = x.transpose(0, 2, 1, 3).reshape(B, -1, D_MODEL)
            return x @ Wo.T + bo
        return _mha(query, key, value, mask, Wq, bq, Wk, bk, Wv, bv, Wo, bo)

    def _L1_ffn_ref(x, gate_w, gate_b, up_w, up_b, gp_w, gp_b, down_w, down_b):
        import jax, jax.numpy as jnp
        import numpy as np
        from jax import lax
        B, S, D = (4, 256, 128)
        E = 8
        K = 2
        F = 408
        NORM_TOPK = True
        bs, slen, dim = x.shape
        xf = x.reshape(-1, dim)
        N = xf.shape[0]
        scores = jax.nn.softmax(xf @ gate_w.T + gate_b, axis=-1)
        top_w, top_idx = lax.top_k(scores, K)
        if NORM_TOPK:
            top_w = top_w / (top_w.sum(-1, keepdims=True) + 1e-20)
        comb = jnp.zeros((N, E), xf.dtype).at[jnp.arange(N)[:, None], top_idx].add(top_w)

        def step(acc, p):
            uw, ub, gw, gb, dw, db, w = p
            h = jax.nn.silu((xf @ gw.T + gb) * (xf @ uw.T + ub))
            return (acc + w[:, None] * (h @ dw.T + db), None)
        y0 = jnp.zeros_like(xf)
        y, _ = lax.scan(step, y0, (up_w, up_b, gp_w, gp_b, down_w, down_b, comb.T))
        return y.reshape(bs, slen, dim)
    x = _layernorm(x + _L0_attn_ref(x, L0_attn_w_q, L0_attn_w_k, L0_attn_w_v, L0_attn_w_o), axis=-1)
    x = _layernorm(x + _L0_xattn_ref(x, ctx_1024), axis=-1)
    x = _layernorm(x + _L0_ffn_ref(x, L0_ffn_weight, L0_ffn_bias, L0_ffn_so_conv_w, L0_ffn_so_conv_b, L0_ffn_so_gamma, L0_ffn_so_beta, L0_ffn_so_lin_w, L0_ffn_so_lin_b, L0_ffn_si_conv_w, L0_ffn_si_conv_b, L0_ffn_si_gamma, L0_ffn_si_beta, L0_ffn_si_lin_w, L0_ffn_si_lin_b), axis=-1)
    x = _layernorm(x + _L1_attn_ref(x, L1_attn_Wq, L1_attn_Wk, L1_attn_Wv, L1_attn_Wo), axis=-1)
    x = _layernorm(x + _L1_xattn_ref(x, ctx_1024, ctx_1024, mask_Bx1xSxS2_if1, L1_xattn_Wq, L1_xattn_bq, L1_xattn_Wk, L1_xattn_bk, L1_xattn_Wv, L1_xattn_bv, L1_xattn_Wo, L1_xattn_bo), axis=-1)
    x = _layernorm(x + _L1_ffn_ref(x, L1_ffn_gate_w, L1_ffn_gate_b, L1_ffn_up_w, L1_ffn_up_b, L1_ffn_gp_w, L1_ffn_gp_b, L1_ffn_down_w, L1_ffn_down_b), axis=-1)
    return x

_drawn_inputs = setup_inputs


def setup_inputs(seed=0):
    import zlib

    import numpy as np

    out = dict(_drawn_inputs(seed))
    spreads = {'L0_ffn_bias': (0.0, 0.1),
     'L0_ffn_so_conv_b': (0.0, 2.0),
     'L0_ffn_so_gamma': (1.0, 0.6),
     'L0_ffn_so_beta': (0.0, 0.8),
     'L0_ffn_so_lin_b': (0.0, 0.8),
     'L0_ffn_si_conv_b': (0.0, 2.0),
     'L0_ffn_si_gamma': (1.0, 0.6),
     'L0_ffn_si_beta': (0.0, 0.8),
     'L0_ffn_si_lin_b': (0.0, 0.8),
     'L1_ffn_gate_b': (0.0, 0.1),
     'L1_ffn_up_b': (0.0, 0.8),
     'L1_ffn_gp_b': (0.0, 0.8),
     'L1_ffn_down_b': (0.0, 0.473)}
    factors = {'L0_ffn_weight': 2.733,
     'L0_ffn_so_conv_w': 5.144,
     'L0_ffn_so_lin_w': 4.647,
     'L0_ffn_si_conv_w': 4.635,
     'L0_ffn_si_lin_w': 4.312,
     'L1_xattn_Wq': 8.0,
     'L1_xattn_bq': 8.0,
     'L1_xattn_Wk': 8.0,
     'L1_xattn_bk': 64.0,
     'L1_xattn_Wv': 3.067,
     'L1_ffn_up_w': 7.119,
     'L1_ffn_gp_w': 7.085,
     'L1_ffn_down_w': 6.496}
    for name, (base, spread) in spreads.items():
        noise = np.random.default_rng([zlib.crc32(name.encode()), seed]).standard_normal(out[name].shape)
        drawn = base * np.exp(spread * noise) if base else spread * noise
        out[name] = jnp.asarray(drawn.astype(out[name].dtype))
    for name, factor in factors.items():
        out[name] = (out[name] * factor).astype(out[name].dtype)
    return out
```

```python
from contextlib import ExitStack

import numpy as np

import concourse.bass as bass
from concourse import mybir

F32 = mybir.dt.float32
BF16 = mybir.dt.bfloat16
I32 = mybir.dt.int32
U32 = mybir.dt.uint32
ALU = mybir.AluOpType
ACT = mybir.ActivationFunctionType
AX = mybir.AxisListType

B, S, D = 16, 128, 128
P = 128
H = 16
DH0 = 64
DH1 = D // H
HU = 4
NU = H // HU
SEG = HU * S
E, F = 8, 408
FC, FP = 4, F // 4
G = 32
TOPK = 32
C = 8
NBLK = S // C
LR = 1.0 / D
EPS = 1e-5
NEG = -(2.0 ** 100)


def need(eng, sem, value):
    if isinstance(value, int) and value <= 0:
        return
    eng.wait_ge(sem, value)


def decoder_program(nc, a, out):
    with ExitStack() as ctx:
        def sb(name, shape, dt=F32):
            return ctx.enter_context(nc.sbuf_tensor(name, shape, dt))

        part_sems = []

        def sem(name):
            part_sems.append(nc.alloc_semaphore(name=name))
            return part_sems[-1]

        def part_ends():
            nc.clear_and_free_semaphores(list(part_sems))
            part_sems.clear()
            nc.all_engine_barrier()

        X = sb("X", [P, B, D])
        XT = sb("XT", [P, B, S])
        RES = sb("RES", [P, B, D])
        CTXT = sb("CTXT", [P, B, S])
        ident = sb("ident", [P, P])
        ident16 = sb("ident16", [P, P], BF16)
        stats = sb("stats", [P, B, 6])
        moments = sb("moments", [P, B, 2])
        rstd = sb("rstd", [P, B])
        half = sb("half", [P, B])

        loaded = sem("loaded")

        def layernorm(name, also_time_major=None, out_to=None):
            stats_ready, var_ready, rstd_ready = sem(name + "_stats"), sem(name + "_var"), sem(name + "_rstd")
            x_ready, t_ready, xt_ready = sem(name + "_x"), sem(name + "_t"), sem(name + "_xt")
            with ExitStack() as scope:
                tp = [scope.enter_context(nc.psum_tensor(f"{name}_tp{i}", [P, 4, P], F32)) for i in range(2)]
                block = scope.enter_context(nc.Block())

                @block.vector
                def _(dve):
                    for b in range(B):
                        ins = nc.vector.bn_aggr(moments[:, b, :], stats[:, b, :])
                    ins.then_inc(stats_ready, 1)
                    dve.wait_ge(stats_ready, 1)
                    nc.vector.tensor_scalar(rstd[:], moments[:, :, 1], EPS, None, ALU.add).then_inc(var_ready, 1)
                    dve.wait_ge(rstd_ready, 1)
                    for b in range(B):
                        nc.vector.tensor_scalar(X[:, b, :], RES[:, b, :], moments[:, b, 0:1], rstd[:, b:b + 1],
                                                ALU.subtract, ALU.mult).then_inc(x_ready, 1)

                @block.gpsimd
                def _(pool):
                    pool.wait_ge(var_ready, 1)
                    nc.gpsimd.tensor_tensor(rstd[:], rstd[:], half[:], ALU.pow).then_inc(rstd_ready, 1)

                if out_to is not None:
                    stored = sem(name + "_stored")
                    rows = out_to.rearrange("b t c -> t b c")

                    @block.sync
                    def _(sp):
                        for q in range(4):
                            sp.wait_ge(x_ready, 4 * q + 4)
                            sp.dma_start(rows[:, 4 * q:4 * q + 4, :], X[:, 4 * q:4 * q + 4, :]).then_inc(stored, 16)
                        sp.wait_ge(stored, 16 * 4)
                    return

                @block.tensor
                def _(pe):
                    for q in range(B // 4):
                        need(pe, xt_ready, q - 1)
                        for j in range(4):
                            pe.wait_ge(x_ready, 4 * q + j + 1)
                            ins = nc.tensor.transpose(tp[q % 2][:, j, :], X[:, 4 * q + j, :], ident[:])
                        ins.then_inc(t_ready, 1)

                @block.scalar
                def _(act):
                    for q in range(B // 4):
                        act.wait_ge(t_ready, q + 1)
                        if also_time_major is not None:
                            nc.scalar.copy(also_time_major[:, :, 4 * q:4 * q + 4].rearrange("p t b -> p b t"), tp[q % 2][:])
                        nc.scalar.copy(XT[:, 4 * q:4 * q + 4, :], tp[q % 2][:]).then_inc(xt_ready, 1)

        def attention(name, wide, allowed, WO, ZM=None, WVT=None, QT=None, KT=None, VA=None, jmask=None, umask=None,
                      maskint=None, bo_row=None, ones_row=None):
            DV = DH0 if wide else DH1
            VW = DV + 1
            NOT = HU * DV // P if wide else 1
            s_ = lambda what: sem(f"{name}_{what}")
            z_ready, zs_ready = s_("z_ready"), s_("zs_ready")
            stat_ready, v_ready, vs_ready = s_("stat_ready"), s_("v_ready"), s_("vs_ready")
            ones_ready = s_("ones_ready")
            s_ready, max_ready, e_ready, p_ready = s_("s_ready"), s_("max_ready"), s_("e_ready"), s_("p_ready")
            t_ready, pt_ready, pv_ready, rl_ready = s_("t_ready"), s_("pt_ready"), s_("pv_ready"), s_("rl_ready")
            on_ready, ot_ready, ots_ready = s_("on_ready"), s_("ot_ready"), s_("ots_ready")
            y_ready, res_ready, st_ready, bias_ready = s_("y_ready"), s_("res_ready"), s_("st_ready"), s_("bias_ready")
            keys_ready = s_("keys_ready")
            with ExitStack() as scope:
                def lsb(what, shape, dt=F32):
                    return scope.enter_context(nc.sbuf_tensor(f"{name}_{what}", shape, dt))

                def lps(what, shape):
                    return scope.enter_context(nc.psum_tensor(f"{name}_{what}", shape, F32))

                stat = lsb("stat", [P, 2, S] if wide else [P, 2, NU, S])
                Eb = lsb("E", [P, 2, HU, S])
                Pb = lsb("P", [P, 2, HU, S])
                PT = lsb("PT", [P, 2, HU, S])
                mx = lsb("mx", [P, 2, HU])
                rl = lsb("rl", [P, 2, HU])
                ON = lsb("ON", [P, 2, HU * DV if wide else D])
                OT = lsb("OT", [P, 2, max(NOT, 1), S])
                sp = [lps(f"sp{i}", [P, HU, S]) for i in range(2)]
                tp = [lps(f"tp{i}", [P, HU, S]) for i in range(2)]
                op = lps("op", [P, HU, VW])
                otp = lps("otp", [P, 2, S])
                yp = lps("yp", [P, D])
                if wide:
                    zp = lps("zp", [P, SEG])
                    zs = lsb("zs", [P, 2, SEG])
                    VS = lsb("VS", [P, 2, H, VW])
                else:
                    kx = lsb("kx", [P, 2, HU, S])
                if maskint is not None:
                    mi = lsb("mi", [P, 2, S], I32)
                    mb = lsb("mb", [P, 2, S], BF16)
                    mask_landed = [s_(f"mask_landed{i}") for i in range(2)]

                def run(eng, slot, drain=4):
                    for j in range(8):
                        slot(0, j, lambda lag: j >= lag)
                    with eng.Fori(1, B // 2) as i:
                        for j in range(8):
                            slot(i, j, lambda lag: True)
                    for j in range(drain):
                        slot(B // 2, j, lambda lag: j < lag)

                block = scope.enter_context(nc.Block())

                @block.gpsimd
                def _(pool):
                    if wide:
                        nc.gpsimd.memset(VS[:, :, :, DV:VW], 1.0).then_inc(ones_ready, 1)

                    def slot(i, j, live):
                        k = 8 * i + j
                        if j % NU == 0 and live(0):
                            b = 2 * i + j // NU
                            r = j // NU
                            if maskint is not None:
                                pool.wait_ge(mask_landed[r], 16 * i + 16)
                            need(pool, s_ready, k - NU)
                            if wide:
                                need(pool, v_ready, 4 * i + 2 * r - 2)
                            if wide:
                                nc.gpsimd.tensor_copy(stat[:, r, :], XT[:, b, :]).then_inc(stat_ready, 1)
                            else:
                                nc.gpsimd.tensor_tensor(
                                    stat[:, r], QT[:, b, :].unsqueeze(1).to_broadcast([P, NU, S]),
                                    umask[:].unsqueeze(2).to_broadcast([P, NU, S]), ALU.mult).then_inc(stat_ready, 1)
                            if not wide:
                                nc.gpsimd.tensor_tensor(
                                    kx[:, r], KT[:, b, :].unsqueeze(1).to_broadcast([P, HU, S]),
                                    jmask[:].unsqueeze(2).to_broadcast([P, HU, S]), ALU.mult).then_inc(keys_ready, 1)
                            if maskint is not None:
                                nc.gpsimd.tensor_scalar(mb[:, r, :], mi[:, r, :], 0.0, NEG,
                                                        ALU.is_equal, ALU.mult).then_inc(bias_ready, 1)

                    run(pool, slot, 0)

                @block.sync
                def _(sp_eng):
                    if maskint is not None:
                        def slot(i, j, live):
                            if j % NU == 0:
                                r = j // NU
                                need(sp_eng, bias_ready, 2 * i + r - 1)
                                sp_eng.dma_start(mi[:, r, :], maskint[2 * i + r]).then_inc(mask_landed[r], 16)
                        run(sp_eng, slot, 0)

                @block.tensor
                def _(pe):
                    if wide:
                        pe.wait_ge(ones_ready, 1)

                    def slot(i, j, live):
                        k = 8 * i + j
                        u = j % NU
                        if wide and live(0):
                            need(pe, zs_ready, k)
                            if u in (2, 3):
                                need(pe, vs_ready, 4 * i + 2 * (j // NU) + u - 1)
                            for h in range(HU):
                                ins = nc.tensor.matmul(zp[:, S * h:S * h + S], ZM[:, HU * u + h, :],
                                                       XT[:, 2 * i + j // NU, :], start=True, stop=True)
                            ins.then_inc(z_ready, 1)
                        if live(4) and (wide or u == 3):
                            n = k - 4
                            need(pe, on_ready, n + 1)
                            need(pe, ots_ready, n if wide else (n - 3) // 4 if isinstance(n, int) else 2 * i + j // NU - 1)
                            for m in range(NOT):
                                src = ON[:, j % 2, P * m:P * m + P] if wide else ON[:, (j // NU + 1) % 2, :]
                                ins = nc.tensor.transpose(otp[:, m, :], src, ident[:])
                            ins.then_inc(ot_ready, 1)
                        if live(1):
                            n, r, v = k - 1, ((j - 1) // NU) % 2, (j - 1) % NU
                            need(pe, stat_ready, 2 * i + (j - 1) // NU + 1)
                            need(pe, e_ready, n - 1)
                            if wide:
                                pe.wait_ge(zs_ready, n + 1)
                                nc.tensor.matmul(sp[(j - 1) % 2][:], stat[:, r, :], zs[:, (j - 1) % 2, :], start=True, stop=False)
                            else:
                                need(pe, keys_ready, 2 * i + (j - 1) // NU + 1)
                                nc.tensor.matmul(sp[(j - 1) % 2][:], stat[:, r, v, :], kx[:, r], start=True, stop=False)
                            if maskint is not None:
                                need(pe, bias_ready, 2 * i + (j - 1) // NU + 1)
                            bias = allowed[:] if maskint is None else mb[:, r, :]
                            nc.tensor.matmul(sp[(j - 1) % 2][:], ident16[:], bias.unsqueeze(1).to_broadcast([P, HU, S]),
                                             start=False, stop=True).then_inc(s_ready, 1)
                        if wide and live(0) and u in (1, 2):
                            pe.wait_ge(zs_ready, k + 1)
                            r = j // NU
                            need(pe, stat_ready, 2 * i + r + 1)
                            nc.tensor.matmul(zp[:], stat[:, r, :], WVT[:, SEG * (u - 1):SEG * u],
                                             start=True, stop=True).then_inc(v_ready, 1)
                        if live(2):
                            n = k - 2
                            pe.wait_ge(p_ready, n + 1)
                            need(pe, pt_ready, n - 1)
                            for h in range(HU):
                                ins = nc.tensor.transpose(tp[j % 2][:, h, :], Pb[:, j % 2, h, :], ident[:])
                            ins.then_inc(t_ready, 1)
                        if live(3):
                            n, v = k - 3, (j - 3) % NU
                            r = ((j - 3) // NU) % 2
                            pe.wait_ge(pt_ready, n + 1)
                            need(pe, on_ready, n)
                            if wide:
                                need(pe, vs_ready, 4 * i + 2 * ((j - 3) // NU) + 2)
                            for h in range(HU):
                                hh = HU * v + h
                                vals = VS[:, r, hh, :] if wide else VA[:, 2 * i + (j - 3) // NU, hh, :]
                                ins = nc.tensor.matmul(op[:, h, :], PT[:, (j - 3) % 2, h, :], vals, start=True, stop=True)
                            ins.then_inc(pv_ready, 1)
                        if live(4) and (wide or u == 3):
                            n, v = k - 4, (j - 4) % NU
                            if wide:
                                pe.wait_ge(ots_ready, n + 1)
                                if v == 0:
                                    need(pe, res_ready, 2 * i + (j - 4) // NU)
                                for m in range(NOT):
                                    ins = nc.tensor.matmul(yp[:], OT[:, j % 2, m, :], WO[:, NOT * v + m, :],
                                                           start=(v == 0 and m == 0), stop=(v == NU - 1 and m == NOT - 1))
                            else:
                                bb = 2 * i + (j - 4) // NU
                                pe.wait_ge(ots_ready, bb + 1)
                                need(pe, res_ready, bb)
                                ins = nc.tensor.matmul(yp[:], OT[:, (j // NU + 1) % 2, 0, :], WO[:, 0, :],
                                                       start=True, stop=bo_row is None)
                                if bo_row is not None:
                                    ins = nc.tensor.matmul(yp[:], ones_row[:], bo_row[:], start=False, stop=True)
                            ins.then_inc(y_ready, 1)

                    run(pe, slot)

                @block.scalar
                def _(act):
                    def slot(i, j, live):
                        k = 8 * i + j
                        if wide and live(0):
                            act.wait_ge(z_ready, k + 1)
                            need(act, s_ready, k - 1)
                            nc.scalar.copy(zs[:, j % 2, :], zp[:]).then_inc(zs_ready, 1)
                        if live(2):
                            n = k - 2
                            act.wait_ge(t_ready, n + 1)
                            need(act, pv_ready, n - 1)
                            nc.scalar.copy(PT[:, j % 2], tp[j % 2][:]).then_inc(pt_ready, 1)
                        if live(1):
                            n = k - 1
                            act.wait_ge(e_ready, n + 1)
                            need(act, t_ready, n - 1)
                            nc.scalar.activation(Pb[:, (j - 1) % 2], Eb[:, (j - 1) % 2], ACT.Exp).then_inc(p_ready, 1)

                    run(act, slot)

                @block.vector
                def _(dve):
                    def slot(i, j, live):
                        k = 8 * i + j
                        u = j % NU
                        if live(4) and (wide or u == 3):
                            n = k - 4
                            if wide:
                                dve.wait_ge(ot_ready, n + 1)
                                need(dve, y_ready, n - 1)
                                nc.vector.tensor_copy(OT[:, j % 2], otp[:]).then_inc(ots_ready, 1)
                            else:
                                bb = 2 * i + (j - 4) // NU
                                dve.wait_ge(ot_ready, bb + 1)
                                need(dve, y_ready, bb)
                                nc.vector.tensor_copy(OT[:, (j // NU + 1) % 2, 0, :], otp[:, 0, :]).then_inc(ots_ready, 1)
                        if live(1):
                            n, q = k - 1, (j - 1) % 2
                            dve.wait_ge(s_ready, n + 1)
                            need(dve, e_ready, n - 1)
                            nc.vector.tensor_reduce(mx[:, q, :], sp[q][:], AX.X, ALU.max).then_inc(max_ready, 1)
                            dve.wait_ge(max_ready, n + 1)
                            need(dve, p_ready, n - 1)
                            nc.vector.tensor_tensor(Eb[:, q], sp[q][:], mx[:, q, :].unsqueeze(2).to_broadcast([P, HU, S]),
                                                    ALU.subtract).then_inc(e_ready, 1)
                        if wide and live(0) and u in (1, 2):
                            r = j // NU
                            dve.wait_ge(v_ready, 4 * i + 2 * r + u)
                            need(dve, pv_ready, k - u - NU)
                            nc.vector.tensor_copy(VS[:, r, 8 * (u - 1):8 * u, 0:DV],
                                                  zp[:].rearrange("p (h d) -> p h d", d=DV)).then_inc(vs_ready, 1)
                        if live(3):
                            n, q = k - 3, (j - 3) % 2
                            dve.wait_ge(pv_ready, n + 1)
                            nc.vector.reciprocal(rl[:, q, :], op[:, :, DV]).then_inc(rl_ready, 1)
                            dve.wait_ge(rl_ready, n + 1)
                            if wide:
                                need(dve, ot_ready, n - 1)
                                o = ON[:, q, :]
                            else:
                                v, bb = (j - 3) % NU, 2 * i + (j - 3) // NU
                                need(dve, ot_ready, bb)
                                o = ON[:, ((j - 3) // NU) % 2, 32 * v:32 * v + 32]
                            nc.vector.tensor_tensor(o.rearrange("p (h d) -> p h d", d=DV), op[:, :, 0:DV],
                                                    rl[:, q, :].unsqueeze(2).to_broadcast([P, HU, DV]),
                                                    ALU.mult).then_inc(on_ready, 1)
                        if live(4) and u == 3:
                            b = 2 * i + (j - 4) // NU
                            dve.wait_ge(y_ready, (4 * b + 4) if wide else (b + 1))
                            nc.vector.tensor_tensor(RES[:, b, :], yp[:], X[:, b, :], ALU.add).then_inc(res_ready, 1)
                            dve.wait_ge(res_ready, b + 1)
                            nc.vector.bn_stats(stats[:, b, :], RES[:, b, :]).then_inc(st_ready, 1)

                    run(dve, slot)

        def recurrence(XTt, YT):
            s_ = lambda what: sem(f"rec_{what}")
            (far_gram_ready, far_gram_kept, zeroed, xblk_ready, gram_ready, gram_kept, masked_ready, gb_ready, gb_kept,
             w0_ready, far_ready, near_ready, ut_ready, ut_kept, p_ready, y_ready, sq_ready, q_ready, a_ready, r_ready,
             u_ready, yt_ready, a0_ready, c_loaded) = [s_(w) for w in (
                 "far_gram_ready far_gram_kept zeroed xblk_ready gram_ready gram_kept masked_ready gb_ready gb_kept "
                 "w0_ready far_ready near_ready ut_ready ut_kept p_ready y_ready sq_ready q_ready a_ready r_ready "
                 "u_ready yt_ready a0_ready c_loaded").split()]
            ut_landed = [s_(f"ut_landed{i}") for i in range(2)]
            CB = C * B
            with ExitStack() as scope:
                def lsb(what, shape, dt=F32):
                    return scope.enter_context(nc.sbuf_tensor(f"rec_{what}", shape, dt))

                def lps(what, shape):
                    return scope.enter_context(nc.psum_tensor(f"rec_{what}", shape, F32))

                GF = lsb("GF", [P, B, S + C])
                UT = lsb("UT", [P, B, D])
                sel = lsb("sel", [P, C])
                same = lsb("same", [P, 2, CB])
                xblk = lsb("xblk", [P, 2, CB])
                graw = lsb("graw", [P, 2 * CB])
                gm = lsb("gm", [P, 2, 2 * CB])
                NG = B * C * (C - 1) // 2
                GB = lsb("GB", [P, 2, NG])
                uTk = lsb("uTk", [P, 2, D])
                pm = lsb("pm", [P, C, B])
                Y = lsb("Y", [P, C, B])
                sq = lsb("sq", [P, B])
                gt = lsb("gt", [P, C - 1, B])
                qt = lsb("qt", [P, C - 1, B])
                AH = lsb("AH", [P, C + 1, B])
                RA = lsb("RA", [P, C, B])
                U = lsb("U", [P, C, B])
                rp = [lps(f"rp{i}", [P, B, C]) for i in range(2)]
                gp = lps("gp", [P, 2 * CB])
                gbp = lps("gbp", [P, NG])
                utp = lps("utp", [P, D])
                fgp = [lps(f"fgp{i}", [P, 4, S]) for i in range(2)]
                first = [sum(B * (C - 1 - r) for r in range(s)) for s in range(C)]
                block = scope.enter_context(nc.Block())

                def blocks(eng, slot):
                    for j in range(2):
                        slot(j, j)
                    with eng.Fori(1, NBLK // 2) as i:
                        for j in range(2):
                            slot(2 * i + j, j)

                @block.gpsimd
                def _(pool):
                    nc.gpsimd.memset(XTt[:, S:S + 2 * C, :], 0.0).then_inc(zeroed, 1)
                    nc.gpsimd.memset(GF[:, :, S:S + C], 0.0).then_inc(zeroed, 1)
                    nc.gpsimd.memset(UT[:], 0.0).then_inc(zeroed, 1)

                    def prepare(k, j):
                        need(pool, gram_ready, k - 1)
                        nc.gpsimd.tensor_copy(xblk[:, j, :], XTt[:, bass.ds(C * k, C), :].rearrange("p t b -> p (t b)")
                                              ).then_inc(xblk_ready, 1)
                        pool.wait_ge(gram_kept, k + 1)
                        need(pool, near_ready, k)
                        need(pool, gb_ready, k - 1)
                        nc.gpsimd.tensor_tensor(gm[:, j, :], graw[:], same[:].rearrange("p a c -> p (a c)"),
                                                ALU.mult).then_inc(masked_ready, 1)

                    pool.wait_ge(zeroed, 1)
                    pool.wait_ge(c_loaded, 32)
                    prepare(0, 0)

                    def slot(k, j):
                        prepare(k + 1, 1 - j)
                        pool.wait_ge(y_ready, C * k + C)
                        nc.gpsimd.tensor_copy(YT[:, bass.ds(C * k, C), :], Y[:]).then_inc(yt_ready, 1)

                    blocks(pool, slot)

                @block.sync
                def _(sp):
                    sp.dma_start(sel[:], a["sel"]).then_inc(c_loaded, 16)
                    sp.dma_start(same[:], a["same"]).then_inc(c_loaded, 16)

                    for k in range(NBLK):
                        sp.wait_ge(ut_kept, k + 1)
                        sp.wait_ge(far_ready, k + 1)
                        sp.dma_start(UT[C * k:C * k + C, :, :], uTk[:, k % 2, :]).then_inc(ut_landed[k % 2], 16)
                    for j in range(2):
                        sp.wait_ge(ut_landed[j], 16 * (NBLK // 2))

                @block.tensor
                def _(pe):
                    for q in range(4):
                        need(pe, far_gram_kept, q - 1)
                        for r in range(4):
                            ins = nc.tensor.matmul(fgp[q % 2][:, r, :], XT[:, 4 * q + r, :], XT[:, 4 * q + r, :],
                                                   start=True, stop=True)
                        ins.then_inc(far_gram_ready, 1)

                    def prepare(k, j):
                        pe.wait_ge(xblk_ready, k + 1)
                        need(pe, gram_kept, k)
                        nc.tensor.matmul(gp[:], xblk[:, j, :], XTt[:, bass.ds(C * k, 2 * C), :].rearrange("p t b -> p (t b)"),
                                         start=True, stop=True).then_inc(gram_ready, 1)
                        need(pe, p_ready, C * (k - 2) + 1)
                        for b in range(B):
                            ins = nc.tensor.matmul(rp[j][:, b, :], CTXT[:, b, :], XTt[:, bass.ds(C * k, C), b],
                                                   start=(b == 0), stop=False, skip_group_check=True)
                        ins.then_inc(w0_ready, 1)
                        pe.wait_ge(masked_ready, k + 1)
                        need(pe, gb_kept, k)
                        for s in range(C - 1):
                            n = B * (C - 1 - s)
                            ins = nc.tensor.matmul(gbp[:, first[s]:first[s] + n], sel[:, s:s + 1].to_broadcast([P, P]),
                                                   gm[:, j, B * (s + 1):CB], start=True, stop=True)
                        ins.then_inc(gb_ready, 1)

                    prepare(0, 0)
                    pe.wait_ge(w0_ready, 1)
                    pe.sem_inc(near_ready, 1)
                    pe.wait_ge(far_gram_kept, 4)

                    def slot(k, j):
                        prepare(k + 1, 1 - j)
                        need(pe, ut_landed[1 - j], 16 * ((k + 1) // 2) if isinstance(k, int) else 8 * (k - j) + 16 * j)
                        for b in range(B):
                            ins = nc.tensor.matmul(rp[1 - j][:, b, :], UT[:, b, :], GF[:, b, bass.ds(C * k + C, C)],
                                                   start=False, stop=False, skip_group_check=True)
                        ins.then_inc(far_ready, 1)
                        pe.wait_ge(u_ready, C * k + C)
                        need(pe, ut_kept, k)
                        nc.tensor.transpose(utp[:], U[:].rearrange("p s b -> p (s b)"), ident[:]).then_inc(ut_ready, 1)
                        pe.wait_ge(ut_kept, k + 1)
                        nc.tensor.matmul(rp[1 - j][:], uTk[:, j, :],
                                         gm[:, j, CB:2 * CB].rearrange("p (t b) -> p b t", b=B),
                                         start=False, stop=True, skip_group_check=True).then_inc(near_ready, 1)

                    blocks(pe, slot)

                @block.scalar
                def _(act):
                    act.wait_ge(zeroed, 3)
                    for q in range(4):
                        act.wait_ge(far_gram_ready, q + 1)
                        nc.scalar.copy(GF[:, 4 * q:4 * q + 4, 0:S], fgp[q % 2][:]).then_inc(far_gram_kept, 1)

                    def keep_gram(k):
                        act.wait_ge(gram_ready, k + 1)
                        need(act, masked_ready, k)
                        nc.scalar.copy(graw[:], gp[:]).then_inc(gram_kept, 1)

                    def keep_gb(k, j):
                        act.wait_ge(gb_ready, k + 1)
                        need(act, p_ready, C * (k - 1))
                        nc.scalar.mul(GB[:, j, :], gbp[:], LR).then_inc(gb_kept, 1)

                    keep_gram(0)
                    keep_gb(0, 0)

                    def slot(k, j):
                        need(act, yt_ready, k)
                        for s in range(C):
                            act.wait_ge(p_ready, C * k + s + 1)
                            nc.scalar.activation(Y[:, s, :], pm[:, s, :], ACT.Sigmoid).then_inc(y_ready, 1)
                            if s == 1:
                                keep_gram(k + 1)
                            if s == 5:
                                keep_gb(k + 1, 1 - j)
                        act.wait_ge(ut_ready, k + 1)
                        need(act, near_ready, k)
                        need(act, ut_landed[j], 16 * (k // 2) if isinstance(k, int) else 8 * (k - j))
                        nc.scalar.copy(uTk[:, j, :], utp[:]).then_inc(ut_kept, 1)

                    blocks(act, slot)

                @block.vector
                def _(dve):
                    nc.vector.memset(AH[:, C, :], 1.0).then_inc(a0_ready, 1)
                    dve.wait_ge(a0_ready, 1)

                    def slot(k, j):
                        need(dve, a_ready, C * k)
                        nc.vector.tensor_copy(AH[:, 0, :], AH[:, C, :]).then_inc(a0_ready, 1)
                        dve.wait_ge(near_ready, k + 1)
                        nc.vector.tensor_tensor(pm[:], rp[j][:].rearrange("p b t -> p t b"),
                                                AH[:, C, :].unsqueeze(1).to_broadcast([P, C, B]), ALU.mult).then_inc(p_ready, 1)
                        dve.wait_ge(gb_kept, k + 1)
                        dve.wait_ge(a0_ready, k + 2)
                        for s in range(C):
                            n = C - 1 - s
                            dve.wait_ge(y_ready, C * k + s + 1)
                            y = Y[:, s, :]
                            nc.vector.scalar_tensor_tensor(sq[:], y, -LR, y, ALU.mult, ALU.mult).then_inc(sq_ready, 1)
                            if n:
                                nc.vector.tensor_tensor(gt[:, 0:n], GB[:, j, first[s]:first[s] + B * n].rearrange("p (t b) -> p t b", b=B),
                                                        y.unsqueeze(1).to_broadcast([P, n, B]), ALU.mult)
                            dve.wait_ge(sq_ready, C * k + s + 1)
                            if n:
                                nc.vector.scalar_tensor_tensor(qt[:, 0:n], sq[:].unsqueeze(1).to_broadcast([P, n, B]), 1.0,
                                                               pm[:, s + 1:C, :], ALU.add, ALU.mult).then_inc(q_ready, 1)
                                dve.wait_ge(q_ready, (C - 1) * k + s + 1)
                                nc.vector.tensor_tensor(pm[:, s + 1:C, :], qt[:, 0:n], gt[:, 0:n], ALU.add).then_inc(p_ready, 1)
                            nc.vector.scalar_tensor_tensor(AH[:, s + 1, :], sq[:], 1.0, AH[:, s, :], ALU.add, ALU.mult).then_inc(a_ready, 1)
                            dve.wait_ge(a_ready, C * k + s + 1)
                            nc.vector.reciprocal(RA[:, s, :], AH[:, s + 1, :]).then_inc(r_ready, 1)
                            dve.wait_ge(r_ready, C * k + s + 1)
                            need(dve, ut_ready, k)
                            nc.vector.scalar_tensor_tensor(U[:, s, :], y, LR, RA[:, s, :], ALU.mult, ALU.mult).then_inc(u_ready, 1)

                    blocks(dve, slot)

        def add_recurrence(YT):
            t_ready, res_ready, st_ready = sem("addrec_t_ready"), sem("addrec_res_ready"), sem("addrec_st_ready")
            with ExitStack() as scope:
                tp = [scope.enter_context(nc.psum_tensor(f"addrec_tp{i}", [P, 4, P], F32)) for i in range(2)]
                block = scope.enter_context(nc.Block())

                @block.tensor
                def _(pe):
                    for q in range(B // 4):
                        need(pe, res_ready, q - 1)
                        for j in range(4):
                            ins = nc.tensor.transpose(tp[q % 2][:, j, :], YT[:, 0:S, 4 * q + j], ident[:])
                        ins.then_inc(t_ready, 1)

                @block.vector
                def _(dve):
                    for q in range(B // 4):
                        dve.wait_ge(t_ready, q + 1)
                        nc.vector.tensor_tensor(RES[:, 4 * q:4 * q + 4, :], tp[q % 2][:], X[:, 4 * q:4 * q + 4, :],
                                                ALU.add).then_inc(res_ready, 1)
                        dve.wait_ge(res_ready, q + 1)
                        for j in range(4):
                            nc.vector.bn_stats(stats[:, 4 * q + j, :], RES[:, 4 * q + j, :]).then_inc(st_ready, 1)

        def narrow_operands(name, WQT, WKT, WVT, keys_from, QT, KT, VA, bias_q=None, bias_k=None, bv_row=None,
                            ones_row=None):
            s_ = lambda what: sem(f"{name}_{what}")
            ones_ready, q_ready, q_kept, k_ready, k_kept, v_ready, v_kept = [s_(w) for w in (
                "ones_ready q_ready q_kept k_ready k_kept v_ready v_kept").split()]
            scale = float(DH1) ** -0.5
            with ExitStack() as scope:
                def lps(what, shape):
                    return scope.enter_context(nc.psum_tensor(f"{name}_{what}", shape, F32))

                qp = [lps(f"qp{i}", [P, 4, S]) for i in range(2)]
                kp = [lps(f"kp{i}", [P, 4, S]) for i in range(2)]
                vp = [lps(f"vp{i}", [P, 4, D]) for i in range(2)]
                block = scope.enter_context(nc.Block())

                @block.gpsimd
                def _(pool):
                    nc.gpsimd.memset(VA[:, :, :, DH1:DH1 + 1], 1.0).then_inc(ones_ready, 1)

                @block.tensor
                def _(pe):
                    for q in range(B // 4):
                        need(pe, k_kept, q - 1)
                        nc.tensor.matmul(kp[q % 2][:], WKT[:], keys_from[:, 4 * q:4 * q + 4, :], start=True, stop=True).then_inc(k_ready, 1)
                        need(pe, q_kept, q - 1)
                        nc.tensor.matmul(qp[q % 2][:], WQT[:], XT[:, 4 * q:4 * q + 4, :], start=True, stop=True).then_inc(q_ready, 1)
                        need(pe, v_kept, q - 1)
                        for j in range(4):
                            ins = nc.tensor.matmul(vp[q % 2][:, j, :], keys_from[:, 4 * q + j, :], WVT[:],
                                                   start=True, stop=bv_row is None)
                            if bv_row is not None:
                                ins = nc.tensor.matmul(vp[q % 2][:, j, :], ones_row[:], bv_row[:], start=False, stop=True)
                        ins.then_inc(v_ready, 1)

                @block.scalar
                def _(act):
                    for q in range(B // 4):
                        act.wait_ge(k_ready, q + 1)
                        act_bias = 0.0 if bias_k is None else bias_k[:, 0:1]
                        nc.scalar.activation(KT[:, 4 * q:4 * q + 4, :], kp[q % 2][:], ACT.Identity, bias=act_bias).then_inc(k_kept, 1)
                        act.wait_ge(v_ready, q + 1)
                        nc.scalar.copy(VA[:, 4 * q:4 * q + 4, :, 0:DH1],
                                       vp[q % 2][:].rearrange("p b (h d) -> p b h d", d=DH1)).then_inc(v_kept, 1)

                @block.vector
                def _(dve):
                    for q in range(B // 4):
                        dve.wait_ge(q_ready, q + 1)
                        if bias_q is None:
                            ins = nc.vector.tensor_scalar(QT[:, 4 * q:4 * q + 4, :], qp[q % 2][:], scale, None, ALU.mult)
                        else:
                            ins = nc.vector.tensor_scalar(QT[:, 4 * q:4 * q + 4, :], qp[q % 2][:], bias_q[:, 0:1], scale,
                                                          ALU.add, ALU.mult)
                        ins.then_inc(q_kept, 1)

        def gated_layer():
            s_ = lambda what: sem(f"gl_{what}")
            (landed, cleared, wc_ready, xc_ready, xc_kept, st_ready, ag_ready, ve_ready, rs_ready, sc_ready, bi_ready,
             xa_ready) = [s_(w) for w in (
                 "landed cleared wc_ready xc_ready xc_kept st_ready ag_ready ve_ready rs_ready sc_ready bi_ready "
                 "xa_ready").split()]
            G2 = 2 * G
            with ExitStack() as scope:
                def lsb(what, shape, dt=F32):
                    return scope.enter_context(nc.sbuf_tensor(f"gl_{what}", shape, dt))

                W = lsb("W", [P, D])
                groups = lsb("groups", [P, G])
                convw = lsb("convw", [P, 2])
                WC = lsb("WC", [P, G2])
                chan = lsb("chan", [G2, 3])
                LW = lsb("LW", [G2 + 1, 2 * D])
                XC = lsb("XC", [G2, B, S])
                XA = lsb("XA", [G2 + 1, B, S])
                bst = lsb("bst", [G2, 4, 6])
                bag = lsb("bag", [G2, 2])
                brs = lsb("brs", [G2, 1])
                bhalf = lsb("bhalf", [G2, 1])
                bsc = lsb("bsc", [G2, 1])
                bms = lsb("bms", [G2, 1])
                bbi = lsb("bbi", [G2, 1])
                brow = lsb("brow", [1, D])
                ones1 = lsb("ones1", [1, P])
                ms_ready = s_("ms_ready")

                with ExitStack() as inner:
                    xcp = [inner.enter_context(nc.psum_tensor(f"gl_xcp{i}", [G2, 4, S], F32)) for i in range(4)]
                    block = inner.enter_context(nc.Block())

                    @block.sync
                    def _(sp):
                        sp.dma_start(convw[:], a["convw"]).then_inc(landed, 16)
                        sp.dma_start(groups[:], a["groups"]).then_inc(landed, 16)
                        sp.dma_start(chan[:], a["chan"]).then_inc(landed, 16)
                        sp.dma_start(W[:], a["ffw"]).then_inc(landed, 16)
                        sp.dma_start(brow[:], a["ffb"]).then_inc(landed, 16)
                        sp.wait_ge(cleared, 1)
                        sp.dma_start(LW[0:G, 0:D], a["lwo"]).then_inc(landed, 16)
                        sp.dma_start(LW[G:G2, D:2 * D], a["lwi"]).then_inc(landed, 16)
                        sp.dma_start(LW[G2:G2 + 1, 0:D], a["lbo"]).then_inc(landed, 16)
                        sp.dma_start(LW[G2:G2 + 1, D:2 * D], a["lbi"]).then_inc(landed, 16)
                        sp.wait_ge(landed, 16 * 9)

                    @block.gpsimd
                    def _(pool):
                        nc.gpsimd.memset(LW[:], 0.0).then_inc(cleared, 1)
                        nc.gpsimd.memset(bhalf[:], -0.5).then_inc(cleared, 1)
                        pool.wait_ge(landed, 16 * 9)
                        for v in range(2):
                            nc.gpsimd.tensor_scalar(WC[:, G * v:G * v + G], groups[:], convw[:, v:v + 1], None,
                                                    ALU.mult).then_inc(wc_ready, 1)
                        pool.wait_ge(ve_ready, 1)
                        pool.wait_ge(cleared, 2)
                        nc.gpsimd.tensor_tensor(brs[:], brs[:], bhalf[:], ALU.pow).then_inc(rs_ready, 1)

                    @block.tensor
                    def _(pe):
                        pe.wait_ge(wc_ready, 2)
                        for q in range(4):
                            nc.tensor.matmul(xcp[q][:], WC[:], XT[:, 4 * q:4 * q + 4, :], start=True, stop=True).then_inc(xc_ready, 1)

                    @block.scalar
                    def _(act):
                        act.wait_ge(landed, 16 * 9)
                        for q in range(4):
                            act.wait_ge(xc_ready, q + 1)
                            nc.scalar.activation(XC[:, 4 * q:4 * q + 4, :], xcp[q][:], ACT.Identity, bias=chan[:, 0:1]).then_inc(xc_kept, 1)
                        act.wait_ge(bi_ready, 1)
                        for q in range(4):
                            nc.scalar.activation(XA[0:G2, 4 * q:4 * q + 4, :], XC[:, 4 * q:4 * q + 4, :], ACT.Gelu,
                                                 bias=bbi[:], scale=bsc[:]).then_inc(xa_ready, 1)

                    @block.vector
                    def _(dve):
                        nc.vector.memset(XA[G2:G2 + 1], 1.0)
                        nc.vector.memset(ones1[:], 1.0)
                        for q in range(4):
                            dve.wait_ge(xc_kept, q + 1)
                            nc.vector.bn_stats(bst[:, q, :], XC[:, 4 * q:4 * q + 4, :].rearrange("p b s -> p (b s)")).then_inc(st_ready, 1)
                        dve.wait_ge(st_ready, 4)
                        nc.vector.bn_aggr(bag[:], bst[:].rearrange("p q s -> p (q s)")).then_inc(ag_ready, 1)
                        dve.wait_ge(ag_ready, 1)
                        nc.vector.tensor_scalar(brs[:], bag[:, 1:2], EPS, None, ALU.add).then_inc(ve_ready, 1)
                        dve.wait_ge(rs_ready, 1)
                        nc.vector.tensor_tensor(bsc[:], brs[:], chan[:, 1:2], ALU.mult).then_inc(sc_ready, 1)
                        dve.wait_ge(sc_ready, 1)
                        nc.vector.tensor_tensor(bms[:], bag[:, 0:1], bsc[:], ALU.mult).then_inc(ms_ready, 1)
                        dve.wait_ge(ms_ready, 1)
                        nc.vector.tensor_tensor(bbi[:], chan[:, 2:3], bms[:], ALU.subtract).then_inc(bi_ready, 1)

                (xs_ready, as_ready, lg_ready, mx_ready, e_ready, m_ready, w_ready, sel_ready, rs2_ready, nr_ready,
                 xg_ready, xt_ready, xt_kept, y_ready, full_ready, t1_ready, t2_ready, res_ready, bs_ready) = [s_(w) for w in (
                     "xs_ready as_ready lg_ready mx_ready e_ready m_ready w_ready sel_ready rs2_ready nr_ready "
                     "xg_ready xt_ready xt_kept y_ready full_ready t1_ready t2_ready res_ready bs_ready").split()]
                xs = lsb("xs", [P, 2, S])
                xas = lsb("xas", [G2 + 1, 2, S])
                nmx = lsb("nmx", [P, 2, 2])
                ex = lsb("ex", [P, 2, 2, D])
                ssum = lsb("ssum", [P, 2, 2])
                m8 = lsb("m8", [P, 2, 8])
                wk = lsb("wk", [P, 2, D])
                sel = lsb("sel", [P, 2, 2, D])
                rs2 = lsb("rs2", [P, 2, 2])
                nrs = lsb("nrs", [P, 2, 2])
                xg = lsb("xg", [P, 2, D])
                xgt = lsb("xgt", [P, 2, S])
                t1 = lsb("t1", [P, 2, D])
                t2 = lsb("t2", [P, 2, D])
                lgp = [scope.enter_context(nc.psum_tensor(f"gl_lgp{i}", [P, 2, D], F32)) for i in range(2)]
                fup = [scope.enter_context(nc.psum_tensor(f"gl_fup{i}", [P, D], F32)) for i in range(2)]
                xtp = scope.enter_context(nc.psum_tensor("gl_xtp", [P, S], F32))
                y2p = scope.enter_context(nc.psum_tensor("gl_y2p", [P, D], F32))
                block = scope.enter_context(nc.Block())
                ROUNDS = TOPK // 8

                def run(eng, slot):
                    slot(0, 0, lambda lag: lag == 0)
                    slot(1, 1, lambda lag: True)
                    with eng.Fori(1, B // 2) as i:
                        for r in range(2):
                            slot(2 * i + r, r, lambda lag: True)
                    slot(B, 0, lambda lag: lag == 1)

                @block.gpsimd
                def _(pool):
                    def slot(b, r, live):
                        if live(0):
                            need(pool, lg_ready, b - 1)
                            nc.gpsimd.tensor_copy(xas[:, r, :], XA[:, b, :]).then_inc(as_ready, 1)
                            need(pool, full_ready, b - 1)
                            nc.gpsimd.tensor_copy(xs[:, r, :], XT[:, b, :]).then_inc(xs_ready, 1)
                    run(pool, slot)

                @block.tensor
                def _(pe):
                    def slot(b, r, live):
                        if live(0):
                            pe.wait_ge(as_ready, b + 1)
                            need(pe, e_ready, 2 * b - 2)
                            nc.tensor.matmul(lgp[r][:], xas[:, r, :], LW[:], start=True, stop=True).then_inc(lg_ready, 1)
                            pe.wait_ge(xs_ready, b + 1)
                            need(pe, t1_ready, b - 1)
                            nc.tensor.matmul(fup[r][:], xs[:, r, :], W[:], start=True, stop=True).then_inc(full_ready, 1)
                        if live(1):
                            n = b - 1
                            pe.wait_ge(xg_ready, n + 1)
                            need(pe, xt_kept, n)
                            nc.tensor.transpose(xtp[:], xg[:, 1 - r, :], ident[:]).then_inc(xt_ready, 1)
                            pe.wait_ge(xt_kept, n + 1)
                            need(pe, res_ready, n)
                            nc.tensor.matmul(y2p[:], xgt[:, 1 - r, :], W[:], start=True, stop=False)
                            nc.tensor.matmul(y2p[:], ones1[:], brow[:], start=False, stop=True).then_inc(y_ready, 1)
                    run(pe, slot)

                @block.scalar
                def _(act):
                    def slot(b, r, live):
                        if live(0):
                            act.wait_ge(mx_ready, b + 1)
                            need(act, xg_ready, b - 1)
                            need(act, t1_ready, b - 1)
                            for v in range(2):
                                nc.scalar.activation(ex[:, r, v, :], lgp[r][:, v, :], ACT.Exp, bias=nmx[:, r, v:v + 1],
                                                     accum_out=ssum[:, r, v:v + 1]).then_inc(e_ready, 1)
                        if live(1):
                            act.wait_ge(xt_ready, b)
                            need(act, y_ready, b - 1)
                            nc.scalar.copy(xgt[:, 1 - r, :], xtp[:]).then_inc(xt_kept, 1)
                    run(act, slot)

                @block.vector
                def _(dve):
                    def slot(b, r, live):
                        if live(0):
                            dve.wait_ge(lg_ready, b + 1)
                            need(dve, e_ready, 2 * b - 2)
                            nc.vector.tensor_reduce(nmx[:, r, :], lgp[r][:], AX.X, ALU.max, negate=True).then_inc(mx_ready, 1)
                        if live(1):
                            n = b - 1
                            dve.wait_ge(y_ready, n + 1)
                            dve.wait_ge(t2_ready, n + 1)
                            nc.vector.tensor_tensor(RES[:, n, :], y2p[:], t2[:, 1 - r, :], ALU.add).then_inc(res_ready, 1)
                            dve.wait_ge(res_ready, n + 1)
                            nc.vector.bn_stats(stats[:, n, :], RES[:, n, :]).then_inc(bs_ready, 1)
                        if live(0):
                            dve.wait_ge(e_ready, 2 * b + 2)
                            nc.vector.reciprocal(rs2[:, r, :], ssum[:, r, :]).then_inc(rs2_ready, 1)
                            dve.sem_clear(m_ready)
                            dve.sem_clear(w_ready)
                            for z in range(ROUNDS):
                                for v in range(2):
                                    w = ex[:, r, v, :] if z == 0 else wk[:, v, :]
                                    if z:
                                        dve.wait_ge(w_ready, 2 * (z - 1) + v + 1)
                                    nc.vector.max(m8[:, v, :], w).then_inc(m_ready, 1)
                                for v in range(2):
                                    w = ex[:, r, v, :] if z == 0 else wk[:, v, :]
                                    dve.wait_ge(m_ready, 2 * z + v + 1)
                                    nc.vector.match_replace(wk[:, v, :], m8[:, v, :], w, -1.0).then_inc(w_ready, 1)
                            dve.wait_ge(rs2_ready, b + 1)
                            nc.vector.tensor_scalar(nrs[:, r, :], rs2[:, r, :], -1.0, None, ALU.mult).then_inc(nr_ready, 1)
                            for v in (1, 0):
                                dve.wait_ge(w_ready, 2 * ROUNDS)
                                nc.vector.scalar_tensor_tensor(sel[:, r, v, :], wk[:, v, :], 0.0, ex[:, r, v, :],
                                                               ALU.max, ALU.subtract).then_inc(sel_ready, 1)
                            dve.wait_ge(nr_ready, b + 1)
                            dve.wait_ge(sel_ready, 2 * b + 2)
                            need(dve, xt_ready, b - 1)
                            nc.vector.scalar_tensor_tensor(xg[:, r, :], sel[:, r, 1, :], nrs[:, r, 1:2], X[:, b, :],
                                                           ALU.mult, ALU.mult).then_inc(xg_ready, 1)
                            dve.wait_ge(full_ready, b + 1)
                            nc.vector.scalar_tensor_tensor(t1[:, r, :], sel[:, r, 0, :], nrs[:, r, 0:1], fup[r][:],
                                                           ALU.mult, ALU.mult).then_inc(t1_ready, 1)
                            dve.wait_ge(t1_ready, b + 1)
                            nc.vector.tensor_tensor(t2[:, r, :], t1[:, r, :], X[:, b, :], ALU.add).then_inc(t2_ready, 1)
                    run(dve, slot)

        def experts():
            s_ = lambda what: sem(f"moe_{what}")
            (landed, lg_ready, mx_ready, d_ready, e_ready, sum_ready, rc_ready, sc_ready, v8_ready, i8_ready, if_ready,
             den_ready, rden_ready, wt_ready, eq_ready, pr_ready, comb_ready, ct_ready, ct_kept, db_ready, acc_ready,
             cst_ready) = [
                s_(w) for w in ("landed lg_ready mx_ready d_ready e_ready sum_ready rc_ready sc_ready v8_ready i8_ready "
                                "if_ready den_ready rden_ready wt_ready eq_ready pr_ready comb_ready ct_ready ct_kept "
                                "db_ready acc_ready cst_ready").split()]
            with ExitStack() as scope:
                def lsb(what, shape, dt=F32):
                    return scope.enter_context(nc.sbuf_tensor(f"moe_{what}", shape, dt))

                GPT = lsb("GPT", [P, E, F])
                UPT = lsb("UPT", [P, E, F])
                DWT = lsb("DWT", [FP, FC, E, D])
                gb = lsb("gb", [FP, E, FC])
                ub = lsb("ub", [FP, E, FC])
                gwT = lsb("gwT", [P, E])
                gbr = lsb("gbr", [1, E])
                ones1 = lsb("ones1", [1, P])
                db = lsb("db", [E, D])
                number = lsb("number", [P, E])
                comb = lsb("comb", [P, B, E])
                combT = lsb("combT", [E, B, S])
                with ExitStack() as inner:
                    def isb(what, shape, dt=F32):
                        return inner.enter_context(nc.sbuf_tensor(f"moe_{what}", shape, dt))

                    mx = isb("mx", [P, B])
                    df = isb("df", [P, B, E])
                    ee = isb("ee", [P, B, E])
                    su = isb("su", [P, B])
                    rc = isb("rc", [P, B])
                    score = isb("score", [P, B, E])
                    v8 = isb("v8", [P, B, 8])
                    i8 = isb("i8", [P, B, 8], U32)
                    i8f = isb("i8f", [P, B, 8])
                    den = isb("den", [P, B])
                    rden = isb("rden", [P, B])
                    wt = isb("wt", [P, B, 2])
                    eq = isb("eq", [P, 2, B, E])
                    pr = isb("pr", [P, 2, B, E])
                    glp = inner.enter_context(nc.psum_tensor("moe_glp", [P, B, E], F32))
                    ctp = [inner.enter_context(nc.psum_tensor(f"moe_ctp{i}", [E, 4, S], F32)) for i in range(2)]
                    dbp = [inner.enter_context(nc.psum_tensor(f"moe_dbp{i}", [P, 4, D], F32)) for i in range(2)]
                    block = inner.enter_context(nc.Block())

                    @block.sync
                    def _(sp):
                        sp.dma_start(gwT[:], a["gwT"]).then_inc(landed, 16)
                        sp.dma_start(gbr[:], a["gbr"]).then_inc(landed, 16)
                        sp.dma_start(db[:], a["db"]).then_inc(landed, 16)
                        sp.dma_start(number[:], a["number"]).then_inc(landed, 16)
                        sp.dma_start(GPT[:], a["gpT"]).then_inc(landed, 16)
                        sp.dma_start(UPT[:], a["upT"]).then_inc(landed, 16)
                        sp.dma_start(DWT[:], a["dwT"]).then_inc(landed, 16)
                        sp.dma_start(gb[:], a["gpb"]).then_inc(landed, 16)
                        sp.dma_start(ub[:], a["upb"]).then_inc(landed, 16)
                        sp.wait_ge(landed, 16 * 9)

                    @block.gpsimd
                    def _(pool):
                        nc.gpsimd.memset(ones1[:], 1.0).then_inc(cst_ready, 1)

                    @block.tensor
                    def _(pe):
                        pe.wait_ge(cst_ready, 1)
                        pe.wait_ge(landed, 16 * 9)
                        for b in range(B):
                            nc.tensor.matmul(glp[:, b, :], XT[:, b, :], gwT[:], start=True, stop=False)
                            ins = nc.tensor.matmul(glp[:, b, :], ones1[:], gbr[:], start=False, stop=True)
                        ins.then_inc(lg_ready, 1)
                        pe.wait_ge(comb_ready, 1)
                        for q in range(4):
                            need(pe, ct_kept, q - 1)
                            for j in range(4):
                                ins = nc.tensor.transpose(ctp[q % 2][:, j, :], comb[:, 4 * q + j, :], ident[:])
                            ins.then_inc(ct_ready, 1)
                            pe.wait_ge(ct_kept, q + 1)
                            need(pe, acc_ready, q - 1)
                            for j in range(4):
                                ins = nc.tensor.matmul(dbp[q % 2][:, j, :], combT[:, 4 * q + j, :], db[:], start=True, stop=True)
                            ins.then_inc(db_ready, 1)

                    @block.scalar
                    def _(act):
                        act.wait_ge(d_ready, 1)
                        nc.scalar.activation(ee[:], df[:], ACT.Exp).then_inc(e_ready, 1)
                        for q in range(4):
                            act.wait_ge(ct_ready, q + 1)
                            nc.scalar.copy(combT[:, 4 * q:4 * q + 4, :], ctp[q % 2][:]).then_inc(ct_kept, 1)

                    @block.vector
                    def _(dve):
                        bc = lambda ap: ap.unsqueeze(2).to_broadcast([P, B, E])
                        dve.wait_ge(lg_ready, 1)
                        nc.vector.tensor_reduce(mx[:], glp[:], AX.X, ALU.max).then_inc(mx_ready, 1)
                        dve.wait_ge(mx_ready, 1)
                        nc.vector.tensor_tensor(df[:], glp[:], bc(mx[:]), ALU.subtract).then_inc(d_ready, 1)
                        dve.wait_ge(e_ready, 1)
                        nc.vector.tensor_reduce(su[:], ee[:], AX.X, ALU.add).then_inc(sum_ready, 1)
                        dve.wait_ge(sum_ready, 1)
                        nc.vector.reciprocal(rc[:], su[:]).then_inc(rc_ready, 1)
                        dve.wait_ge(rc_ready, 1)
                        nc.vector.tensor_tensor(score[:], ee[:], bc(rc[:]), ALU.mult).then_inc(sc_ready, 1)
                        dve.wait_ge(sc_ready, 1)
                        for b in range(B):
                            nc.vector.max(v8[:, b, :], score[:, b, :]).then_inc(v8_ready, 1)
                        for b in range(B):
                            dve.wait_ge(v8_ready, b + 1)
                            nc.vector.max_index(i8[:, b, :], v8[:, b, :], score[:, b, :]).then_inc(i8_ready, 1)
                        dve.wait_ge(i8_ready, B)
                        nc.vector.tensor_copy(i8f[:], i8[:]).then_inc(if_ready, 1)
                        nc.vector.tensor_tensor(den[:], v8[:, :, 0], v8[:, :, 1], ALU.add).then_inc(den_ready, 1)
                        dve.wait_ge(den_ready, 1)
                        nc.vector.tensor_scalar(den[:], den[:], 1e-20, None, ALU.add).then_inc(den_ready, 1)
                        dve.wait_ge(den_ready, 2)
                        nc.vector.reciprocal(rden[:], den[:]).then_inc(rden_ready, 1)
                        dve.wait_ge(rden_ready, 1)
                        nc.vector.tensor_tensor(wt[:], v8[:, :, 0:2], rden[:].unsqueeze(2).to_broadcast([P, B, 2]),
                                                ALU.mult).then_inc(wt_ready, 1)
                        dve.wait_ge(if_ready, 1)
                        for z in range(2):
                            nc.vector.tensor_tensor(eq[:, z], number[:].unsqueeze(1).to_broadcast([P, B, E]), bc(i8f[:, :, z]),
                                                    ALU.is_equal).then_inc(eq_ready, 1)
                        dve.wait_ge(wt_ready, 1)
                        for z in range(2):
                            dve.wait_ge(eq_ready, z + 1)
                            nc.vector.tensor_tensor(pr[:, z], eq[:, z], bc(wt[:, :, z]), ALU.mult).then_inc(pr_ready, 1)
                        dve.wait_ge(pr_ready, 2)
                        nc.vector.tensor_tensor(comb[:], pr[:, 0], pr[:, 1], ALU.add).then_inc(comb_ready, 1)
                        for q in range(4):
                            dve.wait_ge(db_ready, q + 1)
                            nc.vector.tensor_tensor(RES[:, 4 * q:4 * q + 4, :], dbp[q % 2][:], X[:, 4 * q:4 * q + 4, :],
                                                    ALU.add).then_inc(acc_ready, 1)

                (g_ready, u_ready, g_kept, h_ready, h_kept, dn_ready, sum2_ready, st_ready) = [
                    s_(w) for w in "g_ready u_ready g_kept h_ready h_kept dn_ready sum2_ready st_ready".split()]
                UN = E * FC
                gs = lsb("gs", [FP, 2, 4, S])
                h0 = lsb("h0", [FP, 2, 4, S])
                hs = lsb("hs", [FP, 2, 4, S])
                gp = [scope.enter_context(nc.psum_tensor(f"moe_gp{i}", [FP, 4, S], F32)) for i in range(2)]
                up = [scope.enter_context(nc.psum_tensor(f"moe_up{i}", [FP, 4, S], F32)) for i in range(2)]
                dn = [scope.enter_context(nc.psum_tensor(f"moe_dn{i}", [P, 4, D], F32)) for i in range(2)]
                block = scope.enter_context(nc.Block())

                def run(eng, slot):
                    for j in range(UN):
                        slot(0, j, lambda lag: j >= lag)
                    with eng.Fori(1, B // 4) as q:
                        for j in range(UN):
                            slot(q, j, lambda lag: True)
                    for j in range(2):
                        slot(B // 4, j, lambda lag: j < lag)

                @block.tensor
                def _(pe):
                    def slot(q, j, live):
                        k = UN * q + j
                        if live(0):
                            e, f = j // FC, j % FC
                            need(pe, g_kept, k - 1)
                            rhs = XT[:, bass.ds(4 * q, 4), :]
                            nc.tensor.matmul(gp[j % 2][:], GPT[:, e, FP * f:FP * f + FP], rhs, start=True, stop=True).then_inc(g_ready, 1)
                            need(pe, h_ready, k - 1)
                            nc.tensor.matmul(up[j % 2][:], UPT[:, e, FP * f:FP * f + FP], rhs, start=True, stop=True).then_inc(u_ready, 1)
                        if live(2):
                            e, f = ((j - 2) // FC) % E, (j - 2) % FC
                            pe.wait_ge(h_kept, k - 1)
                            if f == 0:
                                need(pe, sum2_ready, 4 * (E * q + (j - 2) // FC - 1))
                            for t in range(4):
                                ins = nc.tensor.matmul(dn[e % 2][:, t, :], hs[:, j % 2, t, :], DWT[:, f, e, :],
                                                       start=(f == 0 and t == 0), stop=(f == FC - 1),
                                                       skip_group_check=True)
                            ins.then_inc(dn_ready, 1)
                    run(pe, slot)

                @block.scalar
                def _(act):
                    def slot(q, j, live):
                        k = UN * q + j
                        if live(0):
                            e, f = j // FC, j % FC
                            act.wait_ge(g_ready, k + 1)
                            need(act, h_ready, k - 1)
                            nc.scalar.activation(gs[:, j % 2], gp[j % 2][:], ACT.Identity, bias=gb[:, e, f:f + 1]).then_inc(g_kept, 1)
                        if live(1):
                            act.wait_ge(h_ready, k)
                            need(act, dn_ready, k - 2)
                            nc.scalar.activation(hs[:, (j - 1) % 2], h0[:, (j - 1) % 2], ACT.Silu).then_inc(h_kept, 1)
                    run(act, slot)

                @block.vector
                def _(dve):
                    def slot(q, j, live):
                        k = UN * q + j
                        if live(0):
                            e, f = j // FC, j % FC
                            dve.wait_ge(u_ready, k + 1)
                            dve.wait_ge(g_kept, k + 1)
                            need(dve, h_kept, k - 1)
                            nc.vector.scalar_tensor_tensor(h0[:, j % 2], up[j % 2][:], ub[:, e, f:f + 1], gs[:, j % 2],
                                                           ALU.add, ALU.mult).then_inc(h_ready, 1)
                        if live(2) and j % FC == 1:
                            e, qq = ((j - 2) // FC) % E, q + (j - 2) // UN
                            dve.wait_ge(dn_ready, k - 1)
                            for t in range(4):
                                b = 4 * qq + t
                                need(dve, sum2_ready, 4 * (E * q + (j - 2) // FC) + t - 3)
                                nc.vector.scalar_tensor_tensor(RES[:, b, :], dn[e % 2][:, t, :], comb[:, b, e:e + 1],
                                                               RES[:, b, :], ALU.mult, ALU.add).then_inc(sum2_ready, 1)
                            if e == E - 1:
                                dve.wait_ge(sum2_ready, 4 * (E * q + (j - 2) // FC) + 4)
                                for t in range(4):
                                    b = 4 * qq + t
                                    nc.vector.bn_stats(stats[:, b, :], RES[:, b, :]).then_inc(st_ready, 1)
                    run(dve, slot)

        with ExitStack() as l0:
            def lsb(name, shape, dt=F32):
                return l0.enter_context(nc.sbuf_tensor(name, shape, dt))

            ZM = lsb("ZM", [P, H, D])
            WQ0 = lsb("WQ0", [DH0, H, D])
            WK0 = lsb("WK0", [DH0, H, D])
            WVT0 = lsb("WVT0", [P, H * DH0])
            WO0 = lsb("WO0", [P, H * DH0 // P, D])
            causal = lsb("causal", [P, S], BF16)
            zm_ready, zms_ready = sem("zm_ready"), sem("zms_ready")
            with ExitStack() as scope:
                zmp = [scope.enter_context(nc.psum_tensor(f"zmp{i}", [P, 4, D], F32)) for i in range(4)]
                block = scope.enter_context(nc.Block())

                @block.sync
                def _(sp):
                    sp.dma_start(WQ0[:], a["wq0"]).then_inc(loaded, 16)
                    sp.dma_start(WK0[:], a["wk0"]).then_inc(loaded, 16)
                    sp.dma_start(XT[:], a["xT"]).then_inc(loaded, 16)
                    sp.dma_start(X[:], a["x"].rearrange("b t c -> t b c")).then_inc(loaded, 16)
                    sp.wait_ge(loaded, 16 * 10)

                @block.gpsimd
                def _(pool):
                    nc.gpsimd.memset(half[:], -0.5)

                @block.scalar
                def _(act):
                    act.dma_start(WVT0[:], a["wvT0"]).then_inc(loaded, 16)
                    act.dma_start(WO0[:], a["wo0"]).then_inc(loaded, 16)
                    act.dma_start(ident[:], a["ident"]).then_inc(loaded, 16)
                    act.dma_start(ident16[:], a["ident16"]).then_inc(loaded, 16)
                    act.dma_start(causal[:], a["causal"]).then_inc(loaded, 16)
                    act.dma_start(CTXT[:], a["ctxT"]).then_inc(loaded, 16)
                    for q in range(4):
                        act.wait_ge(zm_ready, q + 1)
                        nc.scalar.mul(ZM[:, 4 * q:4 * q + 4, :], zmp[q][:], float(DH0) ** -0.5).then_inc(zms_ready, 1)

                @block.tensor
                def _(pe):
                    pe.wait_ge(loaded, 16 * 10)
                    for q in range(4):
                        for j in range(4):
                            h = 4 * q + j
                            ins = nc.tensor.matmul(zmp[q][:, j, :], WK0[:, h, :], WQ0[:, h, :], start=True, stop=True)
                        ins.then_inc(zm_ready, 1)

            attention("a0", True, causal, WO0, ZM=ZM, WVT=WVT0)
        with ExitStack() as l0:
            XTt = l0.enter_context(nc.sbuf_tensor("XTt", [P, S + 2 * C, B], F32))
            YT = l0.enter_context(nc.sbuf_tensor("YT", [P, S, B], F32))
            layernorm("ln0", also_time_major=XTt[:, 0:S, :])
            recurrence(XTt, YT)
            add_recurrence(YT)
        layernorm("ln1")
        part_ends()

        gated_layer()
        layernorm("ln2")
        part_ends()

        with ExitStack() as l1:
            def lsb(name, shape, dt=F32):
                return l1.enter_context(nc.sbuf_tensor(name, shape, dt))

            W1 = lsb("W1", [P, 8, D])
            window = lsb("window", [P, S], BF16)
            jmask = lsb("jmask", [P, HU])
            umask = lsb("umask", [P, NU])
            colb = lsb("colb", [P, 2])
            rowb = lsb("rowb", [1, 2, D])
            ones1 = lsb("ones1", [1, P])
            QT = lsb("QT", [P, B, S])
            KT = lsb("KT", [P, B, S])
            VA = lsb("VA", [P, B, H, DH1 + 1])
            w1_landed = sem("w1_landed")
            with nc.Block() as block:
                @block.sync
                def _(sp):
                    for dst, name in ((W1, "w1"), (window, "window"), (jmask, "jmask"), (umask, "umask"), (colb, "colb"), (rowb, "rowb")):
                        sp.dma_start(dst[:], a[name]).then_inc(w1_landed, 16)
                    sp.wait_ge(w1_landed, 16 * 6)

                @block.gpsimd
                def _(pool):
                    nc.gpsimd.memset(ones1[:], 1.0)

            w = lambda n: W1[:, n, :]
            narrow_operands("n1", w(0), w(1), w(2), XT, QT, KT, VA)
            attention("a1", False, window, W1[:, 3:4, :], QT=QT, KT=KT, VA=VA, jmask=jmask, umask=umask)
            layernorm("ln3")
            part_ends()
            narrow_operands("n2", w(4), w(5), w(6), CTXT, QT, KT, VA, bias_q=colb[:, 0:1], bias_k=colb[:, 1:2],
                            bv_row=rowb[:, 0, :], ones_row=ones1)
            attention("a2", False, None, W1[:, 7:8, :], QT=QT, KT=KT, VA=VA, jmask=jmask, umask=umask, maskint=a["mask"],
                      bo_row=rowb[:, 1, :], ones_row=ones1)
        layernorm("ln4")
        part_ends()

        experts()
        layernorm("ln5", out_to=out)


def host_layout(inputs):
    n = {k: np.asarray(v) for k, v in inputs.items()}
    c = np.ascontiguousarray
    r = np.arange
    t, s = r(S)[:, None], r(S)[None, :]
    g = {
        "x": c(n["x"]),
        "xT": c(n["x"].transpose(2, 0, 1)),
        "ctxT": c(n["ctx_1024"].transpose(2, 0, 1)),
        "wq0": c(n["L0_attn_w_q"].transpose(1, 0, 2)),
        "wk0": c(n["L0_attn_w_k"].transpose(1, 0, 2)),
        "wvT0": c(n["L0_attn_w_v"].reshape(H * DH0, D).T),
        "wo0": c(n["L0_attn_w_o"].reshape(H * DH0 // P, P, D).transpose(1, 0, 2)),
        "ident": np.eye(P, dtype=np.float32),
        "ident16": np.eye(P, dtype=np.float32).astype(mybir.dt.np(BF16)),
        "causal": np.where(s > t, NEG, 0.0).astype(mybir.dt.np(BF16)),
    }
    sb_ = r(C * B)
    g["sel"] = (sb_[:, None] // B == r(C)[None, :]).astype(np.float32)
    g["same"] = np.tile((sb_[:, None] % B == sb_[None, :] % B).astype(np.float32)[:, None, :], (1, 2, 1))
    so, si = "L0_ffn_so_", "L0_ffn_si_"
    g["convw"] = c(np.stack([n[so + "conv_w"].reshape(D), n[si + "conv_w"].reshape(D)], 1))
    g["groups"] = (r(D)[:, None] // 4 == r(G)[None, :]).astype(np.float32)
    g["chan"] = c(np.stack([np.concatenate([n[v + w] for v in (so, si)]) for w in ("conv_b", "gamma", "beta")], 1))
    g["ffw"], g["ffb"] = c(n["L0_ffn_weight"]), c(n["L0_ffn_bias"][None])
    g["lwo"], g["lwi"] = c(n[so + "lin_w"].T), c(n[si + "lin_w"].T)
    g["lbo"], g["lbi"] = c(n[so + "lin_b"][None]), c(n[si + "lin_b"][None])
    g["w1"] = c(np.stack([n["L1_attn_W" + w].T for w in "qkvo"] + [n["L1_xattn_W" + w].T for w in "qkvo"], 1))
    g["window"] = np.where((s > t) | (s < t - 16), NEG, 0.0).astype(mybir.dt.np(BF16))
    g["jmask"] = (r(P)[:, None] % 32 // DH1 == r(HU)[None, :]).astype(np.float32)
    g["umask"] = (r(P)[:, None] // 32 == r(NU)[None, :]).astype(np.float32)
    g["colb"] = c(np.stack([n["L1_xattn_bq"], n["L1_xattn_bk"]], 1))
    g["rowb"] = c(np.stack([n["L1_xattn_bv"], n["L1_xattn_bo"]], 0)[None])
    g["mask"] = c(n["mask_Bx1xSxS2_if1"][:, 0])
    g["gwT"], g["gbr"] = c(n["L1_ffn_gate_w"].T), c(n["L1_ffn_gate_b"][None])
    g["db"] = c(n["L1_ffn_down_b"])
    g["number"] = np.tile(r(E).astype(np.float32)[None], (P, 1))
    g["gpT"], g["upT"] = c(n["L1_ffn_gp_w"].transpose(2, 0, 1)), c(n["L1_ffn_up_w"].transpose(2, 0, 1))
    g["dwT"] = c(n["L1_ffn_down_w"].reshape(E, D, FC, FP).transpose(3, 2, 0, 1))
    g["gpb"] = c(n["L1_ffn_gp_b"].reshape(E, FC, FP).transpose(2, 0, 1))
    g["upb"] = c(n["L1_ffn_up_b"].reshape(E, FC, FP).transpose(2, 0, 1))
    return g


def kernel(**inputs):
    import concourse.bacc as bacc
    from concourse.bass_utils import run_bass_kernel_spmd

    nc = bacc.Bacc("TRN2", target_bir_lowering=False, num_devices=1)
    arrays = {f"in_{name}": v for name, v in host_layout(inputs).items()}
    aps = {name[3:]: nc.dram_tensor(name, v.shape, mybir.dt.from_np(v.dtype), kind="ExternalInput").ap()
           for name, v in arrays.items()}
    out = nc.dram_tensor("out", (B, S, D), F32, kind="ExternalOutput").ap()
    decoder_program(nc, aps, out)
    return run_bass_kernel_spmd(nc, [arrays], core_ids=[0]).results[0]["out"]
```

```python
from contextlib import ExitStack

import numpy as np

import concourse.bass as bass
from concourse import mybir

F32 = mybir.dt.float32
BF16 = mybir.dt.bfloat16
FR = mybir.dt.float32r
I32 = mybir.dt.int32
U32 = mybir.dt.uint32
ALU = mybir.AluOpType
ACT = mybir.ActivationFunctionType
AX = mybir.AxisListType

B, S, D = 16, 128, 128
P = 128
H = 16
DH0 = 64
DH1 = D // H
HU = 4
NU = H // HU
SEG = HU * S
E, F = 8, 408
HID = E * F
NCH = -(-HID // P)
OWNERS = [(P * c // F, min(P * c + P - 1, HID) // F) for c in range(NCH)]
REAL = HID - P * (NCH - 1)
PLANES = sorted(set(OWNERS))
PLANE = [PLANES.index(o) for o in OWNERS]
NP = len(PLANES)
PB = 2
G = 32
TOPK = 32
C = 8
NBLK = S // C
LR = 1.0 / D
EPS = 1e-5
NEG = -(2.0 ** 100)


def need(eng, sem, value):
    if isinstance(value, int) and value <= 0:
        return
    eng.wait_ge(sem, value)


def decoder_program(nc, a, out):
    with ExitStack() as ctx:
        def sb(name, shape, dt=F32):
            return ctx.enter_context(nc.sbuf_tensor(name, shape, dt))

        part_sems = []

        def sem(name):
            part_sems.append(nc.alloc_semaphore(name=name))
            return part_sems[-1]

        def part_ends():
            nc.clear_and_free_semaphores(list(part_sems))
            part_sems.clear()
            nc.all_engine_barrier()

        X = sb("X", [P, B, D])
        XT = sb("XT", [P, B, S])
        RES = sb("RES", [P, B, D])
        CTXT = sb("CTXT", [P, B, S])
        ident = sb("ident", [P, P])
        ident16 = sb("ident16", [P, P], BF16)
        stats = sb("stats", [P, B, 6])
        moments = sb("moments", [P, B, 2])
        rstd = sb("rstd", [P, B])
        half = sb("half", [P, B])

        loaded = sem("loaded")

        gl_landed, w1_landed, moe_landed = [nc.alloc_semaphore(name=n) for n in ("gl_landed", "w1_landed", "moe_landed")]
        lw_cleared = sem("lw_cleared")
        G2 = 2 * G
        ffw = sb("ffw", [P, D])
        groups = sb("groups", [P, G])
        convw = sb("convw", [P, 2])
        chan = sb("chan", [G2, 3])
        LW = sb("LW", [G2 + 1, 2 * D])
        ffb = sb("ffb", [1, D])
        W1 = sb("W1", [P, 8, D])
        window = sb("window", [P, S], BF16)
        jmask = sb("jmask", [P, HU])
        umask = sb("umask", [P, NU])
        colb = sb("colb", [P, 2])
        bo = sb("bo", [1, D])
        bv = sb("bv", [P, D])
        maskint = sb("maskint", [P, B, S], I32)
        gwT = sb("gwT", [P, E])
        gbias = sb("gbias", [P, E])
        number = sb("number", [P, E])
        owner = sb("owner", [3 * 32, NP, P], BF16)
        DWT = sb("DWT", [P, NCH, D])
        gb = sb("gb", [P, NCH])
        ub = sb("ub", [P, NCH])
        gl_loads = [(ffw, "ffw"), (groups, "groups"), (convw, "convw"), (chan, "chan"), (ffb, "ffb")]
        gl_parts = [(LW[0:G, 0:D], "lwo"), (LW[G:G2, D:2 * D], "lwi"), (LW[G2:G2 + 1, 0:D], "lbo"),
                    (LW[G2:G2 + 1, D:2 * D], "lbi")]
        w1_loads = [(W1, "w1"), (window, "window"), (jmask, "jmask"), (umask, "umask"), (colb, "colb"), (bo, "bo"),
                    (maskint, "mask"), (bv, "bv")]
        moe_loads = [(gwT, "gwT"), (gbias, "gbias"), (number, "number"), (owner, "owner"), 
                     (DWT, "dwT"), (gb, "gpb"), (ub, "upb")]
        GL_LANDED = 16 * (len(gl_loads) + len(gl_parts))
        W1_LANDED, MOE_LANDED = 16 * len(w1_loads), 16 * len(moe_loads)

        def products3(out_ap, left, right, start=True, stop=True):
            (lh, ll), (rh, rl) = left, right
            nc.tensor.matmul(out_ap, lh, rh, start=start, stop=False)
            nc.tensor.matmul(out_ap, lh, rl, start=False, stop=False)
            return nc.tensor.matmul(out_ap, ll, rh, start=False, stop=stop)

        def layernorm(name, also_time_major=None, out_to=None, on_xt=None):
            stats_ready, var_ready, rstd_ready = sem(name + "_stats"), sem(name + "_var"), sem(name + "_rstd")
            x_ready, t_ready, xt_ready = sem(name + "_x"), sem(name + "_t"), sem(name + "_xt")
            with ExitStack() as scope:
                tp = [scope.enter_context(nc.psum_tensor(f"{name}_tp{i}", [P, 4, P], F32)) for i in range(2)]
                block = scope.enter_context(nc.Block())

                @block.vector
                def _(dve):
                    def aggregate(q):
                        for b in range(4 * q, 4 * q + 4):
                            nc.vector.bn_aggr(moments[:, b, :], stats[:, b, :]).then_inc(stats_ready, 1)

                    aggregate(0)
                    for q in range(4):
                        if q < 3:
                            aggregate(q + 1)
                        dve.wait_ge(stats_ready, 4 * q + 4)
                        four = slice(4 * q, 4 * q + 4)
                        nc.vector.tensor_scalar(rstd[:, four], moments[:, four, 1], EPS, None, ALU.add).then_inc(var_ready, 1)
                    for b in range(B):
                        if b % 4 == 0:
                            dve.wait_ge(rstd_ready, b // 4 + 1)
                        nc.vector.tensor_scalar(X[:, b, :], RES[:, b, :], moments[:, b, 0:1], rstd[:, b:b + 1],
                                                ALU.subtract, ALU.mult).then_inc(x_ready, 1)

                @block.gpsimd
                def _(pool):
                    for q in range(4):
                        four = slice(4 * q, 4 * q + 4)
                        pool.wait_ge(var_ready, q + 1)
                        nc.gpsimd.tensor_tensor(rstd[:, four], rstd[:, four], half[:, four], ALU.pow).then_inc(rstd_ready, 1)

                if out_to is not None:
                    stored = sem(name + "_stored")
                    rows = out_to.rearrange("b t c -> t b c")

                    @block.sync
                    def _(sp):
                        for q in range(4):
                            sp.wait_ge(x_ready, 4 * q + 4)
                            sp.dma_start(rows[:, 4 * q:4 * q + 4, :], X[:, 4 * q:4 * q + 4, :]).then_inc(stored, 16)
                        sp.wait_ge(stored, 16 * 4)
                    return

                @block.tensor
                def _(pe):
                    for q in range(B // 4):
                        need(pe, xt_ready, q - 1)
                        for j in range(4):
                            pe.wait_ge(x_ready, 4 * q + j + 1)
                            ins = nc.tensor.transpose(tp[q % 2][:, j, :], X[:, 4 * q + j, :], ident[:])
                        ins.then_inc(t_ready, 1)
                        if on_xt is not None and q:
                            pe.wait_ge(xt_ready, q)
                            on_xt(q - 1)
                    if on_xt is not None:
                        pe.wait_ge(xt_ready, B // 4)
                        on_xt(B // 4 - 1)

                @block.scalar
                def _(act):
                    for q in range(B // 4):
                        act.wait_ge(t_ready, q + 1)
                        if also_time_major is not None:
                            nc.scalar.copy(also_time_major[:, :, 4 * q:4 * q + 4].rearrange("p t b -> p b t"), tp[q % 2][:])
                        nc.scalar.copy(XT[:, 4 * q:4 * q + 4, :], tp[q % 2][:]).then_inc(xt_ready, 1)

        def attention(name, wide, allowed, WO, ZM=None, WVT=None, QT=None, KT=None, VA=None, jmask=None, umask=None,
                      maskbias=None, bo_row=None, ones_row=None):
            DV = DH0 if wide else DH1
            VW = DV + 1
            NOT = HU * DV // P if wide else 1
            s_ = lambda what: sem(f"{name}_{what}")
            z_ready, zs_ready = s_("z_ready"), s_("zs_ready")
            stat_ready, v_ready, vs_ready = s_("stat_ready"), s_("v_ready"), s_("vs_ready")
            ones_ready = s_("ones_ready")
            s_ready, max_ready, e_ready, p_ready = s_("s_ready"), s_("max_ready"), s_("e_ready"), s_("p_ready")
            t_ready, pt_ready, pv_ready, rl_ready = s_("t_ready"), s_("pt_ready"), s_("pv_ready"), s_("rl_ready")
            on_ready, ot_ready, ots_ready = s_("on_ready"), s_("ot_ready"), s_("ots_ready")
            y_ready, res_ready, st_ready = s_("y_ready"), s_("res_ready"), s_("st_ready")
            keys_ready = s_("keys_ready")
            with ExitStack() as scope:
                def lsb(what, shape, dt=F32):
                    return scope.enter_context(nc.sbuf_tensor(f"{name}_{what}", shape, dt))

                def lps(what, shape):
                    return scope.enter_context(nc.psum_tensor(f"{name}_{what}", shape, F32))

                if wide:
                    stat = lsb("stat", [P, 2, S])
                else:
                    stat = [lsb("stath", [P, 2, NU, S], FR), lsb("statl", [P, 2, NU, S], FR)]
                Eb = lsb("E", [P, 2, HU, S])
                Pb = lsb("P", [P, 2, HU, S])
                PT = lsb("PT", [P, 2, HU, S])
                mx = lsb("mx", [P, 2, HU])
                rl = lsb("rl", [P, 2, HU])
                ON = lsb("ON", [P, 2, HU * DV if wide else D])
                OT = lsb("OT", [P, 2, max(NOT, 1), S])
                sp = [lps(f"sp{i}", [P, HU, S]) for i in range(2)]
                tp = [lps(f"tp{i}", [P, HU, S]) for i in range(2)]
                op = lps("op", [P, HU, VW])
                otp = lps("otp", [P, 2, S])
                yp = lps("yp", [P, D])
                if wide:
                    zp = lps("zp", [P, SEG])
                    zs = lsb("zs", [P, 2, SEG])
                    VS = lsb("VS", [P, 2, H, VW])
                else:
                    kx = [lsb("kxh", [P, 2, HU, S], FR), lsb("kxl", [P, 2, HU, S], FR)]
                def run(eng, slot, drain=4):
                    for j in range(8):
                        slot(0, j, lambda lag: j >= lag)
                    with eng.Fori(1, B // 2) as i:
                        for j in range(8):
                            slot(i, j, lambda lag: True)
                    for j in range(drain):
                        slot(B // 2, j, lambda lag: j < lag)

                block = scope.enter_context(nc.Block())

                @block.gpsimd
                def _(pool):
                    if wide:
                        nc.gpsimd.memset(VS[:, :, :, DV:VW], 1.0).then_inc(ones_ready, 1)

                    def slot(i, j, live):
                        k = 8 * i + j
                        if j % NU == 0 and live(0):
                            b = 2 * i + j // NU
                            r = j // NU
                            need(pool, s_ready, k - NU)
                            if wide:
                                need(pool, v_ready, 4 * i + 2 * r - 2)
                            if wide:
                                nc.gpsimd.tensor_copy(stat[:, r, :], XT[:, b, :]).then_inc(stat_ready, 1)
                            else:
                                for part in range(2):
                                    nc.gpsimd.tensor_tensor(
                                        stat[part][:, r], QT[part][:, b, :].bitcast(F32).unsqueeze(1).to_broadcast([P, NU, S]),
                                        umask[:].unsqueeze(2).to_broadcast([P, NU, S]), ALU.mult).then_inc(stat_ready, 1)
                                    nc.gpsimd.tensor_tensor(
                                        kx[part][:, r], KT[part][:, b, :].bitcast(F32).unsqueeze(1).to_broadcast([P, HU, S]),
                                        jmask[:].unsqueeze(2).to_broadcast([P, HU, S]), ALU.mult).then_inc(keys_ready, 1)

                    run(pool, slot, 0)

                @block.tensor
                def _(pe):
                    if wide:
                        pe.wait_ge(ones_ready, 1)

                    def slot(i, j, live):
                        k = 8 * i + j
                        u = j % NU
                        if wide and live(0):
                            need(pe, zs_ready, k)
                            if u in (2, 3):
                                need(pe, vs_ready, 4 * i + 2 * (j // NU) + u - 1)
                            for h in range(HU):
                                ins = nc.tensor.matmul(zp[:, S * h:S * h + S], ZM[:, HU * u + h, :],
                                                       XT[:, 2 * i + j // NU, :], start=True, stop=True)
                            ins.then_inc(z_ready, 1)
                        if live(4) and (wide or u == 3):
                            n = k - 4
                            need(pe, on_ready, n + 1)
                            need(pe, ots_ready, n if wide else (n - 3) // 4 if isinstance(n, int) else 2 * i + j // NU - 1)
                            for m in range(NOT):
                                src = ON[:, j % 2, P * m:P * m + P] if wide else ON[:, (j // NU + 1) % 2, :]
                                ins = nc.tensor.transpose(otp[:, m, :], src, ident[:])
                            ins.then_inc(ot_ready, 1)
                        if live(1):
                            n, r, v = k - 1, ((j - 1) // NU) % 2, (j - 1) % NU
                            parts = 1 if wide else 2
                            need(pe, stat_ready, parts * (2 * i + (j - 1) // NU + 1))
                            need(pe, e_ready, n - 1)
                            if wide:
                                pe.wait_ge(zs_ready, n + 1)
                                nc.tensor.matmul(sp[(j - 1) % 2][:], stat[:, r, :], zs[:, (j - 1) % 2, :], start=True, stop=False)
                            else:
                                need(pe, keys_ready, parts * (2 * i + (j - 1) // NU + 1))
                                products3(sp[(j - 1) % 2][:], [x[:, r, v, :] for x in stat], [x[:, r] for x in kx], stop=False)
                            bias = allowed[:] if maskbias is None else maskbias[:, 2 * i + (j - 1) // NU, :]
                            nc.tensor.matmul(sp[(j - 1) % 2][:], ident16[:], bias.unsqueeze(1).to_broadcast([P, HU, S]),
                                             start=False, stop=True).then_inc(s_ready, 1)
                        if wide and live(0) and u in (1, 2):
                            pe.wait_ge(zs_ready, k + 1)
                            r = j // NU
                            need(pe, stat_ready, 2 * i + r + 1)
                            nc.tensor.matmul(zp[:], stat[:, r, :], WVT[:, SEG * (u - 1):SEG * u],
                                             start=True, stop=True).then_inc(v_ready, 1)
                        if live(2):
                            n = k - 2
                            pe.wait_ge(p_ready, n + 1)
                            need(pe, pt_ready, n - 1)
                            for h in range(HU):
                                ins = nc.tensor.transpose(tp[j % 2][:, h, :], Pb[:, j % 2, h, :], ident[:])
                            ins.then_inc(t_ready, 1)
                        if live(3):
                            n, v = k - 3, (j - 3) % NU
                            r = ((j - 3) // NU) % 2
                            pe.wait_ge(pt_ready, n + 1)
                            need(pe, on_ready, n)
                            if wide:
                                need(pe, vs_ready, 4 * i + 2 * ((j - 3) // NU) + 2)
                            for h in range(HU):
                                hh = HU * v + h
                                vals = VS[:, r, hh, :] if wide else VA[:, 2 * i + (j - 3) // NU, hh, :]
                                ins = nc.tensor.matmul(op[:, h, :], PT[:, (j - 3) % 2, h, :], vals, start=True, stop=True)
                            ins.then_inc(pv_ready, 1)
                        if live(4) and (wide or u == 3):
                            n, v = k - 4, (j - 4) % NU
                            if wide:
                                pe.wait_ge(ots_ready, n + 1)
                                if v == 0:
                                    need(pe, res_ready, 2 * i + (j - 4) // NU)
                                for m in range(NOT):
                                    ins = nc.tensor.matmul(yp[:], OT[:, j % 2, m, :], WO[:, NOT * v + m, :],
                                                           start=(v == 0 and m == 0), stop=(v == NU - 1 and m == NOT - 1))
                            else:
                                bb = 2 * i + (j - 4) // NU
                                pe.wait_ge(ots_ready, bb + 1)
                                need(pe, res_ready, bb)
                                ins = nc.tensor.matmul(yp[:], OT[:, (j // NU + 1) % 2, 0, :], WO[:, 0, :],
                                                       start=True, stop=bo_row is None)
                                if bo_row is not None:
                                    ins = nc.tensor.matmul(yp[:], ones_row[:], bo_row[:], start=False, stop=True)
                            ins.then_inc(y_ready, 1)

                    run(pe, slot)

                @block.scalar
                def _(act):
                    def slot(i, j, live):
                        k = 8 * i + j
                        if wide and live(0):
                            act.wait_ge(z_ready, k + 1)
                            need(act, s_ready, k - 1)
                            nc.scalar.copy(zs[:, j % 2, :], zp[:]).then_inc(zs_ready, 1)
                        if live(2):
                            n = k - 2
                            act.wait_ge(t_ready, n + 1)
                            need(act, pv_ready, n - 1)
                            nc.scalar.copy(PT[:, j % 2], tp[j % 2][:]).then_inc(pt_ready, 1)
                        if live(1):
                            n = k - 1
                            act.wait_ge(e_ready, n + 1)
                            need(act, t_ready, n - 1)
                            nc.scalar.activation(Pb[:, (j - 1) % 2], Eb[:, (j - 1) % 2], ACT.Exp,
                                                 scale=1.0 if wide else float(DH1) ** -0.5).then_inc(p_ready, 1)

                    run(act, slot)

                @block.vector
                def _(dve):
                    def slot(i, j, live):
                        k = 8 * i + j
                        u = j % NU
                        if live(4) and (wide or u == 3):
                            n = k - 4
                            if wide:
                                dve.wait_ge(ot_ready, n + 1)
                                need(dve, y_ready, n - 1)
                                nc.vector.tensor_copy(OT[:, j % 2], otp[:]).then_inc(ots_ready, 1)
                            else:
                                bb = 2 * i + (j - 4) // NU
                                dve.wait_ge(ot_ready, bb + 1)
                                need(dve, y_ready, bb)
                                nc.vector.tensor_copy(OT[:, (j // NU + 1) % 2, 0, :], otp[:, 0, :]).then_inc(ots_ready, 1)
                        if live(1):
                            n, q = k - 1, (j - 1) % 2
                            dve.wait_ge(s_ready, n + 1)
                            need(dve, e_ready, n - 1)
                            nc.vector.tensor_reduce(mx[:, q, :], sp[q][:], AX.X, ALU.max).then_inc(max_ready, 1)
                            dve.wait_ge(max_ready, n + 1)
                            need(dve, p_ready, n - 1)
                            nc.vector.tensor_tensor(Eb[:, q], sp[q][:], mx[:, q, :].unsqueeze(2).to_broadcast([P, HU, S]),
                                                    ALU.subtract).then_inc(e_ready, 1)
                        if wide and live(0) and u in (1, 2):
                            r = j // NU
                            dve.wait_ge(v_ready, 4 * i + 2 * r + u)
                            need(dve, pv_ready, k - u - NU)
                            nc.vector.tensor_copy(VS[:, r, 8 * (u - 1):8 * u, 0:DV],
                                                  zp[:].rearrange("p (h d) -> p h d", d=DV)).then_inc(vs_ready, 1)
                        if live(3):
                            n, q = k - 3, (j - 3) % 2
                            dve.wait_ge(pv_ready, n + 1)
                            nc.vector.reciprocal(rl[:, q, :], op[:, :, DV]).then_inc(rl_ready, 1)
                            dve.wait_ge(rl_ready, n + 1)
                            if wide:
                                need(dve, ot_ready, n - 1)
                                o = ON[:, q, :]
                            else:
                                v, bb = (j - 3) % NU, 2 * i + (j - 3) // NU
                                need(dve, ot_ready, bb)
                                o = ON[:, ((j - 3) // NU) % 2, 32 * v:32 * v + 32]
                            nc.vector.tensor_tensor(o.rearrange("p (h d) -> p h d", d=DV), op[:, :, 0:DV],
                                                    rl[:, q, :].unsqueeze(2).to_broadcast([P, HU, DV]),
                                                    ALU.mult).then_inc(on_ready, 1)
                        if live(4) and u == 3:
                            b = 2 * i + (j - 4) // NU
                            dve.wait_ge(y_ready, (4 * b + 4) if wide else (b + 1))
                            nc.vector.tensor_tensor(RES[:, b, :], yp[:], X[:, b, :], ALU.add).then_inc(res_ready, 1)
                            dve.wait_ge(res_ready, b + 1)
                            nc.vector.bn_stats(stats[:, b, :], RES[:, b, :]).then_inc(st_ready, 1)

                    run(dve, slot)

        def recurrence(XTt, YT):
            s_ = lambda what: sem(f"rec_{what}")
            w0x_ready, w0x_kept = s_("w0x_ready"), s_("w0x_kept")
            (far_gram_ready, far_gram_kept, rp_ready, rpb_ready, xblk_ready, gram_ready, gram_kept, masked_ready, prod_ready,
             gb_ready, gb_kept, far_ready, ct_ready, ct_kept, near_ready, t0_ready, u_ready, ut_ready, ut_kept,
             p_ready, pr_ready, y_ready, yt_ready, sq_ready, gt_ready, q_ready, qr_ready, fin_ready, ra_ready,
             c_loaded) = [s_(w) for w in (
                 "far_gram_ready far_gram_kept rp_ready rpb_ready xblk_ready gram_ready gram_kept masked_ready prod_ready "
                 "gb_ready gb_kept far_ready ct_ready ct_kept near_ready t0_ready u_ready ut_ready ut_kept "
                 "p_ready pr_ready y_ready yt_ready sq_ready gt_ready q_ready qr_ready fin_ready ra_ready "
                 "c_loaded").split()]
            ut_landed = [s_(f"ut_landed{i}") for i in range(2)]
            CB = C * B
            NG = B * C * (C - 1) // 2
            first = [sum(B * (C - 1 - r) for r in range(s)) for s in range(C)]
            with ExitStack() as scope:
                def lsb(what, shape, dt=F32):
                    return scope.enter_context(nc.sbuf_tensor(f"rec_{what}", shape, dt))

                W0X = lsb("W0X", [P, B, S + 2 * C])
                same = lsb("same", [P, CB])
                lrs = lsb("lrs", [P, P])
                GF = lsb("GF", [P, B, S + 2 * C])
                UT = lsb("UT", [P, B, D])
                CF = lsb("CF", [P, 2, 1 + C, B])
                xblk = lsb("xblk", [P, 2, CB])
                prod = lsb("prod", [P, 2, NG])

                def products(k, j):
                    need(nc.gpsimd, gb_ready, k - 1)
                    for s in range(C - 1):
                        n = C - 1 - s
                        ins = nc.gpsimd.tensor_tensor(
                            prod[:, j, first[s]:first[s] + B * n].rearrange("p (t b) -> p t b", b=B),
                            XTt[:, bass.ds(C * k + s, 1), :].to_broadcast([P, n, B]),
                            XTt[:, bass.ds(C * k + s + 1, n), :], ALU.mult)
                    ins.then_inc(prod_ready, 1)

                def stationary(k, j):
                    nc.gpsimd.tensor_copy(xblk[:, j, :], XTt[:, bass.ds(C * k, C), :].rearrange("p t b -> p (t b)")
                                          ).then_inc(xblk_ready, 1)

                with ExitStack() as inner:
                    wp = [inner.enter_context(nc.psum_tensor(f"rec_wp{i}", [P, 4, S], F32)) for i in range(4)]
                    fgp = [inner.enter_context(nc.psum_tensor(f"rec_fgp{i}", [P, 4, S], F32)) for i in range(4)]
                    block = inner.enter_context(nc.Block())

                    @block.sync
                    def _(sp):
                        sp.dma_start(same[:], a["same"]).then_inc(c_loaded, 16)
                        sp.wait_ge(c_loaded, 16)

                    @block.gpsimd
                    def _(pool):
                        nc.gpsimd.memset(lrs[:], LR)
                        products(0, 0)
                        stationary(0, 0)
                        stationary(1, 1)
                        products(1, 1)
                        nc.gpsimd.memset(XTt[:, S:S + 3 * C, :], 0.0)
                        nc.gpsimd.memset(W0X[:, :, S:S + 2 * C], 0.0)

                    @block.tensor
                    def _(pe):
                        for q in range(4):
                            for r in range(4):
                                ins = nc.tensor.matmul(wp[q][:, r, :], CTXT[:, 4 * q + r, :], XT[:, 4 * q + r, :],
                                                       start=True, stop=True)
                            ins.then_inc(w0x_ready, 1)
                        for q in range(4):
                            for r in range(4):
                                ins = nc.tensor.matmul(fgp[q][:, r, :], XT[:, 4 * q + r, :], XT[:, 4 * q + r, :],
                                                       start=True, stop=True)
                            ins.then_inc(far_gram_ready, 1)

                    @block.scalar
                    def _(act):
                        for q in range(4):
                            act.wait_ge(w0x_ready, q + 1)
                            nc.scalar.copy(W0X[:, 4 * q:4 * q + 4, 0:S], wp[q][:]).then_inc(w0x_kept, 1)

                    @block.vector
                    def _(dve):
                        nc.vector.memset(GF[:, :, S:S + 2 * C], 0.0)
                        nc.vector.memset(UT[:], 0.0)
                        nc.vector.memset(CF[:, 1, 0, :], 1.0)
                        for q in range(4):
                            dve.wait_ge(far_gram_ready, q + 1)
                            nc.vector.tensor_scalar(GF[:, 4 * q:4 * q + 4, 0:S], fgp[q][:], LR, None, ALU.mult).then_inc(far_gram_kept, 1)

                def lps(what, shape):
                    return scope.enter_context(nc.psum_tensor(f"rec_{what}", shape, F32))

                graw = [lsb("graw0", [P, 3, CB]), lsb("graw1", [P, 2, CB])]
                gm = [lsb("gm0", [P, 3, CB]), lsb("gm1", [P, 2, CB])]
                GB = lsb("GB", [P, 2, NG])
                cTk = lsb("cTk", [P, 2, D])
                uTk = lsb("uTk", [P, 2, D])
                pm = lsb("pm", [P, C, B])
                t0 = lsb("t0", [P, C, B])
                sq = lsb("sq", [P, 2, B])
                gt = lsb("gt", [P, 2, C - 1, B])
                qt = lsb("qt", [P, 2, C - 1, B])
                RA = lsb("RA", [P, B])
                U = lsb("U", [P, C, B])
                rp = lps("rp", [P, B, 2 * C])
                np_ = lps("np", [P, C, B])
                ctp, utp = lps("ctp", [P, D]), lps("utp", [P, D])
                gp = [lps("gp0", [P, 3, CB]), lps("gp1", [P, 2, CB])]
                gbp = [lps(f"gbp{i}", [P, NG]) for i in range(2)]
                block = scope.enter_context(nc.Block())

                def blocks(eng, slot):
                    for j in range(2):
                        slot(j, j)
                    with eng.Fori(1, NBLK // 2) as i:
                        for j in range(2):
                            slot(2 * i + j, j)

                @block.gpsimd
                def _(pool):
                    products(2, 0)

                    def slot(k, j):
                        if j == 0:
                            pool.wait_ge(gram_kept, k + 1)
                            need(pool, rp_ready, k // 2)
                            nc.gpsimd.tensor_tensor(gm[0][:], graw[0][:], same[:].unsqueeze(1).to_broadcast([P, 3, CB]),
                                                    ALU.mult).then_inc(masked_ready, 1)
                            pool.wait_ge(gram_kept, k + 2)
                            need(pool, rpb_ready, k // 2 + 1)
                            nc.gpsimd.tensor_tensor(gm[1][:], graw[1][:], same[:].unsqueeze(1).to_broadcast([P, 2, CB]),
                                                    ALU.mult).then_inc(masked_ready, 1)
                            stationary(k + 2, 0)
                            stationary(k + 3, 1)
                        else:
                            products(k + 2, 1)
                            products(k + 3, 0)
                        pool.wait_ge(ra_ready, k + 1)
                        need(pool, ut_ready, k)
                        nc.gpsimd.tensor_tensor(U[:], CF[:, j, 1:1 + C, :], RA[:].unsqueeze(1).to_broadcast([P, C, B]),
                                                ALU.mult).then_inc(u_ready, 1)

                    blocks(pool, slot)

                @block.sync
                def _(sp):
                    for k in range(NBLK - 1):
                        sp.wait_ge(ut_kept, k + 1)
                        sp.wait_ge(far_ready, k // 2 + 1)
                        sp.dma_start(UT[C * k:C * k + C, :, :], uTk[:, k % 2, :]).then_inc(ut_landed[k % 2], 16)
                    for j in range(2):
                        sp.wait_ge(ut_landed[j], 16 * (NBLK // 2 - j))

                @block.tensor
                def _(pe):
                    def broadcast(k, j):
                        pe.wait_ge(prod_ready, k + 1)
                        need(pe, gb_kept, k - 1)
                        nc.tensor.matmul(gbp[j][:], lrs[:], prod[:, j, :], start=True, stop=True).then_inc(gb_ready, 1)

                    def grams(k, j):
                        pe.wait_ge(xblk_ready, k + 1)
                        need(pe, gram_kept, k - 1)
                        nc.tensor.matmul(gp[j][:], xblk[:, j, :], XTt[:, bass.ds(C * k + C, (3 - j) * C), :],
                                         start=True, stop=True).then_inc(gram_ready, 1)

                    broadcast(0, 0)
                    nc.tensor.matmul(rp[:], ident[:], W0X[:, :, 0:2 * C], start=True, stop=True,
                                     skip_group_check=True).then_inc(rpb_ready, 1)

                    def slot(k, j):
                        first_pair = isinstance(k, int)
                        after_a_block = not (first_pair and k == 0)
                        if after_a_block:
                            pe.wait_ge(fin_ready, C * k)
                            nc.tensor.transpose(ctp[:], CF[:, 1 - j, 1:1 + C, :].rearrange("p s b -> p (s b)"),
                                                ident[:]).then_inc(ct_ready, 1)
                            pe.wait_ge(masked_ready, k)
                            pe.wait_ge(ct_kept, k)
                            nc.tensor.matmul(np_[:], cTk[:, 1 - j, :], gm[1 - j][:, 0, :], start=True, stop=True).then_inc(near_ready, 1)
                        if j == 0:
                            grams(k, 0)
                        def transpose_u():
                            pe.wait_ge(u_ready, k)
                            need(pe, ut_kept, k - 1)
                            nc.tensor.transpose(utp[:], U[:].rearrange("p s b -> p (s b)"), ident[:]).then_inc(ut_ready, 1)

                        if j == 0:
                            if after_a_block:
                                transpose_u()
                            grams(k + 1, 1)
                            broadcast(k + 1, 1)
                            broadcast(k + 2, 0)
                            if after_a_block:
                                pe.wait_ge(t0_ready, k)
                                pe.wait_ge(ut_kept, k)
                                nc.tensor.matmul(rp[:, :, C:2 * C], uTk[:, 1, :], gm[1][:, 1, :].rearrange("p (t b) -> p b t", b=B),
                                                 start=False, stop=True, skip_group_check=True).then_inc(rpb_ready, 1)
                            return
                        if first_pair:
                            transpose_u()
                        pe.wait_ge(t0_ready, k)
                        ins = nc.tensor.matmul(rp[:], ident[:], W0X[:, :, bass.ds(C * k + C, 2 * C)], start=True,
                                               stop=False, skip_group_check=True)
                        if not first_pair:
                            for half_ in ut_landed:
                                pe.wait_ge(half_, 8 * (k - 1))
                            for b in range(B):
                                if b == 2:
                                    transpose_u()
                                ins = nc.tensor.matmul(rp[:, b, :], UT[:, b, :], GF[:, b, bass.ds(C * k + C, 2 * C)],
                                                       start=False, stop=False, skip_group_check=True)
                        ins.then_inc(far_ready, 1)
                        pe.wait_ge(ut_kept, k)
                        nc.tensor.matmul(rp[:], uTk[:, 0, :], gm[0][:, 1:3, :].rearrange("p h (t b) -> p b (h t)", b=B),
                                         start=False, stop=True, skip_group_check=True).then_inc(rp_ready, 1)

                    blocks(pe, slot)

                @block.scalar
                def _(act):
                    def keep_gb(k, j):
                        act.wait_ge(gb_ready, k + 1)
                        nc.scalar.copy(GB[:, j, :], gbp[j][:]).then_inc(gb_kept, 1)

                    keep_gb(0, 0)

                    def slot(k, j):
                        first_block = isinstance(k, int) and k == 0
                        if not first_block:
                            act.wait_ge(ct_ready, k)
                            nc.scalar.copy(cTk[:, 1 - j, :], ctp[:]).then_inc(ct_kept, 1)
                        for s in range(C):
                            act.wait_ge(p_ready, C * k + s + 1)
                            nc.scalar.activation(CF[:, j, 1 + s, :], pm[:, s, :], ACT.Sigmoid).then_inc(y_ready, 1)
                            act.wait_ge(y_ready, C * k + s + 1)
                            nc.scalar.copy(YT[:, bass.ds(C * k + s, 1), :], CF[:, j, 1 + s:2 + s, :]).then_inc(yt_ready, 1)
                            if s == 0 and not first_block:
                                act.wait_ge(ut_ready, k)
                                if j == 1:
                                    need(act, ut_landed[0], 8 * (k - 1))
                                nc.scalar.copy(uTk[:, 1 - j, :], utp[:]).then_inc(ut_kept, 1)
                            if j == 0 and s in (1, 2):
                                act.wait_ge(gram_ready, k + s)
                                need(act, masked_ready, k + s - 2)
                                nc.scalar.copy(graw[s - 1][:], gp[s - 1][:]).then_inc(gram_kept, 1)
                            if s == 4:
                                keep_gb(k + 1, 1 - j)

                    blocks(act, slot)

                @block.vector
                def _(dve):
                    def slot(k, j):
                        if isinstance(k, int) and k == 0:
                            nc.vector.tensor_copy(pm[:, 0, :], W0X[:, :, 0]).then_inc(p_ready, 1)
                            nc.vector.tensor_copy(pm[:, 1:C, :], W0X[:, :, 1:C].rearrange("p b t -> p t b")).then_inc(pr_ready, 1)
                        else:
                            dve.wait_ge(fin_ready, C * k)
                            if j == 0:
                                dve.wait_ge(rp_ready, k // 2)
                            else:
                                dve.wait_ge(rpb_ready, (k + 1) // 2)
                            nc.vector.tensor_tensor(t0[:], rp[:, :, C * j:C * j + C].rearrange("p b t -> p t b"),
                                                    CF[:, 1 - j, 0:1, :].to_broadcast([P, C, B]), ALU.mult).then_inc(t0_ready, 1)
                            need(dve, u_ready, k - 1)
                            nc.vector.reciprocal(RA[:], CF[:, 1 - j, 0, :]).then_inc(ra_ready, 1)
                            dve.wait_ge(t0_ready, k)
                            dve.wait_ge(near_ready, k)
                            nc.vector.tensor_tensor(pm[:, 0, :], np_[:, 0, :], t0[:, 0, :], ALU.add).then_inc(p_ready, 1)
                            nc.vector.tensor_tensor(pm[:, 1:C, :], np_[:, 1:C, :], t0[:, 1:C, :], ALU.add).then_inc(pr_ready, 1)
                        dve.wait_ge(gb_kept, k + 1)
                        for s in range(C):
                            n = C - 1 - s
                            dve.wait_ge(y_ready, C * k + s + 1)
                            y = CF[:, j, 1 + s, :]
                            nc.vector.scalar_tensor_tensor(sq[:, s % 2], y, -LR, y, ALU.mult, ALU.mult).then_inc(sq_ready, 1)
                            if n:
                                nc.vector.tensor_tensor(gt[:, s % 2, 0:n], GB[:, j, first[s]:first[s] + B * n].rearrange("p (t b) -> p t b", b=B),
                                                        y.unsqueeze(1).to_broadcast([P, n, B]), ALU.mult).then_inc(gt_ready, 1)
                            dve.wait_ge(sq_ready, C * k + s + 1)
                            decay = lambda to, src, m: nc.vector.scalar_tensor_tensor(
                                to, sq[:, s % 2].unsqueeze(1).to_broadcast([P, m, B]), 1.0, src, ALU.add, ALU.mult)
                            if n:
                                decay(qt[:, s % 2, 0:1], pm[:, s + 1:s + 2, :], 1).then_inc(q_ready, 1)
                            if n > 1:
                                decay(qt[:, s % 2, 1:n], pm[:, s + 2:C, :], n - 1).then_inc(qr_ready, 1)
                            if n:
                                dve.wait_ge(q_ready, (C - 1) * k + s + 1)
                                nc.vector.tensor_tensor(pm[:, s + 1, :], qt[:, s % 2, 0], gt[:, s % 2, 0], ALU.add).then_inc(p_ready, 1)
                            if s:
                                dve.wait_ge(yt_ready, C * k + s)
                                decay(CF[:, j, 0:s + 1, :], CF[:, j, 0:s + 1, :], s + 1).then_inc(fin_ready, 1)
                            else:
                                decay(CF[:, j, 0:1, :], CF[:, 1 - j, 0:1, :], 1).then_inc(fin_ready, 1)
                            if n > 1:
                                dve.wait_ge(qr_ready, (C - 2) * k + s + 1)
                                nc.vector.tensor_tensor(pm[:, s + 2:C, :], qt[:, s % 2, 1:n], gt[:, s % 2, 1:n], ALU.add).then_inc(pr_ready, 1)

                    blocks(dve, slot)
                    dve.wait_ge(fin_ready, C * NBLK)
                    nc.vector.reciprocal(RA[:], CF[:, (NBLK - 1) % 2, 0, :]).then_inc(ra_ready, 1)

        def add_recurrence(YT):
            t_ready, res_ready, st_ready = sem("addrec_t_ready"), sem("addrec_res_ready"), sem("addrec_st_ready")
            with ExitStack() as scope:
                tp = [scope.enter_context(nc.psum_tensor(f"addrec_tp{i}", [P, 4, P], F32)) for i in range(2)]
                block = scope.enter_context(nc.Block())

                @block.tensor
                def _(pe):
                    for q in range(B // 4):
                        need(pe, res_ready, q - 1)
                        for j in range(4):
                            ins = nc.tensor.transpose(tp[q % 2][:, j, :], YT[:, 0:S, 4 * q + j], ident[:])
                        ins.then_inc(t_ready, 1)

                @block.vector
                def _(dve):
                    for q in range(B // 4):
                        dve.wait_ge(t_ready, q + 1)
                        nc.vector.tensor_tensor(RES[:, 4 * q:4 * q + 4, :], tp[q % 2][:], X[:, 4 * q:4 * q + 4, :],
                                                ALU.add).then_inc(res_ready, 1)
                        dve.wait_ge(res_ready, q + 1)
                        for j in range(4):
                            nc.vector.bn_stats(stats[:, 4 * q + j, :], RES[:, 4 * q + j, :]).then_inc(st_ready, 1)

        def narrow_operands(name, WQT, WKT, WVT, keys_from, QT, KT, VA, bias_q=None, bias_k=None, bias_v=None,
                            ones_row=None, maskbias=None):
            s_ = lambda what: sem(f"{name}_{what}")
            ones_ready, q_ready, q_high, q_kept, k_ready, k_high, k_kept, v_ready, v_kept = [s_(w) for w in (
                "ones_ready q_ready q_high q_kept k_ready k_high k_kept v_ready v_kept").split()]
            with ExitStack() as scope:
                def lps(what, shape):
                    return scope.enter_context(nc.psum_tensor(f"{name}_{what}", shape, F32))

                qp = [lps(f"qp{i}", [P, 4, S]) for i in range(2)]
                kp = [lps(f"kp{i}", [P, 4, S]) for i in range(2)]
                vp = [lps(f"vp{i}", [P, 4, D]) for i in range(2)]
                block = scope.enter_context(nc.Block())

                @block.gpsimd
                def _(pool):
                    nc.gpsimd.memset(VA[:, :, :, DH1:DH1 + 1], 1.0).then_inc(ones_ready, 1)
                    if ones_row is not None:
                        nc.gpsimd.memset(ones_row[:], 1.0).then_inc(ones_ready, 1)
                    pool.wait_ge(w1_landed, W1_LANDED)

                @block.tensor
                def _(pe):
                    pe.wait_ge(w1_landed, W1_LANDED)
                    if ones_row is not None:
                        pe.wait_ge(ones_ready, 2)
                    for q in range(B // 4):
                        need(pe, k_kept, q - 1)
                        nc.tensor.matmul(kp[q % 2][:], WKT[:], keys_from[:, 4 * q:4 * q + 4, :], start=True, stop=True).then_inc(k_ready, 1)
                        need(pe, q_kept, q - 1)
                        nc.tensor.matmul(qp[q % 2][:], WQT[:], XT[:, 4 * q:4 * q + 4, :], start=True, stop=True).then_inc(q_ready, 1)
                        need(pe, v_kept, q - 1)
                        for j in range(4):
                            ins = nc.tensor.matmul(vp[q % 2][:, j, :], keys_from[:, 4 * q + j, :], WVT[:],
                                                   start=True, stop=True)
                        ins.then_inc(v_ready, 1)

                @block.scalar
                def _(act):
                    act.wait_ge(w1_landed, W1_LANDED)
                    for q in range(B // 4):
                        four = slice(4 * q, 4 * q + 4)
                        for ready, high, dst, src, bias in ((k_ready, k_high, KT, kp, bias_k), (q_ready, q_high, QT, qp, bias_q)):
                            act.wait_ge(ready, q + 1)
                            nc.scalar.activation(dst[0][:, four, :], src[q % 2][:], ACT.Identity,
                                                 bias=0.0 if bias is None else bias).then_inc(high, 1)
                        if bias_v is None:
                            act.wait_ge(v_ready, q + 1)
                            nc.scalar.copy(VA[:, four, :, 0:DH1], vp[q % 2][:].rearrange("p b (h d) -> p b h d", d=DH1)).then_inc(v_kept, 1)

                @block.vector
                def _(dve):
                    dve.wait_ge(w1_landed, W1_LANDED)
                    if maskbias is not None:
                        for q in range(B // 4):
                            nc.vector.tensor_scalar(maskbias[:, 4 * q:4 * q + 4, :], maskint[:, 4 * q:4 * q + 4, :], 0.0, NEG,
                                                    ALU.is_equal, ALU.mult)
                    for q in range(B // 4):
                        four = slice(4 * q, 4 * q + 4)
                        for high, kept, dst, src, bias in ((k_high, k_kept, KT, kp, bias_k), (q_high, q_kept, QT, qp, bias_q)):
                            dve.wait_ge(high, q + 1)
                            nc.vector.scalar_tensor_tensor(dst[1][:, four, :], src[q % 2][:], 0.0 if bias is None else bias,
                                                           dst[0][:, four, :].bitcast(F32), ALU.add, ALU.subtract).then_inc(kept, 1)
                        if bias_v is not None:
                            dve.wait_ge(v_ready, q + 1)
                            nc.vector.tensor_tensor(VA[:, four, :, 0:DH1], vp[q % 2][:].rearrange("p b (h d) -> p b h d", d=DH1),
                                                    bias_v.rearrange("p (h d) -> p h d", d=DH1).unsqueeze(1).to_broadcast([P, 4, H, DH1]),
                                                    ALU.add).then_inc(v_kept, 1)

        def gated_layer():
            s_ = lambda what: sem(f"gl_{what}")
            (cleared, wc_ready, xc_ready, xc_kept, st_ready, ag_ready, ve_ready, rs_ready, sc_ready, bi_ready,
             xa_ready) = [s_(w) for w in (
                 "cleared wc_ready xc_ready xc_kept st_ready ag_ready ve_ready rs_ready sc_ready bi_ready "
                 "xa_ready").split()]
            with ExitStack() as scope:
                def lsb(what, shape, dt=F32):
                    return scope.enter_context(nc.sbuf_tensor(f"gl_{what}", shape, dt))

                WC = lsb("WC", [P, G2])
                XC = lsb("XC", [G2, B, S])
                XA = lsb("XA", [G2 + 1, B, S])
                bst = lsb("bst", [G2, 4, 6])
                bag = lsb("bag", [G2, 2])
                brs = lsb("brs", [G2, 1])
                bhalf = lsb("bhalf", [G2, 1])
                bsc = lsb("bsc", [G2, 1])
                bms = lsb("bms", [G2, 1])
                bbi = lsb("bbi", [G2, 1])
                ones1 = lsb("ones1", [1, P])
                ms_ready = s_("ms_ready")
                WS = NCH * P // B
                whole_landed, high_ready = s_("whole_landed"), s_("high_ready")
                splits = (lsb("GP", [P, NCH * P]), GPH, GPL), (lsb("UP", [P, NCH * P]), UPH, UPL)

                with ExitStack() as inner:
                    xcp = [inner.enter_context(nc.psum_tensor(f"gl_xcp{i}", [G2, 4, S], F32)) for i in range(4)]
                    block = inner.enter_context(nc.Block())

                    @block.sync
                    def _(sp):
                        for (whole, _, _), name in zip(splits, ("gpT", "upT")):
                            sp.dma_start(whole[:], a[name]).then_inc(whole_landed, 16)

                    @block.gpsimd
                    def _(pool):
                        nc.gpsimd.memset(bhalf[:], -0.5).then_inc(cleared, 1)
                        pool.wait_ge(gl_landed, GL_LANDED)
                        for v in range(2):
                            nc.gpsimd.tensor_scalar(WC[:, G * v:G * v + G], groups[:], convw[:, v:v + 1], None,
                                                    ALU.mult).then_inc(wc_ready, 1)
                        pool.wait_ge(ve_ready, 1)
                        pool.wait_ge(cleared, 1)
                        nc.gpsimd.tensor_tensor(brs[:], brs[:], bhalf[:], ALU.pow).then_inc(rs_ready, 1)

                    @block.tensor
                    def _(pe):
                        pe.wait_ge(wc_ready, 2)
                        for q in range(4):
                            nc.tensor.matmul(xcp[q][:], WC[:], XT[:, 4 * q:4 * q + 4, :], start=True, stop=True).then_inc(xc_ready, 1)

                    @block.scalar
                    def _(act):
                        act.wait_ge(gl_landed, GL_LANDED)
                        for q in range(4):
                            act.wait_ge(xc_ready, q + 1)
                            nc.scalar.activation(XC[:, 4 * q:4 * q + 4, :], xcp[q][:], ACT.Identity, bias=chan[:, 0:1]).then_inc(xc_kept, 1)
                        act.wait_ge(bi_ready, 1)
                        for q in range(4):
                            nc.scalar.activation(XA[0:G2, 4 * q:4 * q + 4, :], XC[:, 4 * q:4 * q + 4, :], ACT.Gelu,
                                                 bias=bbi[:], scale=bsc[:]).then_inc(xa_ready, 1)

                    @block.vector
                    def _(dve):
                        nc.vector.memset(XA[G2:G2 + 1], 1.0)
                        nc.vector.memset(ones1[:], 1.0)
                        for q in range(4):
                            dve.wait_ge(xc_kept, q + 1)
                            nc.vector.bn_stats(bst[:, q, :], XC[:, 4 * q:4 * q + 4, :].rearrange("p b s -> p (b s)")).then_inc(st_ready, 1)
                        dve.wait_ge(st_ready, 4)
                        nc.vector.bn_aggr(bag[:], bst[:].rearrange("p q s -> p (q s)")).then_inc(ag_ready, 1)
                        dve.wait_ge(ag_ready, 1)
                        nc.vector.tensor_scalar(brs[:], bag[:, 1:2], EPS, None, ALU.add).then_inc(ve_ready, 1)
                        dve.wait_ge(rs_ready, 1)
                        nc.vector.tensor_tensor(bsc[:], brs[:], chan[:, 1:2], ALU.mult).then_inc(sc_ready, 1)
                        dve.wait_ge(sc_ready, 1)
                        nc.vector.tensor_tensor(bms[:], bag[:, 0:1], bsc[:], ALU.mult).then_inc(ms_ready, 1)
                        dve.wait_ge(ms_ready, 1)
                        nc.vector.tensor_tensor(bbi[:], chan[:, 2:3], bms[:], ALU.subtract).then_inc(bi_ready, 1)

                (xs_ready, as_ready, lg_ready, mx_ready, e_ready, m_ready, w_ready, sel_ready, rs2_ready, nr_ready,
                 xg_ready, xt_ready, xt_kept, y_ready, full_ready, t1_ready, t2_ready, res_ready, bs_ready) = [s_(w) for w in (
                     "xs_ready as_ready lg_ready mx_ready e_ready m_ready w_ready sel_ready rs2_ready nr_ready "
                     "xg_ready xt_ready xt_kept y_ready full_ready t1_ready t2_ready res_ready bs_ready").split()]
                xs = lsb("xs", [P, 2, S])
                xas = lsb("xas", [G2 + 1, 2, S])
                nmx = lsb("nmx", [P, 2, 2])
                ex = lsb("ex", [P, 2, 2, D])
                ssum = lsb("ssum", [P, 2, 2])
                m8 = lsb("m8", [P, 2, 8])
                wk = lsb("wk", [P, 2, D])
                sel = lsb("sel", [P, 2, 2, D])
                rs2 = lsb("rs2", [P, 2, 2])
                nrs = lsb("nrs", [P, 2, 2])
                xg = lsb("xg", [P, 2, D])
                xgt = lsb("xgt", [P, 2, S])
                t1 = lsb("t1", [P, 2, D])
                t2 = lsb("t2", [P, 2, D])
                lgp = [scope.enter_context(nc.psum_tensor(f"gl_lgp{i}", [P, 2, D], F32)) for i in range(2)]
                fup = [scope.enter_context(nc.psum_tensor(f"gl_fup{i}", [P, D], F32)) for i in range(2)]
                xtp = scope.enter_context(nc.psum_tensor("gl_xtp", [P, S], F32))
                y2p = scope.enter_context(nc.psum_tensor("gl_y2p", [P, D], F32))
                block = scope.enter_context(nc.Block())
                ROUNDS = TOPK // 8

                def run(eng, slot):
                    for b in range(4):
                        slot(b, b % 2, lambda lag: b >= lag)
                    with eng.Fori(2, B // 2) as i:
                        for r in range(2):
                            slot(2 * i + r, r, lambda lag: True)
                    slot(B, 0, lambda lag: lag > 0)
                    slot(B + 1, 1, lambda lag: lag > 1)

                @block.gpsimd
                def _(pool):
                    def slot(b, r, live):
                        if live(0):
                            need(pool, lg_ready, b - 1)
                            nc.gpsimd.tensor_copy(xas[:, r, :], XA[:, b, :]).then_inc(as_ready, 1)
                            need(pool, full_ready, b - 1)
                            nc.gpsimd.tensor_copy(xs[:, r, :], XT[:, b, :]).then_inc(xs_ready, 1)
                        if live(1):
                            pool.wait_ge(high_ready, b)
                            cols = bass.ds(WS * (b - 1), WS)
                            for whole, high, low in splits:
                                nc.gpsimd.tensor_tensor(low[:, cols], whole[:, cols], high[:, cols].bitcast(F32), ALU.subtract)
                    pool.wait_ge(whole_landed, 32)
                    run(pool, slot)

                @block.tensor
                def _(pe):
                    def slot(b, r, live):
                        if live(0):
                            pe.wait_ge(as_ready, b + 1)
                            need(pe, e_ready, 2 * b - 2)
                            nc.tensor.matmul(lgp[r][:], xas[:, r, :], LW[:], start=True, stop=True).then_inc(lg_ready, 1)
                            pe.wait_ge(xs_ready, b + 1)
                            need(pe, t1_ready, b - 1)
                            nc.tensor.matmul(fup[r][:], xs[:, r, :], ffw[:], start=True, stop=True).then_inc(full_ready, 1)
                        if live(2):
                            n = b - 2
                            pe.wait_ge(xg_ready, n + 1)
                            need(pe, xt_kept, n)
                            nc.tensor.transpose(xtp[:], xg[:, r, :], ident[:]).then_inc(xt_ready, 1)
                            pe.wait_ge(xt_kept, n + 1)
                            need(pe, res_ready, n)
                            nc.tensor.matmul(y2p[:], xgt[:, r, :], ffw[:], start=True, stop=False)
                            nc.tensor.matmul(y2p[:], ones1[:], ffb[:], start=False, stop=True).then_inc(y_ready, 1)
                    run(pe, slot)

                @block.scalar
                def _(act):
                    def slot(b, r, live):
                        if live(0):
                            act.wait_ge(mx_ready, b + 1)
                            need(act, xg_ready, b - 1)
                            need(act, t1_ready, b - 1)
                            for v in range(2):
                                nc.scalar.activation(ex[:, r, v, :], lgp[r][:, v, :], ACT.Exp, bias=nmx[:, r, v:v + 1],
                                                     accum_out=ssum[:, r, v:v + 1]).then_inc(e_ready, 1)
                            cols = bass.ds(WS * b, WS)
                            for whole, high, _ in splits:
                                ins = nc.scalar.copy(high[:, cols], whole[:, cols])
                            ins.then_inc(high_ready, 1)
                        if live(2):
                            n = b - 2
                            act.wait_ge(xt_ready, n + 1)
                            need(act, y_ready, n - 1)
                            nc.scalar.copy(xgt[:, r, :], xtp[:]).then_inc(xt_kept, 1)
                    act.wait_ge(whole_landed, 32)
                    run(act, slot)

                @block.vector
                def _(dve):
                    def slot(b, r, live):
                        if live(0):
                            dve.wait_ge(lg_ready, b + 1)
                            need(dve, e_ready, 2 * b - 2)
                            nc.vector.tensor_reduce(nmx[:, r, :], lgp[r][:], AX.X, ALU.max, negate=True).then_inc(mx_ready, 1)
                        n, p = b - 1, 1 - r
                        if live(1):
                            dve.wait_ge(e_ready, 2 * n + 2)
                            nc.vector.reciprocal(rs2[:, p, :], ssum[:, p, :]).then_inc(rs2_ready, 1)
                            dve.sem_clear(m_ready)
                            dve.sem_clear(w_ready)
                            for z in range(ROUNDS):
                                for v in range(2):
                                    w = ex[:, p, v, :] if z == 0 else wk[:, v, :]
                                    if z:
                                        dve.wait_ge(w_ready, 2 * (z - 1) + v + 1)
                                    nc.vector.max(m8[:, v, :], w).then_inc(m_ready, 1)
                                for v in range(2):
                                    w = ex[:, p, v, :] if z == 0 else wk[:, v, :]
                                    dve.wait_ge(m_ready, 2 * z + v + 1)
                                    nc.vector.match_replace(wk[:, v, :], m8[:, v, :], w, -1.0).then_inc(w_ready, 1)
                            dve.wait_ge(rs2_ready, n + 1)
                            nc.vector.tensor_scalar(nrs[:, p, :], rs2[:, p, :], -1.0, None, ALU.mult).then_inc(nr_ready, 1)
                            for v in (1, 0):
                                dve.wait_ge(w_ready, 2 * ROUNDS)
                                nc.vector.scalar_tensor_tensor(sel[:, p, v, :], wk[:, v, :], 0.0, ex[:, p, v, :],
                                                               ALU.max, ALU.subtract).then_inc(sel_ready, 1)
                        if live(2):
                            dve.wait_ge(y_ready, b - 1)
                            dve.wait_ge(t2_ready, b - 1)
                            nc.vector.tensor_tensor(RES[:, b - 2, :], y2p[:], t2[:, r, :], ALU.add).then_inc(res_ready, 1)
                        if live(1):
                            dve.wait_ge(nr_ready, n + 1)
                            dve.wait_ge(sel_ready, 2 * n + 2)
                            need(dve, xt_ready, n - 1)
                            nc.vector.scalar_tensor_tensor(xg[:, p, :], sel[:, p, 1, :], nrs[:, p, 1:2], X[:, n, :],
                                                           ALU.mult, ALU.mult).then_inc(xg_ready, 1)
                            dve.wait_ge(full_ready, n + 1)
                            nc.vector.scalar_tensor_tensor(t1[:, p, :], sel[:, p, 0, :], nrs[:, p, 0:1], fup[p][:],
                                                           ALU.mult, ALU.mult).then_inc(t1_ready, 1)
                        if live(2):
                            dve.wait_ge(res_ready, b - 1)
                            nc.vector.bn_stats(stats[:, b - 2, :], RES[:, b - 2, :]).then_inc(bs_ready, 1)
                        if live(1):
                            dve.wait_ge(t1_ready, n + 1)
                            nc.vector.tensor_tensor(t2[:, p, :], t1[:, p, :], X[:, n, :], ALU.add).then_inc(t2_ready, 1)
                    run(dve, slot)

        def moe_sems(names):
            return [sem(f"moe_{w}") for w in names.split()]

        def route(glp, XTH, XTL, combT16):
            (mx_ready, d_ready, e_ready, sum_ready, rc_ready, sc_ready, v8_ready, i8_ready, if_ready, den_ready,
             rden_ready, wt_ready, eq_ready, pr_ready, comb_ready, ct_ready, ct_kept, cst_ready, part_ready,
             xth_ready) = moe_sems(
                "mx_ready d_ready e_ready sum_ready rc_ready sc_ready v8_ready i8_ready if_ready den_ready "
                "rden_ready wt_ready eq_ready pr_ready comb_ready ct_ready ct_kept cst_ready part_ready xth_ready")
            with ExitStack() as inner:
                def isb(what, shape, dt=F32):
                    return inner.enter_context(nc.sbuf_tensor(f"moe_{what}", shape, dt))

                mx = isb("mx", [P, B])
                df = isb("df", [P, B, E])
                ee = isb("ee", [P, B, E])
                su = isb("su", [P, B])
                rc = isb("rc", [P, B])
                score = isb("score", [P, B, E])
                v8 = isb("v8", [P, B, 8])
                i8 = isb("i8", [P, B, 8], U32)
                i8f = isb("i8f", [P, B, 8])
                den = isb("den", [P, B])
                rden = isb("rden", [P, B])
                wt = isb("wt", [P, B, 2])
                eq = isb("eq", [P, 2, B, E])
                pr = isb("pr", [P, 2, B, E])
                comb = isb("comb", [P, B, E])
                lg = isb("lg", [P, B, E])
                rest = isb("rest", [P, B, E])
                parts = isb("parts", [P, B, 3, 32], BF16)
                ctp = [inner.enter_context(nc.psum_tensor(f"moe_ctp{i}", [3 * 32, 4, S], BF16)) for i in range(4)]
                block = inner.enter_context(nc.Block())

                @block.gpsimd
                def _(pool):
                    nc.gpsimd.memset(parts[:], 0.0).then_inc(cst_ready, 1)
                    pool.wait_ge(xth_ready, 1)
                    nc.gpsimd.tensor_tensor(XTL[:], XT[:], XTH[:].bitcast(F32), ALU.subtract)

                @block.tensor
                def _(pe):
                    pe.wait_ge(comb_ready, 1)
                    for q in range(4):
                        for j in range(4):
                            ins = nc.tensor.transpose(ctp[q][:, j, :], parts[:, 4 * q + j].rearrange("p z e -> p (z e)"), ident16[:])
                        ins.then_inc(ct_ready, 1)

                @block.scalar
                def _(act):
                    nc.scalar.copy(XTH[:], XT[:]).then_inc(xth_ready, 1)
                    act.wait_ge(d_ready, 1)
                    nc.scalar.activation(ee[:], df[:], ACT.Exp).then_inc(e_ready, 1)
                    for q in range(4):
                        act.wait_ge(ct_ready, q + 1)
                        nc.scalar.copy(combT16[:, 4 * q:4 * q + 4, :], ctp[q][:]).then_inc(ct_kept, 1)

                @block.vector
                def _(dve):
                    bc = lambda ap: ap.unsqueeze(2).to_broadcast([P, B, E])
                    dve.wait_ge(moe_landed, MOE_LANDED)
                    nc.vector.tensor_tensor(lg[:], glp[:], gbias[:].unsqueeze(1).to_broadcast([P, B, E]),
                                            ALU.add).then_inc(mx_ready, 1)
                    dve.wait_ge(mx_ready, 1)
                    nc.vector.tensor_reduce(mx[:], lg[:], AX.X, ALU.max).then_inc(mx_ready, 1)
                    dve.wait_ge(mx_ready, 2)
                    nc.vector.tensor_tensor(df[:], lg[:], bc(mx[:]), ALU.subtract).then_inc(d_ready, 1)
                    dve.wait_ge(e_ready, 1)
                    nc.vector.tensor_reduce(su[:], ee[:], AX.X, ALU.add).then_inc(sum_ready, 1)
                    dve.wait_ge(sum_ready, 1)
                    nc.vector.reciprocal(rc[:], su[:]).then_inc(rc_ready, 1)
                    dve.wait_ge(rc_ready, 1)
                    nc.vector.tensor_tensor(score[:], ee[:], bc(rc[:]), ALU.mult).then_inc(sc_ready, 1)
                    dve.wait_ge(sc_ready, 1)
                    for b in range(B):
                        nc.vector.max(v8[:, b, :], score[:, b, :]).then_inc(v8_ready, 1)
                    for b in range(B):
                        dve.wait_ge(v8_ready, b + 1)
                        nc.vector.max_index(i8[:, b, :], v8[:, b, :], score[:, b, :]).then_inc(i8_ready, 1)
                    dve.wait_ge(i8_ready, B)
                    nc.vector.tensor_copy(i8f[:], i8[:]).then_inc(if_ready, 1)
                    nc.vector.tensor_tensor(den[:], v8[:, :, 0], v8[:, :, 1], ALU.add).then_inc(den_ready, 1)
                    dve.wait_ge(den_ready, 1)
                    nc.vector.tensor_scalar(den[:], den[:], 1e-20, None, ALU.add).then_inc(den_ready, 1)
                    dve.wait_ge(den_ready, 2)
                    nc.vector.reciprocal(rden[:], den[:]).then_inc(rden_ready, 1)
                    dve.wait_ge(rden_ready, 1)
                    nc.vector.tensor_tensor(wt[:], v8[:, :, 0:2], rden[:].unsqueeze(2).to_broadcast([P, B, 2]),
                                            ALU.mult).then_inc(wt_ready, 1)
                    dve.wait_ge(if_ready, 1)
                    for z in range(2):
                        nc.vector.tensor_tensor(eq[:, z], number[:].unsqueeze(1).to_broadcast([P, B, E]), bc(i8f[:, :, z]),
                                                ALU.is_equal).then_inc(eq_ready, 1)
                    dve.wait_ge(wt_ready, 1)
                    for z in range(2):
                        dve.wait_ge(eq_ready, z + 1)
                        nc.vector.tensor_tensor(pr[:, z], eq[:, z], bc(wt[:, :, z]), ALU.mult).then_inc(pr_ready, 1)
                    dve.wait_ge(pr_ready, 2)
                    nc.vector.tensor_tensor(comb[:], pr[:, 0], pr[:, 1], ALU.add).then_inc(part_ready, 1)
                    dve.wait_ge(cst_ready, 1)
                    for z in range(3):
                        src = comb if z == 0 else rest
                        dve.wait_ge(part_ready, 2 * z + 1)
                        ins = nc.vector.tensor_copy(parts[:, :, z, 0:E], src[:])
                        ins.then_inc(part_ready if z < 2 else comb_ready, 1)
                        if z < 2:
                            dve.wait_ge(part_ready, 2 * z + 2)
                            nc.vector.tensor_tensor(rest[:], src[:], parts[:, :, z, 0:E], ALU.subtract).then_inc(part_ready, 1)

        def experts(XTH, XTL, combT16):
            with ExitStack() as scope:
                s_ = lambda what: sem(f"moe_{what}")

                def lsb(what, shape, dt=F32):
                    return scope.enter_context(nc.sbuf_tensor(f"moe_{what}", shape, dt))

                (g_ready, u_ready, g_kept, h_ready, silu_ready, plane_ready, h_kept, dn_ready, sum2_ready, st_ready) = [
                    s_(w) for w in "g_ready u_ready g_kept h_ready silu_ready plane_ready h_kept dn_ready sum2_ready st_ready".split()]
                gs = lsb("gs", [P, 2, 4, S])
                h0 = lsb("h0", [P, 2, 4, S])
                h1 = lsb("h1", [P, 2, 4, S])
                hs = lsb("hs", [P, 2, 4, S])
                gp = [scope.enter_context(nc.psum_tensor(f"moe_gp{i}", [P, 4, S], F32)) for i in range(2)]
                up = [scope.enter_context(nc.psum_tensor(f"moe_up{i}", [P, 4, S], F32)) for i in range(2)]
                plane = [scope.enter_context(nc.psum_tensor(f"moe_plane{i}", [P, 4, S], F32)) for i in range(PB)]
                dn = scope.enter_context(nc.psum_tensor("moe_dn", [P, 4, D], F32))
                last_unit = [max(c for c in range(NCH) if PLANE[c] == n) for n in range(NP)]
                one = lsb("one", [P, 1])
                one_ready, ones_ready = s_("one_ready"), s_("ones_ready")
                block = scope.enter_context(nc.Block())

                def run(eng, slot):
                    for j in range(NCH):
                        slot(0, j, lambda lag: j >= lag)
                    with eng.Fori(1, B // 4) as q:
                        for j in range(NCH):
                            slot(q, j, lambda lag: True)
                    for j in range(2):
                        slot(B // 4, j, lambda lag: j < lag)

                @block.gpsimd
                def _(pool):
                    nc.gpsimd.memset(one[:], 1.0).then_inc(one_ready, 1)
                    ones = one[REAL:P].unsqueeze(2).to_broadcast([P - REAL, 4, S])

                    def slot(q, j, live):
                        if j == NCH - 1 and live(0):
                            pool.wait_ge(h_kept, NCH * q + j - 1)
                            nc.gpsimd.tensor_tensor(h1[REAL:P, j % 2], ones, ones, ALU.mult).then_inc(ones_ready, 1)
                    pool.wait_ge(one_ready, 1)
                    run(pool, slot)

                @block.tensor
                def _(pe):
                    def slot(q, j, live):
                        k = NCH * q + j
                        if live(0):
                            need(pe, g_kept, k - 1)
                            x = XTH[:, bass.ds(4 * q, 4), :], XTL[:, bass.ds(4 * q, 4), :]
                            cols = slice(P * j, P * j + P)
                            products3(gp[j % 2][:], (GPH[:, cols], GPL[:, cols]), x).then_inc(g_ready, 1)
                            need(pe, h_ready, k - 1)
                            products3(up[j % 2][:], (UPH[:, cols], UPL[:, cols]), x).then_inc(u_ready, 1)
                        if live(2):
                            c = (j - 2) % NCH
                            pe.wait_ge(h_kept, k - 1)
                            if c == 0:
                                need(pe, sum2_ready, q)
                            for t in range(4):
                                ins = nc.tensor.matmul(dn[:, t, :], hs[:, j % 2, t, :], DWT[:, c, :],
                                                       start=(c == 0 and t == 0), stop=(c == NCH - 1),
                                                       skip_group_check=True)
                            ins.then_inc(dn_ready, 1)
                        if live(0):
                            n = PLANE[j]
                            if j == 0 or PLANE[j - 1] != n:
                                need(pe, h_kept, NCH * (q if n >= PB else q - 1) + last_unit[(n - PB) % NP] + 1)
                                nc.tensor.matmul(plane[n % PB][:], owner[:, n, :], combT16[:, bass.ds(4 * q, 4), :],
                                                 start=True, stop=True).then_inc(plane_ready, 1)
                    run(pe, slot)

                @block.scalar
                def _(act):
                    def slot(q, j, live):
                        k = NCH * q + j
                        if live(0):
                            act.wait_ge(g_ready, k + 1)
                            need(act, h_ready, k - 1)
                            nc.scalar.activation(gs[:, j % 2], gp[j % 2][:], ACT.Identity, bias=gb[:, j:j + 1]).then_inc(g_kept, 1)
                        if live(1):
                            act.wait_ge(h_ready, k)
                            need(act, h_kept, k - 2)
                            m = REAL if j == 0 else P
                            nc.scalar.activation(h1[0:m, (j - 1) % 2], h0[0:m, (j - 1) % 2], ACT.Silu).then_inc(silu_ready, 1)
                    run(act, slot)

                @block.vector
                def _(dve):
                    def slot(q, j, live):
                        k = NCH * q + j
                        if live(0):
                            dve.wait_ge(u_ready, k + 1)
                            dve.wait_ge(g_kept, k + 1)
                            need(dve, silu_ready, k - 1)
                            nc.vector.scalar_tensor_tensor(h0[:, j % 2], up[j % 2][:], ub[:, j:j + 1], gs[:, j % 2],
                                                           ALU.add, ALU.mult).then_inc(h_ready, 1)
                        if live(1):
                            c = (j - 1) % NCH
                            n = PLANE[c]
                            dve.wait_ge(silu_ready, k)
                            if j == 0:
                                dve.wait_ge(ones_ready, q)
                            dve.wait_ge(plane_ready, NP * (q if j else q - 1) + n + 1)
                            need(dve, dn_ready, k - 2)
                            nc.vector.tensor_tensor(hs[:, (j - 1) % 2], h1[:, (j - 1) % 2], plane[n % PB][:],
                                                    ALU.mult).then_inc(h_kept, 1)
                        if live(2) and j == 1:
                            done = bass.ds(4 * q - 4, 4)
                            dve.wait_ge(dn_ready, NCH * q)
                            nc.vector.tensor_tensor(RES[:, done, :], dn[:], X[:, done, :], ALU.add).then_inc(sum2_ready, 1)
                            dve.wait_ge(sum2_ready, q)
                            for t in range(4):
                                b = 4 * q - 4 + t
                                nc.vector.bn_stats(stats[:, b, :], RES[:, b, :]).then_inc(st_ready, 1)
                    run(dve, slot)

        with ExitStack() as l0:
            def lsb(name, shape, dt=F32):
                return l0.enter_context(nc.sbuf_tensor(name, shape, dt))

            ZM = lsb("ZM", [P, H, D])
            WQ0 = lsb("WQ0", [DH0, H, D])
            WK0 = lsb("WK0", [DH0, H, D])
            WVT0 = lsb("WVT0", [P, H * DH0])
            WO0 = lsb("WO0", [P, H * DH0 // P, D])
            causal = lsb("causal", [P, S], BF16)
            zm_ready, zms_ready = sem("zm_ready"), sem("zms_ready")
            with ExitStack() as scope:
                zmp = [scope.enter_context(nc.psum_tensor(f"zmp{i}", [P, 4, D], F32)) for i in range(4)]
                block = scope.enter_context(nc.Block())

                @block.sync
                def _(sp):
                    sp.dma_start(WQ0[:], a["wq0"]).then_inc(loaded, 16)
                    sp.dma_start(WK0[:], a["wk0"]).then_inc(loaded, 16)
                    sp.dma_start(XT[:], a["xT"]).then_inc(loaded, 16)
                    sp.dma_start(X[:], a["x"].rearrange("b t c -> t b c")).then_inc(loaded, 16)
                    sp.wait_ge(loaded, 16 * 10)
                    for dst, name in gl_loads:
                        sp.dma_start(dst[:], a[name]).then_inc(gl_landed, 16)
                    sp.wait_ge(lw_cleared, 1)
                    for dst, name in gl_parts:
                        sp.dma_start(dst, a[name]).then_inc(gl_landed, 16)
                    for dst, name in w1_loads:
                        sp.dma_start(dst[:], a[name]).then_inc(w1_landed, 16)
                    for dst, name in moe_loads:
                        sp.dma_start(dst[:], a[name]).then_inc(moe_landed, 16)

                @block.gpsimd
                def _(pool):
                    nc.gpsimd.memset(LW[:], 0.0).then_inc(lw_cleared, 1)
                    nc.gpsimd.memset(half[:], -0.5)

                @block.scalar
                def _(act):
                    act.dma_start(WVT0[:], a["wvT0"]).then_inc(loaded, 16)
                    act.dma_start(WO0[:], a["wo0"]).then_inc(loaded, 16)
                    act.dma_start(ident[:], a["ident"]).then_inc(loaded, 16)
                    act.dma_start(ident16[:], a["ident16"]).then_inc(loaded, 16)
                    act.dma_start(causal[:], a["causal"]).then_inc(loaded, 16)
                    act.dma_start(CTXT[:], a["ctxT"]).then_inc(loaded, 16)
                    for q in range(4):
                        act.wait_ge(zm_ready, q + 1)
                        nc.scalar.mul(ZM[:, 4 * q:4 * q + 4, :], zmp[q][:], float(DH0) ** -0.5).then_inc(zms_ready, 1)

                @block.tensor
                def _(pe):
                    pe.wait_ge(loaded, 16 * 10)
                    for q in range(4):
                        for j in range(4):
                            h = 4 * q + j
                            ins = nc.tensor.matmul(zmp[q][:, j, :], WK0[:, h, :], WQ0[:, h, :], start=True, stop=True)
                        ins.then_inc(zm_ready, 1)

            attention("a0", True, causal, WO0, ZM=ZM, WVT=WVT0)
        with ExitStack() as l0:
            XTt = l0.enter_context(nc.sbuf_tensor("XTt", [P, S + 3 * C, B], F32))
            YT = l0.enter_context(nc.sbuf_tensor("YT", [P, S, B], F32))
            layernorm("ln0", also_time_major=XTt[:, 0:S, :])
            recurrence(XTt, YT)
            add_recurrence(YT)
        layernorm("ln1")
        part_ends()

        GPH, GPL = sb("GPH", [P, NCH * P], FR), sb("GPL", [P, NCH * P], FR)
        UPH, UPL = sb("UPH", [P, NCH * P], FR), sb("UPL", [P, NCH * P], FR)
        gated_layer()
        layernorm("ln2")
        part_ends()

        with ExitStack() as l1:
            def lsb(name, shape, dt=F32):
                return l1.enter_context(nc.sbuf_tensor(name, shape, dt))

            ones1 = lsb("ones1", [1, P])
            maskbias = lsb("maskbias", [P, B, S], BF16)
            QT = lsb("QTH", [P, B, S], FR), lsb("QTL", [P, B, S], FR)
            KT = lsb("KTH", [P, B, S], FR), lsb("KTL", [P, B, S], FR)
            VA = lsb("VA", [P, B, H, DH1 + 1])
            w = lambda n: W1[:, n, :]
            narrow_operands("n1", w(0), w(1), w(2), XT, QT, KT, VA)
            attention("a1", False, window, W1[:, 3:4, :], QT=QT, KT=KT, VA=VA, jmask=jmask, umask=umask)
            layernorm("ln3")
            part_ends()
            narrow_operands("n2", w(4), w(5), w(6), CTXT, QT, KT, VA, bias_q=colb[:, 0:1], bias_k=colb[:, 1:2],
                            bias_v=bv[:], ones_row=ones1, maskbias=maskbias)
            attention("a2", False, None, W1[:, 7:8, :], QT=QT, KT=KT, VA=VA, jmask=jmask, umask=umask, maskbias=maskbias,
                      bo_row=bo, ones_row=ones1)
        with ExitStack() as scope:
            glp = scope.enter_context(nc.psum_tensor("moe_glp", [P, B, E], F32))

            def gate(q):
                if q == 0:
                    nc.tensor.wait_ge(moe_landed, MOE_LANDED)
                for b in range(4 * q, 4 * q + 4):
                    nc.tensor.matmul(glp[:, b, :], XT[:, b, :], gwT[:], start=True, stop=True)

            layernorm("ln4", on_xt=gate)
            part_ends()
            XTH, XTL = sb("XTH", [P, B, S], FR), sb("XTL", [P, B, S], FR)
            combT16 = sb("combT16", [3 * 32, B, S], BF16)
            route(glp, XTH, XTL, combT16)
        experts(XTH, XTL, combT16)
        layernorm("ln5", out_to=out)


def host_layout(inputs):
    n = {k: np.asarray(v) for k, v in inputs.items()}
    c = np.ascontiguousarray
    r = np.arange
    t, s = r(S)[:, None], r(S)[None, :]
    g = {
        "x": c(n["x"]),
        "xT": c(n["x"].transpose(2, 0, 1)),
        "ctxT": c(n["ctx_1024"].transpose(2, 0, 1)),
        "wq0": c(n["L0_attn_w_q"].transpose(1, 0, 2)),
        "wk0": c(n["L0_attn_w_k"].transpose(1, 0, 2)),
        "wvT0": c(n["L0_attn_w_v"].reshape(H * DH0, D).T),
        "wo0": c(n["L0_attn_w_o"].reshape(H * DH0 // P, P, D).transpose(1, 0, 2)),
        "ident": np.eye(P, dtype=np.float32),
        "ident16": np.eye(P, dtype=np.float32).astype(mybir.dt.np(BF16)),
        "causal": np.where(s > t, NEG, 0.0).astype(mybir.dt.np(BF16)),
    }
    sb_ = r(C * B)
    g["same"] = np.where(sb_[:, None] % B == sb_[None, :] % B, np.float32(LR), np.float32(0))
    so, si = "L0_ffn_so_", "L0_ffn_si_"
    g["convw"] = c(np.stack([n[so + "conv_w"].reshape(D), n[si + "conv_w"].reshape(D)], 1))
    g["groups"] = (r(D)[:, None] // 4 == r(G)[None, :]).astype(np.float32)
    g["chan"] = c(np.stack([np.concatenate([n[v + w] for v in (so, si)]) for w in ("conv_b", "gamma", "beta")], 1))
    g["ffw"], g["ffb"] = c(n["L0_ffn_weight"]), c(n["L0_ffn_bias"][None])
    g["lwo"], g["lwi"] = c(n[so + "lin_w"].T), c(n[si + "lin_w"].T)
    g["lbo"], g["lbi"] = c(n[so + "lin_b"][None]), c(n[si + "lin_b"][None])
    g["w1"] = c(np.stack([n["L1_attn_W" + w].T for w in "qkvo"] + [n["L1_xattn_W" + w].T for w in "qkvo"], 1))
    g["window"] = np.where((s > t) | (s < t - 16), NEG, 0.0).astype(mybir.dt.np(BF16))
    g["jmask"] = (r(P)[:, None] % 32 // DH1 == r(HU)[None, :]).astype(np.float32)
    g["umask"] = (r(P)[:, None] // 32 == r(NU)[None, :]).astype(np.float32)
    g["colb"] = c(np.stack([n["L1_xattn_bq"], n["L1_xattn_bk"]], 1))
    g["bo"] = c(n["L1_xattn_bo"][None])
    g["bv"] = np.tile(n["L1_xattn_bv"][None], (P, 1))
    g["mask"] = c(n["mask_Bx1xSxS2_if1"][:, 0].transpose(1, 0, 2))
    g["gwT"], g["gbias"] = c(n["L1_ffn_gate_w"].T), np.tile(n["L1_ffn_gate_b"][None], (P, 1))
    g["number"] = np.tile(r(E).astype(np.float32)[None], (P, 1))
    rows = lambda w: c(np.pad(w, [(0, NCH * P - HID)] + [(0, 0)] * (w.ndim - 1)).reshape((NCH, P) + w.shape[1:]).swapaxes(0, 1))
    cols = lambda w: c(np.pad(w.reshape(HID, D), ((0, NCH * P - HID), (0, 0))).T)
    g["gpT"], g["upT"] = cols(n["L1_ffn_gp_w"]), cols(n["L1_ffn_up_w"])
    down = np.pad(n["L1_ffn_down_w"].transpose(0, 2, 1).reshape(HID, D), ((0, NCH * P - HID), (0, 0)))
    down[HID:HID + E] = n["L1_ffn_down_b"]
    g["dwT"] = c(down.reshape(NCH, P, D).swapaxes(0, 1))
    g["gpb"], g["upb"] = rows(n["L1_ffn_gp_b"].reshape(HID)), rows(n["L1_ffn_up_b"].reshape(HID))
    chunk = np.array([OWNERS.index(o) for o in PLANES])
    expert = (P * chunk[:, None] + r(P)[None, :]) // F
    bias_row = P * chunk[:, None] + r(P)[None, :] - HID
    expert = np.where(bias_row >= 0, np.where(bias_row < E, bias_row, -1), expert)
    g["owner"] = (r(96)[:, None, None] % 32 == expert[None]).astype(mybir.dt.np(BF16))
    return g


def kernel(**inputs):
    import concourse.bacc as bacc
    from concourse.bass_utils import run_bass_kernel_spmd

    nc = bacc.Bacc("TRN2", target_bir_lowering=False, num_devices=1)
    arrays = {f"in_{name}": v for name, v in host_layout(inputs).items()}
    aps = {name[3:]: nc.dram_tensor(name, v.shape, mybir.dt.from_np(v.dtype), kind="ExternalInput").ap()
           for name, v in arrays.items()}
    out = nc.dram_tensor("out", (B, S, D), F32, kind="ExternalOutput").ap()
    decoder_program(nc, aps, out)
    return run_bass_kernel_spmd(nc, [arrays], core_ids=[0]).results[0]["out"]
```

```python
from contextlib import ExitStack

import numpy as np

import concourse.bass as bass
from concourse import mybir

F32 = mybir.dt.float32
BF16 = mybir.dt.bfloat16
FR = mybir.dt.float32r
I32 = mybir.dt.int32
U32 = mybir.dt.uint32
ALU = mybir.AluOpType
ACT = mybir.ActivationFunctionType
AX = mybir.AxisListType

B, S, D = 16, 128, 128
P = 128
H = 16
DH0 = 64
DH1 = D // H
HU = 4
NU = H // HU
SEG = HU * S
E, F = 8, 408
HID = E * F
NCH = -(-HID // P)
OWNERS = [(P * c // F, min(P * c + P - 1, HID) // F) for c in range(NCH)]
REAL = HID - P * (NCH - 1)
PLANES = sorted(set(OWNERS))
PLANE = [PLANES.index(o) for o in OWNERS]
NP = len(PLANES)
PB = 2
G = 32
TOPK = 32
C = 8
NBLK = S // C
LR = 1.0 / D
EPS = 1e-5
NEG = -(2.0 ** 100)


def need(eng, sem, value):
    if isinstance(value, int) and value <= 0:
        return
    eng.wait_ge(sem, value)


def decoder_program(nc, a, out):
    with ExitStack() as ctx:
        def sb(name, shape, dt=F32):
            return ctx.enter_context(nc.sbuf_tensor(name, shape, dt))

        part_sems = []

        def sem(name):
            part_sems.append(nc.alloc_semaphore(name=name))
            return part_sems[-1]

        def part_ends():
            nc.clear_and_free_semaphores(list(part_sems))
            part_sems.clear()
            nc.all_engine_barrier()

        X = sb("X", [P, B, D])
        XT = sb("XT", [P, B, S])
        RES = sb("RES", [P, B, D])
        CTXT = sb("CTXT", [P, B, S])
        ident = sb("ident", [P, P])
        ident16 = sb("ident16", [P, P], BF16)
        stats = sb("stats", [P, B, 6])
        moments = sb("moments", [P, B, 2])
        rstd = sb("rstd", [P, B])
        half = sb("half", [P, B])

        qk_landed, loaded = sem("qk_landed"), sem("loaded")
        wo_landed = nc.alloc_semaphore(name="wo_landed")
        late_landed = nc.alloc_semaphore(name="late_landed")

        gl_landed, w1_landed, moe_landed = [nc.alloc_semaphore(name=n) for n in ("gl_landed", "w1_landed", "moe_landed")]
        lw_cleared = sem("lw_cleared")
        G2 = 2 * G
        ffw = sb("ffw", [P, D])
        groups = sb("groups", [P, G])
        convw = sb("convw", [P, 2])
        chan = sb("chan", [G2, 3])
        LW = sb("LW", [G2 + 1, 2 * D])
        ffb = sb("ffb", [1, D])
        W1 = sb("W1", [P, 8, D])
        window = sb("window", [P, S], BF16)
        jmask = sb("jmask", [P, HU])
        umask = sb("umask", [P, NU])
        colb = sb("colb", [P, 2])
        bo = sb("bo", [1, D])
        bv = sb("bv", [P, D])
        maskint = sb("maskint", [P, B, S], I32)
        gwT = sb("gwT", [P, E])
        gbias = sb("gbias", [P, E])
        number = sb("number", [P, E])
        owner = sb("owner", [3 * 32, NP, P], BF16)
        DWT = sb("DWT", [P, NCH, D])
        gb = sb("gb", [P, NCH])
        ub = sb("ub", [P, NCH])
        gl_loads = [(ffw, "ffw"), (groups, "groups"), (convw, "convw"), (chan, "chan"), (ffb, "ffb")]
        gl_parts = [(LW[0:G, 0:D], "lwo"), (LW[G:G2, D:2 * D], "lwi"), (LW[G2:G2 + 1, 0:D], "lbo"),
                    (LW[G2:G2 + 1, D:2 * D], "lbi")]
        w1_loads = [(W1, "w1"), (window, "window"), (jmask, "jmask"), (umask, "umask"), (colb, "colb"), (bo, "bo"),
                    (maskint, "mask"), (bv, "bv")]
        moe_loads = [(gwT, "gwT"), (gbias, "gbias"), (number, "number"), (owner, "owner"),
                     (DWT, "dwT"), (gb, "gpb"), (ub, "upb")]
        LATE_LANDED = 16 * 3
        GL_LANDED = 16 * (len(gl_loads) + len(gl_parts))
        W1_LANDED, MOE_LANDED = 16 * len(w1_loads), 16 * len(moe_loads)

        def products3(out_ap, left, right, start=True, stop=True):
            (lh, ll), (rh, rl) = left, right
            nc.tensor.matmul(out_ap, lh, rh, start=start, stop=False)
            nc.tensor.matmul(out_ap, lh, rl, start=False, stop=False)
            return nc.tensor.matmul(out_ap, ll, rh, start=False, stop=stop)

        def layernorm(name, also_time_major=None, out_to=None, also=None):
            stats_ready, var_ready, rstd_ready = sem(name + "_stats"), sem(name + "_var"), sem(name + "_rstd")
            x_ready, t_ready, xt_ready = sem(name + "_x"), sem(name + "_t"), sem(name + "_xt")
            with ExitStack() as scope:
                beside = {} if also is None else also(scope)
                nothing = lambda *q: None
                tp = [scope.enter_context(nc.psum_tensor(f"{name}_tp{i}", [P, 4, P], F32)) for i in range(2)]
                block = scope.enter_context(nc.Block())

                @block.vector
                def _(dve):
                    def aggregate(q):
                        for b in range(4 * q, 4 * q + 4):
                            nc.vector.bn_aggr(moments[:, b, :], stats[:, b, :]).then_inc(stats_ready, 1)

                    aggregate(0)
                    for q in range(4):
                        if q < 3:
                            aggregate(q + 1)
                        dve.wait_ge(stats_ready, 4 * q + 4)
                        four = slice(4 * q, 4 * q + 4)
                        nc.vector.tensor_scalar(rstd[:, four], moments[:, four, 1], EPS, None, ALU.add).then_inc(var_ready, 1)
                    beside.get("vector_first", nothing)()
                    for q in range(4):
                        dve.wait_ge(rstd_ready, q + 1)
                        for b in range(4 * q, 4 * q + 4):
                            nc.vector.tensor_scalar(X[:, b, :], RES[:, b, :], moments[:, b, 0:1], rstd[:, b:b + 1],
                                                    ALU.subtract, ALU.mult).then_inc(x_ready, 1)
                        if q >= 2:
                            beside.get("vector", nothing)(q - 2)
                    for q in (2, 3):
                        beside.get("vector", nothing)(q)

                @block.gpsimd
                def _(pool):
                    for q in range(4):
                        four = slice(4 * q, 4 * q + 4)
                        pool.wait_ge(var_ready, q + 1)
                        nc.gpsimd.tensor_tensor(rstd[:, four], rstd[:, four], half[:, four], ALU.pow).then_inc(rstd_ready, 1)
                    beside.get("gpsimd", nothing)()

                if out_to is not None:
                    stored = sem(name + "_stored")
                    rows = out_to.rearrange("b t c -> t b c")

                    @block.sync
                    def _(sp):
                        for q in range(4):
                            sp.wait_ge(x_ready, 4 * q + 4)
                            sp.dma_start(rows[:, 4 * q:4 * q + 4, :], X[:, 4 * q:4 * q + 4, :]).then_inc(stored, 16)
                        sp.wait_ge(stored, 16 * 4)
                    return

                @block.tensor
                def _(pe):
                    for q in range(B // 4):
                        need(pe, xt_ready, q - 1)
                        for j in range(4):
                            pe.wait_ge(x_ready, 4 * q + j + 1)
                            ins = nc.tensor.transpose(tp[q % 2][:, j, :], X[:, 4 * q + j, :], ident[:])
                        ins.then_inc(t_ready, 1)
                        if q and "tensor" in beside:
                            pe.wait_ge(xt_ready, q)
                            beside["tensor"](q - 1)
                    if "tensor" in beside:
                        pe.wait_ge(xt_ready, B // 4)
                        beside["tensor"](B // 4 - 1)

                @block.scalar
                def _(act):
                    beside.get("scalar_first", nothing)()
                    for q in range(B // 4):
                        act.wait_ge(t_ready, q + 1)
                        if also_time_major is not None:
                            nc.scalar.copy(also_time_major[:, :, 4 * q:4 * q + 4].rearrange("p t b -> p b t"), tp[q % 2][:])
                        nc.scalar.copy(XT[:, 4 * q:4 * q + 4, :], tp[q % 2][:]).then_inc(xt_ready, 1)
                        if q:
                            beside.get("scalar", nothing)(q - 1)
                    beside.get("scalar", nothing)(B // 4 - 1)

        def attention(name, wide, allowed, WO, ZM=None, WVT=None, QT=None, KT=None, VA=None, jmask=None, umask=None,
                      loads=None, maskbias=None, bo_row=None, ones_row=None):
            DV = DH0 if wide else DH1
            LT, LV, LO = (2, 3, 4) if wide else (3, 4, 5)
            PEEL = 1 if wide else 2
            VW = DV + 1
            NOT = HU * DV // P if wide else 1
            s_ = lambda what: sem(f"{name}_{what}")
            z_ready, zs_ready = s_("z_ready"), s_("zs_ready")
            stat_ready, v_ready, vs_ready = s_("stat_ready"), s_("v_ready"), s_("vs_ready")
            ones_ready = s_("ones_ready")
            s_ready, max_ready, e_ready, p_ready = s_("s_ready"), s_("max_ready"), s_("e_ready"), s_("p_ready")
            t_ready, pt_ready, pv_ready, rl_ready = s_("t_ready"), s_("pt_ready"), s_("pv_ready"), s_("rl_ready")
            on_ready, ot_ready, ots_ready = s_("on_ready"), s_("ot_ready"), s_("ots_ready")
            y_ready, res_ready, st_ready = s_("y_ready"), s_("res_ready"), s_("st_ready")
            keys_ready, high_ready, zh_ready = s_("keys_ready"), s_("high_ready"), s_("zh_ready")
            first_keys = s_("first_keys")
            with ExitStack() as scope:
                def lsb(what, shape, dt=F32):
                    return scope.enter_context(nc.sbuf_tensor(f"{name}_{what}", shape, dt))

                def lps(what, shape):
                    return scope.enter_context(nc.psum_tensor(f"{name}_{what}", shape, F32))

                if wide:
                    stat = [lsb("stath", [P, 2, S], FR), lsb("statl", [P, 2, S], FR)]
                else:
                    stat = [lsb("stath", [P, 2, NU, S], FR), lsb("statl", [P, 2, NU, S], FR)]
                Eb = lsb("E", [P, 2, HU, S])
                Pb = lsb("P", [P, 2, HU, S])
                PT = lsb("PT", [P, 2, HU, S])
                mx = lsb("mx", [P, 2, HU])
                rl = lsb("rl", [P, 2, HU])
                ON = lsb("ON", [P, 2, HU * DV if wide else D])
                OT = lsb("OT", [P, 2, max(NOT, 1), S])
                sp = [lps(f"sp{i}", [P, HU, S]) for i in range(2)]
                tp = [lps(f"tp{i}", [P, HU, S]) for i in range(2)]
                op = lps("op", [P, HU, VW])
                otp = lps("otp", [P, 2, S])
                yp = lps("yp", [P, D])
                if wide:
                    zp = lps("zp", [P, SEG])
                    zs = [lsb("zsh", [P, 2, SEG], FR), lsb("zsl", [P, 2, SEG], FR)]
                    VS = lsb("VS", [P, 2, H, VW])
                else:
                    kx = [lsb("kxh", [P, 2, HU, S], FR), lsb("kxl", [P, 2, HU, S], FR)]
                def keep_keys(eng, part, r, b, ready):
                    eng.tensor_tensor(kx[part][:, r], KT[part][:, b, :].bitcast(F32).unsqueeze(1).to_broadcast([P, HU, S]),
                                      jmask[:].unsqueeze(2).to_broadcast([P, HU, S]), ALU.mult).then_inc(ready, 1)

                def run(eng, slot, drain=LO):
                    for i in range(PEEL):
                        for j in range(8):
                            slot(i, j, lambda lag: 8 * i + j >= lag)
                    if wide:
                        eng.wait_ge(late_landed, LATE_LANDED)
                    with eng.Fori(PEEL, B // 2) as i:
                        for j in range(8):
                            slot(i, j, lambda lag: True)
                    for j in range(drain):
                        slot(B // 2, j, lambda lag: j < lag)

                block = scope.enter_context(nc.Block())

                if loads is not None:
                    @block.sync
                    def _(sp_eng):
                        loads(sp_eng)

                @block.gpsimd
                def _(pool):
                    if wide:
                        nc.gpsimd.memset(VS[:, :, :, DV:VW], 1.0).then_inc(ones_ready, 1)

                    def slot(i, j, live):
                        k = 8 * i + j
                        if j % NU == 0 and live(0):
                            b = 2 * i + j // NU
                            r = j // NU
                            need(pool, s_ready, k - NU)
                            if wide:
                                need(pool, v_ready, 4 * i + 2 * r - 2)
                            if wide:
                                nc.gpsimd.tensor_copy(stat[0][:, r, :], XT[:, b, :]).then_inc(high_ready, 1)
                            else:
                                for part in range(2):
                                    by_vector = isinstance(k, int) and k == 0
                                    nc.gpsimd.tensor_tensor(
                                        stat[part][:, r], QT[part][:, b, :].bitcast(F32).unsqueeze(1).to_broadcast([P, NU, S]),
                                        umask[:].unsqueeze(2).to_broadcast([P, NU, S]), ALU.mult).then_inc(stat_ready, 1)
                                    if not by_vector:
                                        keep_keys(nc.gpsimd, part, r, b, keys_ready)

                    run(pool, slot, 0)

                @block.tensor
                def _(pe):
                    if wide:
                        pe.wait_ge(ones_ready, 1)

                    def slot(i, j, live):
                        k = 8 * i + j
                        u = j % NU
                        if wide and live(0):
                            need(pe, zs_ready, k)
                            if u in (2, 3):
                                need(pe, vs_ready, 4 * i + 2 * (j // NU) + u - 1)
                            for h in range(HU):
                                ins = nc.tensor.matmul(zp[:, S * h:S * h + S], ZM[:, HU * u + h, :],
                                                       XT[:, 2 * i + j // NU, :], start=True, stop=True)
                            ins.then_inc(z_ready, 1)
                        vo, bo_ = (j - LO) % NU, 2 * i + (j - LO) // NU
                        def transpose_output():
                            if live(LO) and (wide or vo == 3):
                                n = k - LO
                                need(pe, on_ready, n + 1)
                                need(pe, ots_ready, n if wide else bo_)
                                for m in range(NOT):
                                    src = ON[:, j % 2, P * m:P * m + P] if wide else ON[:, ((j - LO) // NU) % 2, :]
                                    ins = nc.tensor.transpose(otp[:, m, :], src, ident[:])
                                ins.then_inc(ot_ready, 1)

                        if wide:
                            transpose_output()
                        if live(1):
                            n, r, v = k - 1, ((j - 1) // NU) % 2, (j - 1) % NU
                            parts = 1 if wide else 2
                            need(pe, stat_ready, parts * (2 * i + (j - 1) // NU + 1))
                            need(pe, e_ready, n - 1)
                            if wide:
                                pe.wait_ge(zs_ready, n + 1)
                                products3(sp[(j - 1) % 2][:], [x[:, r, :] for x in stat], [z[:, (j - 1) % 2, :] for z in zs],
                                          stop=False)
                            else:
                                if isinstance(n, int):
                                    pe.wait_ge(first_keys, parts)
                                need(pe, keys_ready, parts * (2 * i + (j - 1) // NU))
                                products3(sp[(j - 1) % 2][:], [x[:, r, v, :] for x in stat], [x[:, r] for x in kx], stop=False)
                            bias = allowed[:] if maskbias is None else maskbias[:, 2 * i + (j - 1) // NU, :]
                            nc.tensor.matmul(sp[(j - 1) % 2][:], ident16[:], bias.unsqueeze(1).to_broadcast([P, HU, S]),
                                             start=False, stop=True).then_inc(s_ready, 1)
                        if not wide:
                            transpose_output()
                        if live(LT):
                            n, q = k - LT, (j - LT) % 2
                            pe.wait_ge(p_ready, n + 1)
                            need(pe, pt_ready, n - 1)
                            for h in range(HU):
                                ins = nc.tensor.transpose(tp[q][:, h, :], Pb[:, q, h, :], ident[:])
                            ins.then_inc(t_ready, 1)
                        if wide and live(0) and u in (1, 2):
                            pe.wait_ge(zs_ready, k + 1)
                            r = j // NU
                            need(pe, stat_ready, 2 * i + r + 1)
                            products3(zp[:], [x[:, r, :] for x in stat], [w[:, SEG * (u - 1):SEG * u] for w in WVT]
                                      ).then_inc(v_ready, 1)
                        if live(LV):
                            n, v = k - LV, (j - LV) % NU
                            r = ((j - LV) // NU) % 2
                            pe.wait_ge(pt_ready, n + 1)
                            need(pe, on_ready, n)
                            if wide:
                                need(pe, vs_ready, 4 * i + 2 * ((j - LV) // NU) + 2)
                            for h in range(HU):
                                hh = HU * v + h
                                vals = VS[:, r, hh, :] if wide else VA[:, 2 * i + (j - LV) // NU, hh, :]
                                ins = nc.tensor.matmul(op[:, h, :], PT[:, (j - LV) % 2, h, :], vals, start=True, stop=True)
                            ins.then_inc(pv_ready, 1)
                        if live(LO) and (wide or vo == 3):
                            n, v = k - LO, vo
                            if wide:
                                if isinstance(n, int) and n == 0:
                                    pe.wait_ge(wo_landed, 16)
                                pe.wait_ge(ots_ready, n + 1)
                                if v == 0:
                                    need(pe, res_ready, bo_)
                                for m in range(NOT):
                                    ins = nc.tensor.matmul(yp[:], OT[:, j % 2, m, :], WO[:, NOT * v + m, :],
                                                           start=(v == 0 and m == 0), stop=(v == NU - 1 and m == NOT - 1))
                            else:
                                pe.wait_ge(ots_ready, bo_ + 1)
                                need(pe, res_ready, bo_)
                                ins = nc.tensor.matmul(yp[:], OT[:, ((j - LO) // NU) % 2, 0, :], WO[:, 0, :],
                                                       start=True, stop=bo_row is None)
                                if bo_row is not None:
                                    ins = nc.tensor.matmul(yp[:], ones_row[:], bo_row[:], start=False, stop=True)
                            ins.then_inc(y_ready, 1)

                    run(pe, slot)

                @block.scalar
                def _(act):
                    def slot(i, j, live):
                        k = 8 * i + j
                        if wide and live(0):
                            act.wait_ge(z_ready, k + 1)
                            need(act, s_ready, k - 1)
                            nc.scalar.copy(zs[0][:, j % 2, :], zp[:]).then_inc(zh_ready, 1)
                        if live(LT):
                            n, q = k - LT, (j - LT) % 2
                            act.wait_ge(t_ready, n + 1)
                            need(act, pv_ready, n - 1)
                            nc.scalar.copy(PT[:, q], tp[q][:]).then_inc(pt_ready, 1)
                        if live(1):
                            n = k - 1
                            act.wait_ge(e_ready, n + 1)
                            need(act, t_ready, n - 1)
                            nc.scalar.activation(Pb[:, (j - 1) % 2], Eb[:, (j - 1) % 2], ACT.Exp,
                                                 scale=1.0 if wide else float(DH1) ** -0.5).then_inc(p_ready, 1)

                    run(act, slot)

                @block.vector
                def _(dve):
                    if not wide:
                        for part in range(2):
                            keep_keys(nc.vector, part, 0, 0, first_keys)

                    def slot(i, j, live):
                        k = 8 * i + j
                        u = j % NU
                        vo, bo_ = (j - LO) % NU, 2 * i + (j - LO) // NU
                        def keep_output():
                            if live(LO) and (wide or vo == 3):
                                n = k - LO
                                if wide:
                                    dve.wait_ge(ot_ready, n + 1)
                                    need(dve, y_ready, n - 1)
                                    nc.vector.tensor_copy(OT[:, j % 2], otp[:]).then_inc(ots_ready, 1)
                                else:
                                    dve.wait_ge(ot_ready, bo_ + 1)
                                    need(dve, y_ready, bo_)
                                    nc.vector.tensor_copy(OT[:, ((j - LO) // NU) % 2, 0, :], otp[:, 0, :]).then_inc(ots_ready, 1)

                        if wide:
                            keep_output()
                            if live(0):
                                dve.wait_ge(zh_ready, k + 1)
                                nc.vector.tensor_tensor(zs[1][:, j % 2, :], zp[:], zs[0][:, j % 2, :].bitcast(F32),
                                                        ALU.subtract).then_inc(zs_ready, 1)
                            if live(0) and u == 0:
                                b, r = 2 * i + j // NU, j // NU
                                dve.wait_ge(high_ready, b + 1)
                                nc.vector.tensor_tensor(stat[1][:, r, :], XT[:, b, :], stat[0][:, r, :].bitcast(F32),
                                                        ALU.subtract).then_inc(stat_ready, 1)
                        if live(1):
                            n, q = k - 1, (j - 1) % 2
                            dve.wait_ge(s_ready, n + 1)
                            need(dve, e_ready, n - 1)
                            nc.vector.tensor_reduce(mx[:, q, :], sp[q][:], AX.X, ALU.max).then_inc(max_ready, 1)
                            dve.wait_ge(max_ready, n + 1)
                            need(dve, p_ready, n - 1)
                            nc.vector.tensor_tensor(Eb[:, q], sp[q][:], mx[:, q, :].unsqueeze(2).to_broadcast([P, HU, S]),
                                                    ALU.subtract).then_inc(e_ready, 1)
                        if not wide:
                            keep_output()
                        if wide and live(0) and u in (1, 2):
                            r = j // NU
                            dve.wait_ge(v_ready, 4 * i + 2 * r + u)
                            need(dve, pv_ready, k - u - NU)
                            nc.vector.tensor_copy(VS[:, r, 8 * (u - 1):8 * u, 0:DV],
                                                  zp[:].rearrange("p (h d) -> p h d", d=DV)).then_inc(vs_ready, 1)
                        if live(LV):
                            n, q = k - LV, (j - LV) % 2
                            dve.wait_ge(pv_ready, n + 1)
                            nc.vector.reciprocal(rl[:, q, :], op[:, :, DV]).then_inc(rl_ready, 1)
                            dve.wait_ge(rl_ready, n + 1)
                            if wide:
                                need(dve, ot_ready, n - 1)
                                o = ON[:, q, :]
                            else:
                                v = (j - LV) % NU
                                need(dve, ot_ready, 2 * i + (j - LV) // NU - 1)
                                o = ON[:, ((j - LV) // NU) % 2, 32 * v:32 * v + 32]
                            nc.vector.tensor_tensor(o.rearrange("p (h d) -> p h d", d=DV), op[:, :, 0:DV],
                                                    rl[:, q, :].unsqueeze(2).to_broadcast([P, HU, DV]),
                                                    ALU.mult).then_inc(on_ready, 1)
                        if live(LO) and vo == 3:
                            b = bo_
                            if wide and isinstance(i, int):
                                dve.wait_ge(late_landed, LATE_LANDED)
                            dve.wait_ge(y_ready, (4 * b + 4) if wide else (b + 1))
                            nc.vector.tensor_tensor(RES[:, b, :], yp[:], X[:, b, :], ALU.add).then_inc(res_ready, 1)
                            dve.wait_ge(res_ready, b + 1)
                            nc.vector.bn_stats(stats[:, b, :], RES[:, b, :]).then_inc(st_ready, 1)

                    run(dve, slot)

        def recurrence(XTt, YT):
            s_ = lambda what: sem(f"rec_{what}")
            w0x_ready, w0x_kept, padded = s_("w0x_ready"), s_("w0x_kept"), s_("padded")
            (far_gram_ready, far_gram_kept, rp_ready, rpb_ready, xblk_ready, gram_ready, gram_kept, masked_ready, prod_ready,
             gb_ready, gb_kept, far_ready, ct_ready, ct_kept, near_ready, t0_ready, u_ready, ut_ready, ut_kept,
             p_ready, pr_ready, y_ready, yt_ready, sq_ready, gt_ready, q_ready, qr_ready, fin_ready, ra_ready,
             c_loaded) = [s_(w) for w in (
                 "far_gram_ready far_gram_kept rp_ready rpb_ready xblk_ready gram_ready gram_kept masked_ready prod_ready "
                 "gb_ready gb_kept far_ready ct_ready ct_kept near_ready t0_ready u_ready ut_ready ut_kept "
                 "p_ready pr_ready y_ready yt_ready sq_ready gt_ready q_ready qr_ready fin_ready ra_ready "
                 "c_loaded").split()]
            ut_landed = [s_(f"ut_landed{i}") for i in range(2)]
            CB = C * B
            NG = B * C * (C - 1) // 2
            first = [sum(B * (C - 1 - r) for r in range(s)) for s in range(C)]
            with ExitStack() as scope:
                def lsb(what, shape, dt=F32):
                    return scope.enter_context(nc.sbuf_tensor(f"rec_{what}", shape, dt))

                W0X = [lsb(f"W0X{w}", [P, B, S + 2 * C], FR) for w in "HL"]
                identR = lsb("identR", [P, P], FR)
                same = lsb("same", [P, CB])
                lrs = lsb("lrs", [P, P])
                GF = lsb("GF", [P, B, S + 2 * C])
                UT = lsb("UT", [P, B, D])
                CF = lsb("CF", [P, 2, 1 + C, B])
                xblk = lsb("xblk", [P, 2, CB])
                prod = lsb("prod", [P, 2, NG])

                def products(k, j):
                    need(nc.gpsimd, gb_ready, k - 1)
                    for s in range(C - 1):
                        n = C - 1 - s
                        ins = nc.gpsimd.tensor_tensor(
                            prod[:, j, first[s]:first[s] + B * n].rearrange("p (t b) -> p t b", b=B),
                            XTt[:, bass.ds(C * k + s, 1), :].to_broadcast([P, n, B]),
                            XTt[:, bass.ds(C * k + s + 1, n), :], ALU.mult)
                    ins.then_inc(prod_ready, 1)

                def stationary(k, j):
                    nc.gpsimd.tensor_copy(xblk[:, j, :], XTt[:, bass.ds(C * k, C), :].rearrange("p t b -> p (t b)")
                                          ).then_inc(xblk_ready, 1)

                with ExitStack() as inner:
                    wp = [inner.enter_context(nc.psum_tensor(f"rec_wp{i}", [P, 4, S], F32)) for i in range(4)]
                    fgp = [inner.enter_context(nc.psum_tensor(f"rec_fgp{i}", [P, 4, S], F32)) for i in range(4)]
                    block = inner.enter_context(nc.Block())

                    @block.sync
                    def _(sp):
                        sp.dma_start(same[:], a["same"]).then_inc(c_loaded, 16)
                        sp.wait_ge(c_loaded, 16)

                    @block.gpsimd
                    def _(pool):
                        nc.gpsimd.memset(lrs[:], LR)
                        products(0, 0)
                        stationary(0, 0)
                        stationary(1, 1)
                        products(1, 1)
                        nc.gpsimd.memset(XTt[:, S:S + 3 * C, :], 0.0).then_inc(padded, 1)
                        pool.wait_ge(padded, 1)
                        for w in W0X:
                            nc.gpsimd.tensor_copy(w[:, :, S:S + 2 * C], XTt[:, S:S + 2 * C, :].rearrange("p t b -> p b t"))

                    @block.tensor
                    def _(pe):
                        pe.wait_ge(late_landed, LATE_LANDED)
                        for q in range(4):
                            for r in range(4):
                                ins = nc.tensor.matmul(wp[q][:, r, :], CTXT[:, 4 * q + r, :], XT[:, 4 * q + r, :],
                                                       start=True, stop=True)
                            ins.then_inc(w0x_ready, 1)
                        for q in range(4):
                            for r in range(4):
                                ins = nc.tensor.matmul(fgp[q][:, r, :], XT[:, 4 * q + r, :], XT[:, 4 * q + r, :],
                                                       start=True, stop=True)
                            ins.then_inc(far_gram_ready, 1)

                    @block.scalar
                    def _(act):
                        for q in range(4):
                            act.wait_ge(w0x_ready, q + 1)
                            nc.scalar.copy(W0X[0][:, 4 * q:4 * q + 4, 0:S], wp[q][:]).then_inc(w0x_kept, 1)

                    @block.vector
                    def _(dve):
                        nc.vector.memset(GF[:, :, S:S + 2 * C], 0.0)
                        nc.vector.memset(UT[:], 0.0)
                        nc.vector.memset(CF[:, 1, 0, :], 1.0)
                        nc.vector.tensor_copy(identR[:], ident[:])
                        for q in range(4):
                            four = slice(4 * q, 4 * q + 4)
                            dve.wait_ge(w0x_kept, q + 1)
                            nc.vector.tensor_tensor(W0X[1][:, four, 0:S], wp[q][:], W0X[0][:, four, 0:S].bitcast(F32), ALU.subtract)
                        for q in range(4):
                            dve.wait_ge(far_gram_ready, q + 1)
                            nc.vector.tensor_scalar(GF[:, 4 * q:4 * q + 4, 0:S], fgp[q][:], LR, None, ALU.mult).then_inc(far_gram_kept, 1)

                def lps(what, shape):
                    return scope.enter_context(nc.psum_tensor(f"rec_{what}", shape, F32))

                graw = [lsb("graw0", [P, 3, CB]), lsb("graw1", [P, 2, CB])]
                gm = [lsb("gm0", [P, 3, CB]), lsb("gm1", [P, 2, CB])]
                GB = lsb("GB", [P, 2, NG])
                cTk = lsb("cTk", [P, 2, D])
                uTk = lsb("uTk", [P, 2, D])
                pm = lsb("pm", [P, C, B])
                t0 = lsb("t0", [P, C, B])
                sq = lsb("sq", [P, 2, B])
                gt = lsb("gt", [P, 2, C - 1, B])
                qt = lsb("qt", [P, 2, C - 1, B])
                RA = lsb("RA", [P, B])
                U = lsb("U", [P, C, B])
                rp = lps("rp", [P, B, 2 * C])
                np_ = lps("np", [P, C, B])
                ctp, utp = lps("ctp", [P, D]), lps("utp", [P, D])
                gp = [lps("gp0", [P, 3, CB]), lps("gp1", [P, 2, CB])]
                gbp = [lps(f"gbp{i}", [P, NG]) for i in range(2)]
                block = scope.enter_context(nc.Block())

                def blocks(eng, slot):
                    for j in range(2):
                        slot(j, j)
                    with eng.Fori(1, NBLK // 2) as i:
                        for j in range(2):
                            slot(2 * i + j, j)

                @block.gpsimd
                def _(pool):
                    products(2, 0)

                    def slot(k, j):
                        if j == 0:
                            pool.wait_ge(gram_kept, k + 1)
                            need(pool, rp_ready, k // 2)
                            nc.gpsimd.tensor_tensor(gm[0][:], graw[0][:], same[:].unsqueeze(1).to_broadcast([P, 3, CB]),
                                                    ALU.mult).then_inc(masked_ready, 1)
                            pool.wait_ge(gram_kept, k + 2)
                            need(pool, rpb_ready, k // 2 + 1)
                            nc.gpsimd.tensor_tensor(gm[1][:], graw[1][:], same[:].unsqueeze(1).to_broadcast([P, 2, CB]),
                                                    ALU.mult).then_inc(masked_ready, 1)
                            stationary(k + 2, 0)
                            stationary(k + 3, 1)
                        else:
                            products(k + 2, 1)
                            products(k + 3, 0)
                        pool.wait_ge(ra_ready, k + 1)
                        need(pool, ut_ready, k)
                        nc.gpsimd.tensor_tensor(U[:], CF[:, j, 1:1 + C, :], RA[:].unsqueeze(1).to_broadcast([P, C, B]),
                                                ALU.mult).then_inc(u_ready, 1)

                    blocks(pool, slot)

                @block.sync
                def _(sp):
                    for k in range(NBLK - 1):
                        sp.wait_ge(ut_kept, k + 1)
                        sp.wait_ge(far_ready, k // 2 + 1)
                        sp.dma_start(UT[C * k:C * k + C, :, :], uTk[:, k % 2, :]).then_inc(ut_landed[k % 2], 16)
                    for j in range(2):
                        sp.wait_ge(ut_landed[j], 16 * (NBLK // 2 - j))

                @block.tensor
                def _(pe):
                    def broadcast(k, j):
                        pe.wait_ge(prod_ready, k + 1)
                        need(pe, gb_kept, k - 1)
                        nc.tensor.matmul(gbp[j][:], lrs[:], prod[:, j, :], start=True, stop=True).then_inc(gb_ready, 1)

                    def grams(k, j):
                        pe.wait_ge(xblk_ready, k + 1)
                        need(pe, gram_kept, k - 1)
                        nc.tensor.matmul(gp[j][:], xblk[:, j, :], XTt[:, bass.ds(C * k + C, (3 - j) * C), :],
                                         start=True, stop=True).then_inc(gram_ready, 1)

                    broadcast(0, 0)
                    def w0x(t):
                        nc.tensor.matmul(rp[:], identR[:], W0X[0][:, :, t], start=True, stop=False, skip_group_check=True)
                        return nc.tensor.matmul(rp[:], identR[:], W0X[1][:, :, t], start=False, stop=False, skip_group_check=True)

                    w0x(slice(0, 2 * C)).then_inc(rpb_ready, 1)

                    def slot(k, j):
                        first_pair = isinstance(k, int)
                        after_a_block = not (first_pair and k == 0)
                        if after_a_block:
                            pe.wait_ge(fin_ready, C * k)
                            nc.tensor.transpose(ctp[:], CF[:, 1 - j, 1:1 + C, :].rearrange("p s b -> p (s b)"),
                                                ident[:]).then_inc(ct_ready, 1)
                            pe.wait_ge(masked_ready, k)
                            pe.wait_ge(ct_kept, k)
                            nc.tensor.matmul(np_[:], cTk[:, 1 - j, :], gm[1 - j][:, 0, :], start=True, stop=True).then_inc(near_ready, 1)
                        if j == 0:
                            grams(k, 0)
                        def transpose_u():
                            pe.wait_ge(u_ready, k)
                            need(pe, ut_kept, k - 1)
                            nc.tensor.transpose(utp[:], U[:].rearrange("p s b -> p (s b)"), ident[:]).then_inc(ut_ready, 1)

                        if j == 0:
                            if after_a_block:
                                transpose_u()
                            grams(k + 1, 1)
                            broadcast(k + 1, 1)
                            broadcast(k + 2, 0)
                            if after_a_block:
                                pe.wait_ge(t0_ready, k)
                                pe.wait_ge(ut_kept, k)
                                nc.tensor.matmul(rp[:, :, C:2 * C], uTk[:, 1, :], gm[1][:, 1, :].rearrange("p (t b) -> p b t", b=B),
                                                 start=False, stop=True, skip_group_check=True).then_inc(rpb_ready, 1)
                            return
                        if first_pair:
                            transpose_u()
                        pe.wait_ge(t0_ready, k)
                        ins = w0x(bass.ds(C * k + C, 2 * C))
                        if not first_pair:
                            for rows_landed in ut_landed:
                                pe.wait_ge(rows_landed, 8 * (k - 1))
                            for b in range(B):
                                if b == 2:
                                    transpose_u()
                                ins = nc.tensor.matmul(rp[:, b, :], UT[:, b, :], GF[:, b, bass.ds(C * k + C, 2 * C)],
                                                       start=False, stop=False, skip_group_check=True)
                        ins.then_inc(far_ready, 1)
                        pe.wait_ge(ut_kept, k)
                        nc.tensor.matmul(rp[:], uTk[:, 0, :], gm[0][:, 1:3, :].rearrange("p h (t b) -> p b (h t)", b=B),
                                         start=False, stop=True, skip_group_check=True).then_inc(rp_ready, 1)

                    blocks(pe, slot)

                @block.scalar
                def _(act):
                    def keep_gb(k, j):
                        act.wait_ge(gb_ready, k + 1)
                        nc.scalar.copy(GB[:, j, :], gbp[j][:]).then_inc(gb_kept, 1)

                    keep_gb(0, 0)

                    def slot(k, j):
                        first_block = isinstance(k, int) and k == 0
                        if not first_block:
                            act.wait_ge(ct_ready, k)
                            nc.scalar.copy(cTk[:, 1 - j, :], ctp[:]).then_inc(ct_kept, 1)
                        for s in range(C):
                            act.wait_ge(p_ready, C * k + s + 1)
                            nc.scalar.activation(CF[:, j, 1 + s, :], pm[:, s, :], ACT.Sigmoid).then_inc(y_ready, 1)
                            act.wait_ge(y_ready, C * k + s + 1)
                            nc.scalar.copy(YT[:, bass.ds(C * k + s, 1), :], CF[:, j, 1 + s:2 + s, :]).then_inc(yt_ready, 1)
                            if s == 0 and not first_block:
                                act.wait_ge(ut_ready, k)
                                if j == 1:
                                    need(act, ut_landed[0], 8 * (k - 1))
                                nc.scalar.copy(uTk[:, 1 - j, :], utp[:]).then_inc(ut_kept, 1)
                            if j == 0 and s in (1, 2):
                                act.wait_ge(gram_ready, k + s)
                                need(act, masked_ready, k + s - 2)
                                nc.scalar.copy(graw[s - 1][:], gp[s - 1][:]).then_inc(gram_kept, 1)
                            if s == 4:
                                keep_gb(k + 1, 1 - j)

                    blocks(act, slot)

                @block.vector
                def _(dve):
                    def slot(k, j):
                        if isinstance(k, int) and k == 0:
                            high, low = [w[:, :, 0:C].bitcast(F32).rearrange("p b t -> p t b") for w in W0X]
                            nc.vector.tensor_tensor(pm[:, 0, :], high[:, 0, :], low[:, 0, :], ALU.add).then_inc(p_ready, 1)
                            nc.vector.tensor_tensor(pm[:, 1:C, :], high[:, 1:C, :], low[:, 1:C, :], ALU.add).then_inc(pr_ready, 1)
                        else:
                            dve.wait_ge(fin_ready, C * k)
                            if j == 0:
                                dve.wait_ge(rp_ready, k // 2)
                            else:
                                dve.wait_ge(rpb_ready, (k + 1) // 2)
                            nc.vector.tensor_tensor(t0[:], rp[:, :, C * j:C * j + C].rearrange("p b t -> p t b"),
                                                    CF[:, 1 - j, 0:1, :].to_broadcast([P, C, B]), ALU.mult).then_inc(t0_ready, 1)
                            need(dve, u_ready, k - 1)
                            nc.vector.reciprocal(RA[:], CF[:, 1 - j, 0, :]).then_inc(ra_ready, 1)
                            dve.wait_ge(t0_ready, k)
                            dve.wait_ge(near_ready, k)
                            nc.vector.tensor_tensor(pm[:, 0, :], np_[:, 0, :], t0[:, 0, :], ALU.add).then_inc(p_ready, 1)
                            nc.vector.tensor_tensor(pm[:, 1:C, :], np_[:, 1:C, :], t0[:, 1:C, :], ALU.add).then_inc(pr_ready, 1)
                        dve.wait_ge(gb_kept, k + 1)
                        for s in range(C):
                            n = C - 1 - s
                            dve.wait_ge(y_ready, C * k + s + 1)
                            y = CF[:, j, 1 + s, :]
                            nc.vector.scalar_tensor_tensor(sq[:, s % 2], y, -LR, y, ALU.mult, ALU.mult).then_inc(sq_ready, 1)
                            if n:
                                nc.vector.tensor_tensor(gt[:, s % 2, 0:n], GB[:, j, first[s]:first[s] + B * n].rearrange("p (t b) -> p t b", b=B),
                                                        y.unsqueeze(1).to_broadcast([P, n, B]), ALU.mult).then_inc(gt_ready, 1)
                            dve.wait_ge(sq_ready, C * k + s + 1)
                            decay = lambda to, src, m: nc.vector.scalar_tensor_tensor(
                                to, sq[:, s % 2].unsqueeze(1).to_broadcast([P, m, B]), 1.0, src, ALU.add, ALU.mult)
                            if n:
                                decay(qt[:, s % 2, 0:1], pm[:, s + 1:s + 2, :], 1).then_inc(q_ready, 1)
                            if n > 1:
                                decay(qt[:, s % 2, 1:n], pm[:, s + 2:C, :], n - 1).then_inc(qr_ready, 1)
                            if n:
                                dve.wait_ge(q_ready, (C - 1) * k + s + 1)
                                nc.vector.tensor_tensor(pm[:, s + 1, :], qt[:, s % 2, 0], gt[:, s % 2, 0], ALU.add).then_inc(p_ready, 1)
                            if s:
                                dve.wait_ge(yt_ready, C * k + s)
                                decay(CF[:, j, 0:s + 1, :], CF[:, j, 0:s + 1, :], s + 1).then_inc(fin_ready, 1)
                            else:
                                decay(CF[:, j, 0:1, :], CF[:, 1 - j, 0:1, :], 1).then_inc(fin_ready, 1)
                            if n > 1:
                                dve.wait_ge(qr_ready, (C - 2) * k + s + 1)
                                nc.vector.tensor_tensor(pm[:, s + 2:C, :], qt[:, s % 2, 1:n], gt[:, s % 2, 1:n], ALU.add).then_inc(pr_ready, 1)

                    blocks(dve, slot)
                    dve.wait_ge(fin_ready, C * NBLK)
                    nc.vector.reciprocal(RA[:], CF[:, (NBLK - 1) % 2, 0, :]).then_inc(ra_ready, 1)

        def add_recurrence(YT):
            t_ready, res_ready, st_ready = sem("addrec_t_ready"), sem("addrec_res_ready"), sem("addrec_st_ready")
            with ExitStack() as scope:
                tp = [scope.enter_context(nc.psum_tensor(f"addrec_tp{i}", [P, 4, P], F32)) for i in range(2)]
                block = scope.enter_context(nc.Block())

                @block.tensor
                def _(pe):
                    for q in range(B // 4):
                        need(pe, res_ready, q - 1)
                        for j in range(4):
                            ins = nc.tensor.transpose(tp[q % 2][:, j, :], YT[:, 0:S, 4 * q + j], ident[:])
                        ins.then_inc(t_ready, 1)

                @block.vector
                def _(dve):
                    for q in range(B // 4):
                        dve.wait_ge(t_ready, q + 1)
                        nc.vector.tensor_tensor(RES[:, 4 * q:4 * q + 4, :], tp[q % 2][:], X[:, 4 * q:4 * q + 4, :],
                                                ALU.add).then_inc(res_ready, 1)
                        dve.wait_ge(res_ready, q + 1)
                        for j in range(4):
                            nc.vector.bn_stats(stats[:, 4 * q + j, :], RES[:, 4 * q + j, :]).then_inc(st_ready, 1)

        def narrow_operands(name, WQT, WKT, WVT, keys_from, QT, KT, VA, bias_q=None, bias_k=None, bias_v=None,
                            ones_row=None, maskbias=None):
            s_ = lambda what: sem(f"{name}_{what}")
            q_ready, q_high, q_kept, k_ready, k_high, k_kept, v_ready, v_kept = [s_(w) for w in (
                "q_ready q_high q_kept k_ready k_high k_kept v_ready v_kept").split()]

            def also(scope):
                qp, kp, vp = [[scope.enter_context(nc.psum_tensor(f"{name}_{w}{i}", [P, 4, S], F32)) for i in range(2)]
                              for w in ("qp", "kp", "vp")]
                heads = lambda t: t.rearrange("p b (h d) -> p b h d", d=DH1)

                def on_gpsimd():
                    nc.gpsimd.memset(VA[:, :, :, DH1:DH1 + 1], 1.0)
                    if ones_row is not None:
                        nc.gpsimd.memset(ones_row[:], 1.0)
                    nc.gpsimd.wait_ge(w1_landed, W1_LANDED)

                def on_tensor(q):
                    pe = nc.tensor
                    if q == 0:
                        pe.wait_ge(w1_landed, W1_LANDED)
                    need(pe, k_kept, q - 1)
                    pe.matmul(kp[q % 2][:], WKT[:], keys_from[:, 4 * q:4 * q + 4, :], start=True, stop=True).then_inc(k_ready, 1)
                    need(pe, q_kept, q - 1)
                    pe.matmul(qp[q % 2][:], WQT[:], XT[:, 4 * q:4 * q + 4, :], start=True, stop=True).then_inc(q_ready, 1)
                    need(pe, v_kept, q - 1)
                    for j in range(4):
                        ins = pe.matmul(vp[q % 2][:, j, :], keys_from[:, 4 * q + j, :], WVT[:], start=True, stop=True)
                    ins.then_inc(v_ready, 1)

                def on_scalar(q):
                    act = nc.scalar
                    if q == 0:
                        act.wait_ge(w1_landed, W1_LANDED)
                    four = slice(4 * q, 4 * q + 4)
                    for ready, high, dst, src, bias in ((k_ready, k_high, KT, kp, bias_k), (q_ready, q_high, QT, qp, bias_q)):
                        act.wait_ge(ready, q + 1)
                        act.activation(dst[0][:, four, :], src[q % 2][:], ACT.Identity,
                                       bias=0.0 if bias is None else bias).then_inc(high, 1)
                    if bias_v is None:
                        act.wait_ge(v_ready, q + 1)
                        act.copy(VA[:, four, :, 0:DH1], heads(vp[q % 2][:])).then_inc(v_kept, 1)

                def on_vector_first():
                    nc.vector.wait_ge(w1_landed, W1_LANDED)
                    if maskbias is not None:
                        for q in range(B // 4):
                            nc.vector.tensor_scalar(maskbias[:, 4 * q:4 * q + 4, :], maskint[:, 4 * q:4 * q + 4, :], 0.0, NEG,
                                                    ALU.is_equal, ALU.mult)

                def on_vector(q):
                    dve = nc.vector
                    four = slice(4 * q, 4 * q + 4)
                    for high, kept, dst, src, bias in ((k_high, k_kept, KT, kp, bias_k), (q_high, q_kept, QT, qp, bias_q)):
                        dve.wait_ge(high, q + 1)
                        dve.scalar_tensor_tensor(dst[1][:, four, :], src[q % 2][:], 0.0 if bias is None else bias,
                                                 dst[0][:, four, :].bitcast(F32), ALU.add, ALU.subtract).then_inc(kept, 1)
                    if bias_v is not None:
                        dve.wait_ge(v_ready, q + 1)
                        dve.tensor_tensor(VA[:, four, :, 0:DH1], heads(vp[q % 2][:]),
                                          bias_v.rearrange("p (h d) -> p h d", d=DH1).unsqueeze(1).to_broadcast([P, 4, H, DH1]),
                                          ALU.add).then_inc(v_kept, 1)

                return {"gpsimd": on_gpsimd, "tensor": on_tensor, "scalar": on_scalar, "vector_first": on_vector_first,
                        "vector": on_vector}

            return also

        def gated_layer():
            s_ = lambda what: sem(f"gl_{what}")
            (cleared, wc_ready, xc_ready, xc_kept, st_ready, ag_ready, ve_ready, rs_ready, sc_ready, bi_ready,
             xa_ready) = [s_(w) for w in (
                 "cleared wc_ready xc_ready xc_kept st_ready ag_ready ve_ready rs_ready sc_ready bi_ready "
                 "xa_ready").split()]
            with ExitStack() as scope:
                def lsb(what, shape, dt=F32):
                    return scope.enter_context(nc.sbuf_tensor(f"gl_{what}", shape, dt))

                WC = lsb("WC", [P, G2])
                XC = lsb("XC", [G2, B, S])
                XA = lsb("XA", [G2 + 1, B, S])
                bst = lsb("bst", [G2, 4, 6])
                bag = lsb("bag", [G2, 2])
                brs = lsb("brs", [G2, 1])
                bhalf = lsb("bhalf", [G2, 1])
                bsc = lsb("bsc", [G2, 1])
                bms = lsb("bms", [G2, 1])
                bbi = lsb("bbi", [G2, 1])
                ones1 = lsb("ones1", [1, P])
                ms_ready = s_("ms_ready")
                WS = NCH * P // B
                whole_landed, high_ready = s_("whole_landed"), s_("high_ready")
                splits = (lsb("GP", [P, NCH * P]), GPH, GPL), (lsb("UP", [P, NCH * P]), UPH, UPL)

                with ExitStack() as inner:
                    xcp = [inner.enter_context(nc.psum_tensor(f"gl_xcp{i}", [G2, 4, S], F32)) for i in range(4)]
                    block = inner.enter_context(nc.Block())

                    @block.sync
                    def _(sp):
                        for (whole, _, _), name in zip(splits, ("gpT", "upT")):
                            sp.dma_start(whole[:], a[name]).then_inc(whole_landed, 16)

                    @block.gpsimd
                    def _(pool):
                        nc.gpsimd.memset(bhalf[:], -0.5).then_inc(cleared, 1)
                        pool.wait_ge(gl_landed, GL_LANDED)
                        for v in range(2):
                            nc.gpsimd.tensor_scalar(WC[:, G * v:G * v + G], groups[:], convw[:, v:v + 1], None,
                                                    ALU.mult).then_inc(wc_ready, 1)
                        pool.wait_ge(ve_ready, 1)
                        pool.wait_ge(cleared, 1)
                        nc.gpsimd.tensor_tensor(brs[:], brs[:], bhalf[:], ALU.pow).then_inc(rs_ready, 1)

                    @block.tensor
                    def _(pe):
                        pe.wait_ge(wc_ready, 2)
                        for q in range(4):
                            nc.tensor.matmul(xcp[q][:], WC[:], XT[:, 4 * q:4 * q + 4, :], start=True, stop=True).then_inc(xc_ready, 1)

                    @block.scalar
                    def _(act):
                        act.wait_ge(gl_landed, GL_LANDED)
                        for q in range(4):
                            act.wait_ge(xc_ready, q + 1)
                            nc.scalar.activation(XC[:, 4 * q:4 * q + 4, :], xcp[q][:], ACT.Identity, bias=chan[:, 0:1]).then_inc(xc_kept, 1)
                        act.wait_ge(bi_ready, 1)
                        for q in range(4):
                            nc.scalar.activation(XA[0:G2, 4 * q:4 * q + 4, :], XC[:, 4 * q:4 * q + 4, :], ACT.Gelu,
                                                 bias=bbi[:], scale=bsc[:]).then_inc(xa_ready, 1)

                    @block.vector
                    def _(dve):
                        nc.vector.memset(XA[G2:G2 + 1], 1.0)
                        nc.vector.memset(ones1[:], 1.0)
                        for q in range(4):
                            dve.wait_ge(xc_kept, q + 1)
                            nc.vector.bn_stats(bst[:, q, :], XC[:, 4 * q:4 * q + 4, :].rearrange("p b s -> p (b s)")).then_inc(st_ready, 1)
                        dve.wait_ge(st_ready, 4)
                        nc.vector.bn_aggr(bag[:], bst[:].rearrange("p q s -> p (q s)")).then_inc(ag_ready, 1)
                        dve.wait_ge(ag_ready, 1)
                        nc.vector.tensor_scalar(brs[:], bag[:, 1:2], EPS, None, ALU.add).then_inc(ve_ready, 1)
                        dve.wait_ge(rs_ready, 1)
                        nc.vector.tensor_tensor(bsc[:], brs[:], chan[:, 1:2], ALU.mult).then_inc(sc_ready, 1)
                        dve.wait_ge(sc_ready, 1)
                        nc.vector.tensor_tensor(bms[:], bag[:, 0:1], bsc[:], ALU.mult).then_inc(ms_ready, 1)
                        dve.wait_ge(ms_ready, 1)
                        nc.vector.tensor_tensor(bbi[:], chan[:, 2:3], bms[:], ALU.subtract).then_inc(bi_ready, 1)

                (xs_ready, as_ready, lg_ready, mx_ready, e_ready, m_ready, w_ready, sel_ready, rs2_ready, nr_ready,
                 xg_ready, xt_ready, xt_kept, y_ready, full_ready, t1_ready, t2_ready, res_ready, bs_ready) = [s_(w) for w in (
                     "xs_ready as_ready lg_ready mx_ready e_ready m_ready w_ready sel_ready rs2_ready nr_ready "
                     "xg_ready xt_ready xt_kept y_ready full_ready t1_ready t2_ready res_ready bs_ready").split()]
                xs = lsb("xs", [P, 2, S])
                xas = lsb("xas", [G2 + 1, 2, S])
                nmx = lsb("nmx", [P, 2, 2])
                ex = lsb("ex", [P, 2, 2, D])
                ssum = lsb("ssum", [P, 2, 2])
                m8 = lsb("m8", [P, 2, 8])
                wk = lsb("wk", [P, 2, D])
                sel = lsb("sel", [P, 2, 2, D])
                rs2 = lsb("rs2", [P, 2, 2])
                nrs = lsb("nrs", [P, 2, 2])
                xg = lsb("xg", [P, 2, D])
                xgt = lsb("xgt", [P, 2, S])
                t1 = lsb("t1", [P, 2, D])
                t2 = lsb("t2", [P, 2, D])
                lgp = [scope.enter_context(nc.psum_tensor(f"gl_lgp{i}", [P, 2, D], F32)) for i in range(2)]
                fup = [scope.enter_context(nc.psum_tensor(f"gl_fup{i}", [P, D], F32)) for i in range(2)]
                xtp = scope.enter_context(nc.psum_tensor("gl_xtp", [P, S], F32))
                y2p = scope.enter_context(nc.psum_tensor("gl_y2p", [P, D], F32))
                block = scope.enter_context(nc.Block())
                ROUNDS = TOPK // 8

                def run(eng, slot):
                    for b in range(4):
                        slot(b, b % 2, lambda lag: b >= lag)
                    with eng.Fori(2, B // 2) as i:
                        for r in range(2):
                            slot(2 * i + r, r, lambda lag: True)
                    slot(B, 0, lambda lag: lag > 0)
                    slot(B + 1, 1, lambda lag: lag > 1)

                @block.gpsimd
                def _(pool):
                    def slot(b, r, live):
                        if live(0):
                            need(pool, lg_ready, b - 1)
                            nc.gpsimd.tensor_copy(xas[:, r, :], XA[:, b, :]).then_inc(as_ready, 1)
                            need(pool, full_ready, b - 1)
                            nc.gpsimd.tensor_copy(xs[:, r, :], XT[:, b, :]).then_inc(xs_ready, 1)
                        if live(1):
                            pool.wait_ge(high_ready, b)
                            cols = bass.ds(WS * (b - 1), WS)
                            for whole, high, low in splits:
                                nc.gpsimd.tensor_tensor(low[:, cols], whole[:, cols], high[:, cols].bitcast(F32), ALU.subtract)
                    pool.wait_ge(whole_landed, 32)
                    run(pool, slot)

                @block.tensor
                def _(pe):
                    def slot(b, r, live):
                        if live(0):
                            pe.wait_ge(as_ready, b + 1)
                            need(pe, e_ready, 2 * b - 2)
                            nc.tensor.matmul(lgp[r][:], xas[:, r, :], LW[:], start=True, stop=True).then_inc(lg_ready, 1)
                            pe.wait_ge(xs_ready, b + 1)
                            need(pe, t1_ready, b - 1)
                            nc.tensor.matmul(fup[r][:], xs[:, r, :], ffw[:], start=True, stop=True).then_inc(full_ready, 1)
                        if live(2):
                            n = b - 2
                            pe.wait_ge(xg_ready, n + 1)
                            need(pe, xt_kept, n)
                            nc.tensor.transpose(xtp[:], xg[:, r, :], ident[:]).then_inc(xt_ready, 1)
                            pe.wait_ge(xt_kept, n + 1)
                            need(pe, res_ready, n)
                            nc.tensor.matmul(y2p[:], xgt[:, r, :], ffw[:], start=True, stop=False)
                            nc.tensor.matmul(y2p[:], ones1[:], ffb[:], start=False, stop=True).then_inc(y_ready, 1)
                    run(pe, slot)

                @block.scalar
                def _(act):
                    def slot(b, r, live):
                        if live(0):
                            act.wait_ge(mx_ready, b + 1)
                            need(act, xg_ready, b - 1)
                            need(act, t1_ready, b - 1)
                            for v in range(2):
                                nc.scalar.activation(ex[:, r, v, :], lgp[r][:, v, :], ACT.Exp, bias=nmx[:, r, v:v + 1],
                                                     accum_out=ssum[:, r, v:v + 1]).then_inc(e_ready, 1)
                            cols = bass.ds(WS * b, WS)
                            for whole, high, _ in splits:
                                ins = nc.scalar.copy(high[:, cols], whole[:, cols])
                            ins.then_inc(high_ready, 1)
                        if live(2):
                            n = b - 2
                            act.wait_ge(xt_ready, n + 1)
                            need(act, y_ready, n - 1)
                            nc.scalar.copy(xgt[:, r, :], xtp[:]).then_inc(xt_kept, 1)
                    act.wait_ge(whole_landed, 32)
                    run(act, slot)

                @block.vector
                def _(dve):
                    def slot(b, r, live):
                        if live(0):
                            dve.wait_ge(lg_ready, b + 1)
                            need(dve, e_ready, 2 * b - 2)
                            nc.vector.tensor_reduce(nmx[:, r, :], lgp[r][:], AX.X, ALU.max, negate=True).then_inc(mx_ready, 1)
                        n, p = b - 1, 1 - r
                        if live(1):
                            dve.wait_ge(e_ready, 2 * n + 2)
                            nc.vector.reciprocal(rs2[:, p, :], ssum[:, p, :]).then_inc(rs2_ready, 1)
                            dve.sem_clear(m_ready)
                            dve.sem_clear(w_ready)
                            for z in range(ROUNDS):
                                for v in range(2):
                                    w = ex[:, p, v, :] if z == 0 else wk[:, v, :]
                                    if z:
                                        dve.wait_ge(w_ready, 2 * (z - 1) + v + 1)
                                    nc.vector.max(m8[:, v, :], w).then_inc(m_ready, 1)
                                for v in range(2):
                                    w = ex[:, p, v, :] if z == 0 else wk[:, v, :]
                                    dve.wait_ge(m_ready, 2 * z + v + 1)
                                    nc.vector.match_replace(wk[:, v, :], m8[:, v, :], w, -1.0).then_inc(w_ready, 1)
                            dve.wait_ge(rs2_ready, n + 1)
                            nc.vector.tensor_scalar(nrs[:, p, :], rs2[:, p, :], -1.0, None, ALU.mult).then_inc(nr_ready, 1)
                            for v in (1, 0):
                                dve.wait_ge(w_ready, 2 * ROUNDS)
                                nc.vector.scalar_tensor_tensor(sel[:, p, v, :], wk[:, v, :], 0.0, ex[:, p, v, :],
                                                               ALU.max, ALU.subtract).then_inc(sel_ready, 1)
                        if live(2):
                            dve.wait_ge(y_ready, b - 1)
                            dve.wait_ge(t2_ready, b - 1)
                            nc.vector.tensor_tensor(RES[:, b - 2, :], y2p[:], t2[:, r, :], ALU.add).then_inc(res_ready, 1)
                        if live(1):
                            dve.wait_ge(nr_ready, n + 1)
                            dve.wait_ge(sel_ready, 2 * n + 2)
                            need(dve, xt_ready, n - 1)
                            nc.vector.scalar_tensor_tensor(xg[:, p, :], sel[:, p, 1, :], nrs[:, p, 1:2], X[:, n, :],
                                                           ALU.mult, ALU.mult).then_inc(xg_ready, 1)
                            dve.wait_ge(full_ready, n + 1)
                            nc.vector.scalar_tensor_tensor(t1[:, p, :], sel[:, p, 0, :], nrs[:, p, 0:1], fup[p][:],
                                                           ALU.mult, ALU.mult).then_inc(t1_ready, 1)
                        if live(2):
                            dve.wait_ge(res_ready, b - 1)
                            nc.vector.bn_stats(stats[:, b - 2, :], RES[:, b - 2, :]).then_inc(bs_ready, 1)
                        if live(1):
                            dve.wait_ge(t1_ready, n + 1)
                            nc.vector.tensor_tensor(t2[:, p, :], t1[:, p, :], X[:, n, :], ALU.add).then_inc(t2_ready, 1)
                    run(dve, slot)

        def moe_sems(names):
            return [sem(f"moe_{w}") for w in names.split()]

        def route(glp, XTH, XTL, combT16):
            (mx_ready, d_ready, e_ready, sum_ready, rc_ready, sc_ready, v8_ready, i8_ready, if_ready, den_ready,
             rden_ready, wt_ready, eq_ready, pr_ready, comb_ready, ct_ready, ct_kept, cst_ready, part_ready,
             xth_ready) = moe_sems(
                "mx_ready d_ready e_ready sum_ready rc_ready sc_ready v8_ready i8_ready if_ready den_ready "
                "rden_ready wt_ready eq_ready pr_ready comb_ready ct_ready ct_kept cst_ready part_ready xth_ready")
            with ExitStack() as inner:
                def isb(what, shape, dt=F32):
                    return inner.enter_context(nc.sbuf_tensor(f"moe_{what}", shape, dt))

                mx = isb("mx", [P, B])
                df = isb("df", [P, B, E])
                ee = isb("ee", [P, B, E])
                su = isb("su", [P, B])
                rc = isb("rc", [P, B])
                score = isb("score", [P, B, E])
                v8 = isb("v8", [P, B, 8])
                i8 = isb("i8", [P, B, 8], U32)
                i8f = isb("i8f", [P, B, 8])
                den = isb("den", [P, B])
                rden = isb("rden", [P, B])
                wt = isb("wt", [P, B, 2])
                eq = isb("eq", [P, 2, B, E])
                pr = isb("pr", [P, 2, B, E])
                comb = isb("comb", [P, B, E])
                lg = isb("lg", [P, B, E])
                rest = isb("rest", [P, B, E])
                parts = isb("parts", [P, B, 3, 32], BF16)
                ctp = [inner.enter_context(nc.psum_tensor(f"moe_ctp{i}", [3 * 32, 4, S], BF16)) for i in range(4)]
                block = inner.enter_context(nc.Block())

                @block.gpsimd
                def _(pool):
                    nc.gpsimd.memset(parts[:], 0.0).then_inc(cst_ready, 1)
                    pool.wait_ge(xth_ready, 1)
                    nc.gpsimd.tensor_tensor(XTL[:], XT[:], XTH[:].bitcast(F32), ALU.subtract)

                @block.tensor
                def _(pe):
                    pe.wait_ge(comb_ready, 1)
                    for q in range(4):
                        for j in range(4):
                            ins = nc.tensor.transpose(ctp[q][:, j, :], parts[:, 4 * q + j].rearrange("p z e -> p (z e)"), ident16[:])
                        ins.then_inc(ct_ready, 1)

                @block.scalar
                def _(act):
                    nc.scalar.copy(XTH[:], XT[:]).then_inc(xth_ready, 1)
                    act.wait_ge(d_ready, 1)
                    nc.scalar.activation(ee[:], df[:], ACT.Exp).then_inc(e_ready, 1)
                    for q in range(4):
                        act.wait_ge(ct_ready, q + 1)
                        nc.scalar.copy(combT16[:, 4 * q:4 * q + 4, :], ctp[q][:]).then_inc(ct_kept, 1)

                @block.vector
                def _(dve):
                    bc = lambda ap: ap.unsqueeze(2).to_broadcast([P, B, E])
                    dve.wait_ge(moe_landed, MOE_LANDED)
                    nc.vector.tensor_tensor(lg[:], glp[:], gbias[:].unsqueeze(1).to_broadcast([P, B, E]),
                                            ALU.add).then_inc(mx_ready, 1)
                    dve.wait_ge(mx_ready, 1)
                    nc.vector.tensor_reduce(mx[:], lg[:], AX.X, ALU.max).then_inc(mx_ready, 1)
                    dve.wait_ge(mx_ready, 2)
                    nc.vector.tensor_tensor(df[:], lg[:], bc(mx[:]), ALU.subtract).then_inc(d_ready, 1)
                    dve.wait_ge(e_ready, 1)
                    nc.vector.tensor_reduce(su[:], ee[:], AX.X, ALU.add).then_inc(sum_ready, 1)
                    dve.wait_ge(sum_ready, 1)
                    nc.vector.reciprocal(rc[:], su[:]).then_inc(rc_ready, 1)
                    dve.wait_ge(rc_ready, 1)
                    nc.vector.tensor_tensor(score[:], ee[:], bc(rc[:]), ALU.mult).then_inc(sc_ready, 1)
                    dve.wait_ge(sc_ready, 1)
                    for b in range(B):
                        nc.vector.max(v8[:, b, :], score[:, b, :]).then_inc(v8_ready, 1)
                    for b in range(B):
                        dve.wait_ge(v8_ready, b + 1)
                        nc.vector.max_index(i8[:, b, :], v8[:, b, :], score[:, b, :]).then_inc(i8_ready, 1)
                    dve.wait_ge(i8_ready, B)
                    nc.vector.tensor_copy(i8f[:], i8[:]).then_inc(if_ready, 1)
                    nc.vector.tensor_tensor(den[:], v8[:, :, 0], v8[:, :, 1], ALU.add).then_inc(den_ready, 1)
                    dve.wait_ge(den_ready, 1)
                    nc.vector.tensor_scalar(den[:], den[:], 1e-20, None, ALU.add).then_inc(den_ready, 1)
                    dve.wait_ge(den_ready, 2)
                    nc.vector.reciprocal(rden[:], den[:]).then_inc(rden_ready, 1)
                    dve.wait_ge(rden_ready, 1)
                    nc.vector.tensor_tensor(wt[:], v8[:, :, 0:2], rden[:].unsqueeze(2).to_broadcast([P, B, 2]),
                                            ALU.mult).then_inc(wt_ready, 1)
                    dve.wait_ge(if_ready, 1)
                    for z in range(2):
                        nc.vector.tensor_tensor(eq[:, z], number[:].unsqueeze(1).to_broadcast([P, B, E]), bc(i8f[:, :, z]),
                                                ALU.is_equal).then_inc(eq_ready, 1)
                    dve.wait_ge(wt_ready, 1)
                    for z in range(2):
                        dve.wait_ge(eq_ready, z + 1)
                        nc.vector.tensor_tensor(pr[:, z], eq[:, z], bc(wt[:, :, z]), ALU.mult).then_inc(pr_ready, 1)
                    dve.wait_ge(pr_ready, 2)
                    nc.vector.tensor_tensor(comb[:], pr[:, 0], pr[:, 1], ALU.add).then_inc(part_ready, 1)
                    dve.wait_ge(cst_ready, 1)
                    for z in range(3):
                        src = comb if z == 0 else rest
                        dve.wait_ge(part_ready, 2 * z + 1)
                        ins = nc.vector.tensor_copy(parts[:, :, z, 0:E], src[:])
                        ins.then_inc(part_ready if z < 2 else comb_ready, 1)
                        if z < 2:
                            dve.wait_ge(part_ready, 2 * z + 2)
                            nc.vector.tensor_tensor(rest[:], src[:], parts[:, :, z, 0:E], ALU.subtract).then_inc(part_ready, 1)

        def experts(XTH, XTL, combT16, DWH, DWL):
            with ExitStack() as scope:
                s_ = lambda what: sem(f"moe_{what}")

                def lsb(what, shape, dt=F32):
                    return scope.enter_context(nc.sbuf_tensor(f"moe_{what}", shape, dt))

                (g_ready, u_ready, g_kept, h_ready, silu_ready, plane_ready, hx_ready, hh_ready, hl_ready, dn_ready,
                 dt_kept, tr_ready, sum2_ready, st_ready) = [
                    s_(w) for w in ("g_ready u_ready g_kept h_ready silu_ready plane_ready hx_ready hh_ready hl_ready "
                                    "dn_ready dt_kept tr_ready sum2_ready st_ready").split()]
                gs = lsb("gs", [P, 2, 4, S])
                h0 = lsb("h0", [P, 2, 4, S])
                h1 = lsb("h1", [P, 2, 4, S])
                hx = lsb("hx", [P, 2, 4, S])
                hh, hl = lsb("hh", [P, 2, 4, S], FR), lsb("hl", [P, 2, 4, S], FR)
                dT = lsb("dT", [P, 4, S])
                gp = [scope.enter_context(nc.psum_tensor(f"moe_gp{i}", [P, 4, S], F32)) for i in range(2)]
                up = [scope.enter_context(nc.psum_tensor(f"moe_up{i}", [P, 4, S], F32)) for i in range(2)]
                plane = [scope.enter_context(nc.psum_tensor(f"moe_plane{i}", [P, 4, S], F32)) for i in range(PB)]
                dn = scope.enter_context(nc.psum_tensor("moe_dn", [P, 4, S], F32))
                trp = scope.enter_context(nc.psum_tensor("moe_trp", [P, 4, D], F32))
                last_unit = [max(c for c in range(NCH) if PLANE[c] == n) for n in range(NP)]
                one = lsb("one", [P, 1])
                one_ready, ones_ready = s_("one_ready"), s_("ones_ready")
                block = scope.enter_context(nc.Block())

                def run(eng, slot):
                    for j in range(NCH):
                        slot(0, j, lambda lag: j >= lag)
                    with eng.Fori(1, B // 4) as q:
                        for j in range(NCH):
                            slot(q, j, lambda lag: True)
                    for j in range(4):
                        slot(B // 4, j, lambda lag: j < lag)

                @block.gpsimd
                def _(pool):
                    nc.gpsimd.memset(one[:], 1.0).then_inc(one_ready, 1)
                    ones = one[REAL:P].unsqueeze(2).to_broadcast([P - REAL, 4, S])

                    def slot(q, j, live):
                        k = NCH * q + j
                        p = (j - 1) % 2
                        last = j == NCH - 1 and live(0)
                        if last:
                            pool.wait_ge(hl_ready, k - 1)
                            nc.gpsimd.tensor_tensor(h1[REAL:P, j % 2], ones, ones, ALU.mult).then_inc(ones_ready, 1)
                        if live(1):
                            if last:
                                pool.wait_ge(ones_ready, q + 1)
                            pool.wait_ge(hh_ready, k)
                            nc.gpsimd.tensor_tensor(hl[:, p], hx[:, p], hh[:, p].bitcast(F32), ALU.subtract).then_inc(hl_ready, 1)
                    pool.wait_ge(one_ready, 1)
                    run(pool, slot)

                @block.tensor
                def _(pe):
                    def slot(q, j, live):
                        k = NCH * q + j
                        if live(0):
                            need(pe, g_kept, k - 1)
                            x = XTH[:, bass.ds(4 * q, 4), :], XTL[:, bass.ds(4 * q, 4), :]
                            cols = slice(P * j, P * j + P)
                            products3(gp[j % 2][:], (GPH[:, cols], GPL[:, cols]), x).then_inc(g_ready, 1)
                            need(pe, h_ready, k - 1)
                            products3(up[j % 2][:], (UPH[:, cols], UPL[:, cols]), x).then_inc(u_ready, 1)
                        if live(4) and j == 3:
                            pe.wait_ge(dt_kept, q)
                            for b in range(4):
                                ins = nc.tensor.transpose(trp[:, b, :], dT[:, b, :], ident[:])
                            ins.then_inc(tr_ready, 1)
                        if live(3):
                            c = (j - 3) % NCH
                            pe.wait_ge(hl_ready, k - 2)
                            if c == 0:
                                need(pe, dt_kept, q)
                            products3(dn[:], (DWH[:, c, :], DWL[:, c, :]), (hh[:, (j - 3) % 2], hl[:, (j - 3) % 2]),
                                      start=(c == 0), stop=(c == NCH - 1)).then_inc(dn_ready, 1)
                        if live(0):
                            n = PLANE[j]
                            if j == 0 or PLANE[j - 1] != n:
                                need(pe, hh_ready, NCH * (q if n >= PB else q - 1) + last_unit[(n - PB) % NP] + 1)
                                nc.tensor.matmul(plane[n % PB][:], owner[:, n, :], combT16[:, bass.ds(4 * q, 4), :],
                                                 start=True, stop=True).then_inc(plane_ready, 1)
                    run(pe, slot)

                @block.scalar
                def _(act):
                    def slot(q, j, live):
                        k = NCH * q + j
                        if live(0):
                            act.wait_ge(g_ready, k + 1)
                            need(act, h_ready, k - 1)
                            nc.scalar.activation(gs[:, j % 2], gp[j % 2][:], ACT.Identity, bias=gb[:, j:j + 1]).then_inc(g_kept, 1)
                        if live(1):
                            act.wait_ge(h_ready, k)
                            need(act, hh_ready, k - 2)
                            m = REAL if j == 0 else P
                            nc.scalar.activation(h1[0:m, (j - 1) % 2], h0[0:m, (j - 1) % 2], ACT.Silu).then_inc(silu_ready, 1)
                        if live(3) and j == 2:
                            act.wait_ge(dn_ready, NCH * q)
                            nc.scalar.copy(dT[:], dn[:]).then_inc(dt_kept, 1)
                    run(act, slot)

                @block.vector
                def _(dve):
                    def slot(q, j, live):
                        k = NCH * q + j
                        if live(0):
                            dve.wait_ge(u_ready, k + 1)
                            dve.wait_ge(g_kept, k + 1)
                            need(dve, silu_ready, k - 1)
                            nc.vector.scalar_tensor_tensor(h0[:, j % 2], up[j % 2][:], ub[:, j:j + 1], gs[:, j % 2],
                                                           ALU.add, ALU.mult).then_inc(h_ready, 1)
                        if live(1):
                            c = (j - 1) % NCH
                            n = PLANE[c]
                            dve.wait_ge(silu_ready, k)
                            if j == 0:
                                dve.wait_ge(ones_ready, q)
                            dve.wait_ge(plane_ready, NP * (q if j else q - 1) + n + 1)
                            need(dve, hl_ready, k - 2)
                            nc.vector.tensor_tensor(hx[:, (j - 1) % 2], h1[:, (j - 1) % 2], plane[n % PB][:],
                                                    ALU.mult).then_inc(hx_ready, 1)
                            need(dve, dn_ready, k - 2)
                            nc.vector.tensor_tensor(hh[:, (j - 1) % 2], h1[:, (j - 1) % 2], plane[n % PB][:],
                                                    ALU.mult).then_inc(hh_ready, 1)
                        if live(4) and j == 3:
                            done = bass.ds(4 * q - 4, 4)
                            dve.wait_ge(tr_ready, q)
                            nc.vector.tensor_tensor(RES[:, done, :], trp[:], X[:, done, :], ALU.add).then_inc(sum2_ready, 1)
                            dve.wait_ge(sum2_ready, q)
                            for t in range(4):
                                b = 4 * q - 4 + t
                                nc.vector.bn_stats(stats[:, b, :], RES[:, b, :]).then_inc(st_ready, 1)
                    run(dve, slot)

        with ExitStack() as l0:
            def lsb(name, shape, dt=F32):
                return l0.enter_context(nc.sbuf_tensor(name, shape, dt))

            ZM = lsb("ZM", [P, H, D])
            WQ0 = lsb("WQ0", [DH0, H, D])
            WK0 = lsb("WK0", [DH0, H, D])
            WVT0 = lsb("WVT0", [P, H * DH0])
            WVH, WVL = lsb("WVH", [P, H * DH0], FR), lsb("WVL", [P, H * DH0], FR)
            WO0 = lsb("WO0", [P, H * DH0 // P, D])
            causal = lsb("causal", [P, S], BF16)
            zm_ready, zms_ready, wvh_ready = sem("zm_ready"), sem("zms_ready"), sem("wvh_ready")
            with ExitStack() as scope:
                zmp = [scope.enter_context(nc.psum_tensor(f"zmp{i}", [P, 4, D], F32)) for i in range(4)]
                block = scope.enter_context(nc.Block())

                @block.sync
                def _(sp):
                    sp.dma_start(WQ0[:], a["wq0"]).then_inc(qk_landed, 16)
                    sp.dma_start(XT[:, 0:4, :], a["xT"][:, 0:4, :]).then_inc(loaded, 16)
                    sp.wait_ge(loaded, 16 * 5)

                @block.gpsimd
                def _(pool):
                    nc.gpsimd.memset(LW[:], 0.0).then_inc(lw_cleared, 1)
                    nc.gpsimd.memset(half[:], -0.5)

                @block.scalar
                def _(act):
                    act.dma_start(WK0[:], a["wk0"]).then_inc(qk_landed, 16)
                    act.dma_start(WVT0[:], a["wvT0"]).then_inc(loaded, 16)
                    act.dma_start(ident[:], a["ident"]).then_inc(loaded, 16)
                    act.dma_start(ident16[:], a["ident16"]).then_inc(loaded, 16)
                    act.dma_start(causal[:], a["causal"]).then_inc(loaded, 16)
                    for q in range(4):
                        act.wait_ge(zm_ready, q + 1)
                        nc.scalar.mul(ZM[:, 4 * q:4 * q + 4, :], zmp[q][:], float(DH0) ** -0.5).then_inc(zms_ready, 1)
                    act.wait_ge(loaded, 16 * 5)
                    nc.scalar.copy(WVH[:], WVT0[:]).then_inc(wvh_ready, 1)

                @block.vector
                def _(dve):
                    dve.wait_ge(loaded, 16 * 5)
                    dve.wait_ge(wvh_ready, 1)
                    nc.vector.tensor_tensor(WVL[:], WVT0[:], WVH[:].bitcast(F32), ALU.subtract)

                @block.tensor
                def _(pe):
                    pe.wait_ge(qk_landed, 16 * 2)
                    for q in range(4):
                        for j in range(4):
                            h = 4 * q + j
                            ins = nc.tensor.matmul(zmp[q][:, j, :], WK0[:, h, :], WQ0[:, h, :], start=True, stop=True)
                        ins.then_inc(zm_ready, 1)

            def later_loads(sp):
                sp.dma_start(WO0[:], a["wo0"]).then_inc(wo_landed, 16)
                sp.dma_start(XT[:, 4:B, :], a["xT"][:, 4:B, :]).then_inc(late_landed, 16)
                sp.dma_start(X[:], a["x"].rearrange("b t c -> t b c")).then_inc(late_landed, 16)
                sp.dma_start(CTXT[:], a["ctxT"]).then_inc(late_landed, 16)
                for dst, name in gl_loads:
                    sp.dma_start(dst[:], a[name]).then_inc(gl_landed, 16)
                sp.wait_ge(lw_cleared, 1)
                for dst, name in gl_parts:
                    sp.dma_start(dst, a[name]).then_inc(gl_landed, 16)
                for dst, name in w1_loads:
                    sp.dma_start(dst[:], a[name]).then_inc(w1_landed, 16)
                for dst, name in moe_loads:
                    sp.dma_start(dst[:], a[name]).then_inc(moe_landed, 16)

            attention("a0", True, causal, WO0, ZM=ZM, WVT=(WVH, WVL), loads=later_loads)
        with ExitStack() as l0:
            XTt = l0.enter_context(nc.sbuf_tensor("XTt", [P, S + 3 * C, B], F32))
            YT = l0.enter_context(nc.sbuf_tensor("YT", [P, S, B], F32))
            layernorm("ln0", also_time_major=XTt[:, 0:S, :])
            recurrence(XTt, YT)
            add_recurrence(YT)
        layernorm("ln1")
        part_ends()

        GPH, GPL = sb("GPH", [P, NCH * P], FR), sb("GPL", [P, NCH * P], FR)
        UPH, UPL = sb("UPH", [P, NCH * P], FR), sb("UPL", [P, NCH * P], FR)
        gated_layer()
        with ExitStack() as l1:
            def lsb(name, shape, dt=F32):
                return l1.enter_context(nc.sbuf_tensor(name, shape, dt))

            ones1 = lsb("ones1", [1, P])
            maskbias = lsb("maskbias", [P, B, S], BF16)
            QT = lsb("QTH", [P, B, S], FR), lsb("QTL", [P, B, S], FR)
            KT = lsb("KTH", [P, B, S], FR), lsb("KTL", [P, B, S], FR)
            VA = lsb("VA", [P, B, H, DH1 + 1])
            w = lambda n: W1[:, n, :]
            layernorm("ln2", also=narrow_operands("n1", w(0), w(1), w(2), XT, QT, KT, VA))
            part_ends()
            attention("a1", False, window, W1[:, 3:4, :], QT=QT, KT=KT, VA=VA, jmask=jmask, umask=umask)
            layernorm("ln3", also=narrow_operands(
                "n2", w(4), w(5), w(6), CTXT, QT, KT, VA, bias_q=colb[:, 0:1], bias_k=colb[:, 1:2], bias_v=bv[:],
                ones_row=ones1, maskbias=maskbias))
            part_ends()
            attention("a2", False, None, W1[:, 7:8, :], QT=QT, KT=KT, VA=VA, jmask=jmask, umask=umask, maskbias=maskbias,
                      bo_row=bo, ones_row=ones1)
        with ExitStack() as scope:
            glp = scope.enter_context(nc.psum_tensor("moe_glp", [P, B, E], F32))

            DWH, DWL = sb("DWH", [P, NCH, D], FR), sb("DWL", [P, NCH, D], FR)
            dwh_ready = sem("dwh_ready")

            def gate_and_split(_):
                def on_tensor(q):
                    if q == 0:
                        nc.tensor.wait_ge(moe_landed, MOE_LANDED)
                    for b in range(4 * q, 4 * q + 4):
                        nc.tensor.matmul(glp[:, b, :], XT[:, b, :], gwT[:], start=True, stop=True)

                def on_scalar_first():
                    nc.scalar.wait_ge(moe_landed, MOE_LANDED)
                    nc.scalar.copy(DWH[:], DWT[:]).then_inc(dwh_ready, 1)

                def on_gpsimd():
                    nc.gpsimd.wait_ge(moe_landed, MOE_LANDED)
                    nc.gpsimd.wait_ge(dwh_ready, 1)
                    nc.gpsimd.tensor_tensor(DWL[:], DWT[:], DWH[:].bitcast(F32), ALU.subtract)

                return {"tensor": on_tensor, "scalar_first": on_scalar_first, "gpsimd": on_gpsimd}

            layernorm("ln4", also=gate_and_split)
            part_ends()
            XTH, XTL = sb("XTH", [P, B, S], FR), sb("XTL", [P, B, S], FR)
            combT16 = sb("combT16", [3 * 32, B, S], BF16)
            route(glp, XTH, XTL, combT16)
        experts(XTH, XTL, combT16, DWH, DWL)
        layernorm("ln5", out_to=out)


def host_layout(inputs):
    n = {k: np.asarray(v) for k, v in inputs.items()}
    c = np.ascontiguousarray
    r = np.arange
    t, s = r(S)[:, None], r(S)[None, :]
    g = {
        "x": c(n["x"]),
        "xT": c(n["x"].transpose(2, 0, 1)),
        "ctxT": c(n["ctx_1024"].transpose(2, 0, 1)),
        "wq0": c(n["L0_attn_w_q"].transpose(1, 0, 2)),
        "wk0": c(n["L0_attn_w_k"].transpose(1, 0, 2)),
        "wvT0": c(n["L0_attn_w_v"].reshape(H * DH0, D).T),
        "wo0": c(n["L0_attn_w_o"].reshape(H * DH0 // P, P, D).transpose(1, 0, 2)),
        "ident": np.eye(P, dtype=np.float32),
        "ident16": np.eye(P, dtype=np.float32).astype(mybir.dt.np(BF16)),
        "causal": np.where(s > t, NEG, 0.0).astype(mybir.dt.np(BF16)),
    }
    sb_ = r(C * B)
    g["same"] = np.where(sb_[:, None] % B == sb_[None, :] % B, np.float32(LR), np.float32(0))
    so, si = "L0_ffn_so_", "L0_ffn_si_"
    g["convw"] = c(np.stack([n[so + "conv_w"].reshape(D), n[si + "conv_w"].reshape(D)], 1))
    g["groups"] = (r(D)[:, None] // 4 == r(G)[None, :]).astype(np.float32)
    g["chan"] = c(np.stack([np.concatenate([n[v + w] for v in (so, si)]) for w in ("conv_b", "gamma", "beta")], 1))
    g["ffw"], g["ffb"] = c(n["L0_ffn_weight"]), c(n["L0_ffn_bias"][None])
    g["lwo"], g["lwi"] = c(n[so + "lin_w"].T), c(n[si + "lin_w"].T)
    g["lbo"], g["lbi"] = c(n[so + "lin_b"][None]), c(n[si + "lin_b"][None])
    g["w1"] = c(np.stack([n["L1_attn_W" + w].T for w in "qkvo"] + [n["L1_xattn_W" + w].T for w in "qkvo"], 1))
    g["window"] = np.where((s > t) | (s < t - 16), NEG, 0.0).astype(mybir.dt.np(BF16))
    g["jmask"] = (r(P)[:, None] % 32 // DH1 == r(HU)[None, :]).astype(np.float32)
    g["umask"] = (r(P)[:, None] // 32 == r(NU)[None, :]).astype(np.float32)
    g["colb"] = c(np.stack([n["L1_xattn_bq"], n["L1_xattn_bk"]], 1))
    g["bo"] = c(n["L1_xattn_bo"][None])
    g["bv"] = np.tile(n["L1_xattn_bv"][None], (P, 1))
    g["mask"] = c(n["mask_Bx1xSxS2_if1"][:, 0].transpose(1, 0, 2))
    g["gwT"], g["gbias"] = c(n["L1_ffn_gate_w"].T), np.tile(n["L1_ffn_gate_b"][None], (P, 1))
    g["number"] = np.tile(r(E).astype(np.float32)[None], (P, 1))
    rows = lambda w: c(np.pad(w, [(0, NCH * P - HID)] + [(0, 0)] * (w.ndim - 1)).reshape((NCH, P) + w.shape[1:]).swapaxes(0, 1))
    cols = lambda w: c(np.pad(w.reshape(HID, D), ((0, NCH * P - HID), (0, 0))).T)
    g["gpT"], g["upT"] = cols(n["L1_ffn_gp_w"]), cols(n["L1_ffn_up_w"])
    down = np.pad(n["L1_ffn_down_w"].transpose(0, 2, 1).reshape(HID, D), ((0, NCH * P - HID), (0, 0)))
    down[HID:HID + E] = n["L1_ffn_down_b"]
    g["dwT"] = c(down.reshape(NCH, P, D).swapaxes(0, 1))
    g["gpb"], g["upb"] = rows(n["L1_ffn_gp_b"].reshape(HID)), rows(n["L1_ffn_up_b"].reshape(HID))
    chunk = np.array([OWNERS.index(o) for o in PLANES])
    expert = (P * chunk[:, None] + r(P)[None, :]) // F
    bias_row = P * chunk[:, None] + r(P)[None, :] - HID
    expert = np.where(bias_row >= 0, np.where(bias_row < E, bias_row, -1), expert)
    g["owner"] = (r(96)[:, None, None] % 32 == expert[None]).astype(mybir.dt.np(BF16))
    return g


def kernel(**inputs):
    import concourse.bacc as bacc
    from concourse.bass_utils import run_bass_kernel_spmd

    nc = bacc.Bacc("TRN2", target_bir_lowering=False, num_devices=1)
    arrays = {f"in_{name}": v for name, v in host_layout(inputs).items()}
    aps = {name[3:]: nc.dram_tensor(name, v.shape, mybir.dt.from_np(v.dtype), kind="ExternalInput").ap()
           for name, v in arrays.items()}
    out = nc.dram_tensor("out", (B, S, D), F32, kind="ExternalOutput").ap()
    decoder_program(nc, aps, out)
    return run_bass_kernel_spmd(nc, [arrays], core_ids=[0]).results[0]["out"]
```
